# Optimizing a Trainium2 kernel written in Bass

```python
import numpy as np
import jax
import jax.numpy as jnp

def _softmax(x, axis=-1):
    return jax.nn.softmax(x, axis=axis)

def _gelu(x):
    return jax.nn.gelu(x, approximate=True)

def _silu(x):
    return jax.nn.silu(x)

def _sigmoid(x):
    return jax.nn.sigmoid(x)

def _layernorm(x, axis=-1, eps=1e-05):
    m = jnp.mean(x, axis=axis, keepdims=True)
    v = jnp.var(x, axis=axis, keepdims=True)
    return (x - m) / jnp.sqrt(v + eps)

def _scatter_add(tgt, idx, src, axis=0):
    return tgt.at[idx].add(src)

def _segment_sum(src, seg, n):
    return jax.ops.segment_sum(src, seg, n)
kernel_name = 'mk_xattn_ffn_d2_seqx_r4_8facd6'

def setup_inputs(seed: int=0):
    np.random.seed(seed)
    _w = jnp.asarray

    def _rec_inputs():
        import jax
        import jax.numpy as jnp
        _rk = jax.random.key(seed)
        x = 0.002226 + 0.9996 * jax.random.normal(jax.random.fold_in(_rk, 1), (2, 1024, 256), jnp.float32)
        _lenS = 1024 - jax.random.randint(jax.random.fold_in(_rk, 7), (2,), 0, max(1, 1024 // 4) + 1, jnp.int32)
        _lenS2 = 64 - jax.random.randint(jax.random.fold_in(_rk, 8), (2,), 0, max(1, 64 // 4) + 1, jnp.int32)
        _ctx_1024P = jax.random.normal(jax.random.fold_in(_rk, 11), (2, 16, 256), jnp.float32)
        _ctx_1024c = jax.random.dirichlet(jax.random.fold_in(_rk, 511), 0.3 * jnp.ones((16,), jnp.float32), (2, 64))
        _ctx_1024t = jnp.einsum('bsk,bkd->bsd', _ctx_1024c, _ctx_1024P)
        _ctx_1024t = _ctx_1024t * jax.lax.rsqrt(jnp.mean(jnp.square(_ctx_1024t)) + 1e-12) * 0.953939
        ctx_1024 = -0.000125008 + 0.999885 * (_ctx_1024t + 0.3 * jax.random.normal(jax.random.fold_in(_rk, 611), (2, 64, 256), jnp.float32))
        _validS = jnp.arange(1024)[None, :] < _lenS[:, None]
        _validS2 = jnp.arange(64)[None, :] < _lenS2[:, None]
        _causal = jnp.tril(jnp.ones((1024, 1024), dtype=bool))
        mask_BxSxS2_bk0 = jnp.logical_not(jnp.broadcast_to(_validS2[:, None, :], (2, 1024, 64)))
        return (x, ctx_1024, mask_BxSxS2_bk0)
    x, ctx_1024, mask_BxSxS2_bk0 = _rec_inputs()

    def _L0_xattn_setup():
        import jax, jax.numpy as jnp
        import numpy as np
        DIM = 256
        HEADS = 16
        DIM_HEAD = 64
        INNER = HEADS * DIM_HEAD
        EPS = 1e-05

        def _layernorm(x, w, b):
            m = jnp.mean(x, axis=-1, keepdims=True)
            v = jnp.mean(jnp.square(x - m), axis=-1, keepdims=True)
            return (x - m) * jax.lax.rsqrt(v + EPS) * w + b
        key = jax.random.key(seed)
        ks = jax.random.split(key, 9)
        B, N, L = (8, 1024, 64)
        x = jax.random.normal(ks[0], (B, N, DIM), dtype=jnp.float32)
        latents = jax.random.normal(ks[1], (B, L, DIM), dtype=jnp.float32)
        s = 1.0 / np.sqrt(DIM)
        Wq = jax.random.normal(ks[2], (DIM, INNER), dtype=jnp.float32) * s
        Wkv = jax.random.normal(ks[3], (DIM, 2 * INNER), dtype=jnp.float32) * s
        Wo = jax.random.normal(ks[4], (INNER, DIM), dtype=jnp.float32) * (1.0 / np.sqrt(INNER))
        ln1_w = jnp.ones((DIM,), jnp.float32)
        ln1_b = jnp.zeros((DIM,), jnp.float32)
        ln2_w = jnp.ones((DIM,), jnp.float32)
        ln2_b = jnp.zeros((DIM,), jnp.float32)
        return {'x': x, 'latents': latents, 'Wq': Wq, 'Wkv': Wkv, 'Wo': Wo, 'ln1_w': ln1_w, 'ln1_b': ln1_b, 'ln2_w': ln2_w, 'ln2_b': ln2_b}
    _L0_xattn_all = _L0_xattn_setup()
    _L0_xattn_in = {k: v for k, v in _L0_xattn_all.items() if k in ('Wq', 'Wkv', 'Wo', 'ln1_w', 'ln1_b', 'ln2_w', 'ln2_b')}
    del _L0_xattn_all

    def _L0_ffn_setup():
        import jax, jax.numpy as jnp
        import numpy as np
        B, L, D, H, E, TOP_K = (4, 512, 256, 1024, 8, 2)
        LN_EPS = 1e-05
        key = jax.random.key(seed)
        ks = jax.random.split(key, 8)
        x = jax.random.normal(ks[0], (B, L, D), dtype=jnp.float32)
        gate_w = jax.random.normal(ks[1], (D, E), dtype=jnp.float32) / np.sqrt(D)
        w1 = jax.random.normal(ks[2], (E, D, H), dtype=jnp.float32) / np.sqrt(D)
        b1 = jnp.zeros((E, H), dtype=jnp.float32)
        w2 = jax.random.normal(ks[3], (E, H, D), dtype=jnp.float32) / np.sqrt(H)
        b2 = jnp.zeros((E, D), dtype=jnp.float32)
        gamma = jnp.ones((D,), dtype=jnp.float32)
        beta = jnp.zeros((D,), dtype=jnp.float32)
        return {'x': x, 'gate_w': gate_w, 'w1': w1, 'b1': b1, 'w2': w2, 'b2': b2, 'gamma': gamma, 'beta': beta}
    _L0_ffn_all = _L0_ffn_setup()
    _L0_ffn_in = {k: v for k, v in _L0_ffn_all.items() if k in ('gate_w', 'w1', 'b1', 'w2', 'b2', 'gamma', 'beta')}
    del _L0_ffn_all

    def _L1_xattn_setup():
        import jax, jax.numpy as jnp
        import numpy as np
        NUM_HEADS = 16

        def softmax1(attn):
            padded = jnp.pad(attn, ((0, 0), (0, 0), (0, 0), (0, 1)))
            return jax.nn.softmax(padded, axis=-1)[..., :-1]
        key = jax.random.key(seed)
        ks = jax.random.split(key, 7)
        B, N, M, C = (2, 256, 1024, 256)
        x = jax.random.normal(ks[0], (B, N, C), dtype=jnp.float32)
        context = jax.random.normal(ks[1], (B, M, C), dtype=jnp.float32)
        mask = jax.random.randint(ks[2], (B, N, M), 0, 2) > 0
        s = 1.0 / np.sqrt(C)
        Wq = jax.random.normal(ks[3], (C, C), dtype=jnp.float32) * s
        Wkv = jax.random.normal(ks[4], (C, 2 * C), dtype=jnp.float32) * s
        Wproj = jax.random.normal(ks[5], (C, C), dtype=jnp.float32) * s
        bproj = jnp.zeros((C,), dtype=jnp.float32)
        return {'x': x, 'context': context, 'mask': mask, 'Wq': Wq, 'Wkv': Wkv, 'Wproj': Wproj, 'bproj': bproj}
    _L1_xattn_all = _L1_xattn_setup()
    _L1_xattn_in = {k: v for k, v in _L1_xattn_all.items() if k in ('Wq', 'Wkv', 'Wproj', 'bproj')}
    del _L1_xattn_all

    def _L1_ffn_setup():
        import jax, jax.numpy as jnp
        import numpy as np
        B, S, D_MODEL, D_FF = (4, 512, 256, 1024)

        def _quantum_transform(hidden, theta, w_real, w_imag):
            imag = w_imag * jnp.sin(theta + hidden * 0.1)
            quantum_phase = jnp.cos(theta) * w_real + jnp.sin(theta) * w_imag
            return hidden + quantum_phase * imag * 0.1
        key = jax.random.key(seed)
        ks = jax.random.split(key, 8)
        return {'x': jax.random.normal(ks[0], (B, S, D_MODEL), dtype=jnp.float32), 'W1': jax.random.normal(ks[1], (D_MODEL, D_FF), dtype=jnp.float32) * (1.0 / np.sqrt(D_MODEL)), 'b1': jnp.zeros((D_FF,), dtype=jnp.float32), 'quantum_phases': jax.random.normal(ks[2], (D_FF,), dtype=jnp.float32) * (2.0 * np.pi), 'quantum_weights_real': jax.random.normal(ks[3], (D_FF,), dtype=jnp.float32) * 0.1, 'quantum_weights_imag': jax.random.normal(ks[4], (D_FF,), dtype=jnp.float32) * 0.1, 'W2': jax.random.normal(ks[5], (D_FF, D_MODEL), dtype=jnp.float32) * (1.0 / np.sqrt(D_FF)), 'b2': jnp.zeros((D_MODEL,), dtype=jnp.float32)}
    _L1_ffn_all = _L1_ffn_setup()
    _L1_ffn_in = {k: v for k, v in _L1_ffn_all.items() if k in ('W1', 'b1', 'quantum_phases', 'quantum_weights_real', 'quantum_weights_imag', 'W2', 'b2')}
    del _L1_ffn_all
    return {'x': x, 'ctx_1024': ctx_1024, 'mask_BxSxS2_bk0': mask_BxSxS2_bk0, 'L0_xattn_Wq': _L0_xattn_in['Wq'], 'L0_xattn_Wkv': _L0_xattn_in['Wkv'], 'L0_xattn_Wo': _L0_xattn_in['Wo'], 'L0_xattn_ln1_w': _L0_xattn_in['ln1_w'], 'L0_xattn_ln1_b': _L0_xattn_in['ln1_b'], 'L0_xattn_ln2_w': _L0_xattn_in['ln2_w'], 'L0_xattn_ln2_b': _L0_xattn_in['ln2_b'], 'L0_ffn_gate_w': _L0_ffn_in['gate_w'], 'L0_ffn_w1': _L0_ffn_in['w1'], 'L0_ffn_b1': _L0_ffn_in['b1'], 'L0_ffn_w2': _L0_ffn_in['w2'], 'L0_ffn_b2': _L0_ffn_in['b2'], 'L0_ffn_gamma': _L0_ffn_in['gamma'], 'L0_ffn_beta': _L0_ffn_in['beta'], 'L1_xattn_Wq': _L1_xattn_in['Wq'], 'L1_xattn_Wkv': _L1_xattn_in['Wkv'], 'L1_xattn_Wproj': _L1_xattn_in['Wproj'], 'L1_xattn_bproj': _L1_xattn_in['bproj'], 'L1_ffn_W1': _L1_ffn_in['W1'], 'L1_ffn_b1': _L1_ffn_in['b1'], 'L1_ffn_quantum_phases': _L1_ffn_in['quantum_phases'], 'L1_ffn_quantum_weights_real': _L1_ffn_in['quantum_weights_real'], 'L1_ffn_quantum_weights_imag': _L1_ffn_in['quantum_weights_imag'], 'L1_ffn_W2': _L1_ffn_in['W2'], 'L1_ffn_b2': _L1_ffn_in['b2']}

def reference(x, ctx_1024, mask_BxSxS2_bk0, L0_xattn_Wq, L0_xattn_Wkv, L0_xattn_Wo, L0_xattn_ln1_w, L0_xattn_ln1_b, L0_xattn_ln2_w, L0_xattn_ln2_b, L0_ffn_gate_w, L0_ffn_w1, L0_ffn_b1, L0_ffn_w2, L0_ffn_b2, L0_ffn_gamma, L0_ffn_beta, L1_xattn_Wq, L1_xattn_Wkv, L1_xattn_Wproj, L1_xattn_bproj, L1_ffn_W1, L1_ffn_b1, L1_ffn_quantum_phases, L1_ffn_quantum_weights_real, L1_ffn_quantum_weights_imag, L1_ffn_W2, L1_ffn_b2):
    import jax
    import jax.numpy as jnp

    def _L0_xattn_ref(x, latents, Wq, Wkv, Wo, ln1_w, ln1_b, ln2_w, ln2_b):
        import jax, jax.numpy as jnp
        import numpy as np
        DIM = 256
        HEADS = 16
        DIM_HEAD = 64
        INNER = HEADS * DIM_HEAD
        EPS = 1e-05

        def _layernorm(x, w, b):
            m = jnp.mean(x, axis=-1, keepdims=True)
            v = jnp.mean(jnp.square(x - m), axis=-1, keepdims=True)
            return (x - m) * jax.lax.rsqrt(v + EPS) * w + b
        B, L, _ = latents.shape
        xn = _layernorm(x, ln1_w, ln1_b)
        ln = _layernorm(latents, ln2_w, ln2_b)
        q = ln @ Wq
        kv_input = jnp.concatenate([xn, ln], axis=-2)
        kv = kv_input @ Wkv
        k, v = jnp.split(kv, 2, axis=-1)

        def heads(t):
            b, s, _ = t.shape
            return t.reshape(b, s, HEADS, DIM_HEAD).transpose(0, 2, 1, 3)
        q, k, v = (heads(q), heads(k), heads(v))
        scale = 1.0 / np.sqrt(np.sqrt(DIM_HEAD))
        logits = jnp.einsum('bhld,bhsd->bhls', q * scale, k * scale)
        w = jax.nn.softmax(logits.astype(jnp.float32), axis=-1).astype(logits.dtype)
        out = jnp.einsum('bhls,bhsd->bhld', w, v)
        out = out.transpose(0, 2, 1, 3).reshape(B, L, INNER)
        return out @ Wo

    def _L0_ffn_ref(x, gate_w, w1, b1, w2, b2, gamma, beta):
        import jax, jax.numpy as jnp
        import numpy as np
        B, L, D, H, E, TOP_K = (4, 512, 256, 1024, 8, 2)
        LN_EPS = 1e-05
        residual = x
        mu = jnp.mean(x, axis=-1, keepdims=True)
        var = jnp.mean(jnp.square(x - mu), axis=-1, keepdims=True)
        xn = (x - mu) * jax.lax.rsqrt(var + LN_EPS) * gamma + beta
        probs = jax.nn.softmax(jnp.einsum('bld,de->ble', xn, gate_w), axis=-1)
        w, idx = jax.lax.top_k(probs, TOP_K)
        w = w / jnp.sum(w, axis=-1, keepdims=True)
        cw = jnp.sum(w[..., None] * jax.nn.one_hot(idx, E, dtype=x.dtype), axis=2)
        h = jax.nn.gelu(jnp.einsum('bld,edh->eblh', xn, w1) + b1[:, None, None, :], approximate=False)
        out_e = jnp.einsum('eblh,ehd->ebld', h, w2) + b2[:, None, None, :]
        output = jnp.einsum('ble,ebld->bld', cw, out_e)
        return output + residual

    def _L1_xattn_ref(x, context, mask, Wq, Wkv, Wproj, bproj):
        import jax, jax.numpy as jnp
        import numpy as np
        NUM_HEADS = 16

        def softmax1(attn):
            padded = jnp.pad(attn, ((0, 0), (0, 0), (0, 0), (0, 1)))
            return jax.nn.softmax(padded, axis=-1)[..., :-1]
        B, N, C = x.shape
        M = context.shape[1]
        H = NUM_HEADS
        d = C // H
        scale = d ** (-0.5)
        q = (x @ Wq).reshape(B, N, H, d).transpose(0, 2, 1, 3)
        kv = (context @ Wkv).reshape(B, M, 2, H, d)
        k = kv[:, :, 0].transpose(0, 2, 1, 3)
        v = kv[:, :, 1].transpose(0, 2, 1, 3)
        attn = jnp.einsum('bhnd,bhmd->bhnm', q, k) * scale
        neg = -jnp.finfo(attn.dtype).max
        attn = jnp.where(mask[:, None, :, :], neg, attn)
        attn = softmax1(attn)
        out = jnp.einsum('bhnm,bhmd->bhnd', attn, v)
        out = out.transpose(0, 2, 1, 3).reshape(B, N, C)
        return out @ Wproj + bproj

    def _L1_ffn_ref(x, W1, b1, quantum_phases, quantum_weights_real, quantum_weights_imag, W2, b2):
        import jax, jax.numpy as jnp
        import numpy as np
        B, S, D_MODEL, D_FF = (4, 512, 256, 1024)

        def _quantum_transform(hidden, theta, w_real, w_imag):
            imag = w_imag * jnp.sin(theta + hidden * 0.1)
            quantum_phase = jnp.cos(theta) * w_real + jnp.sin(theta) * w_imag
            return hidden + quantum_phase * imag * 0.1
        hidden = jnp.einsum('bsd,df->bsf', x, W1) + b1
        q = _quantum_transform(hidden, quantum_phases, quantum_weights_real, quantum_weights_imag)
        act = jax.nn.relu(q)
        return jnp.einsum('bsf,fd->bsd', act, W2) + b2
    x = x + _L0_xattn_ref(ctx_1024, _layernorm(x, axis=-1), L0_xattn_Wq, L0_xattn_Wkv, L0_xattn_Wo, L0_xattn_ln1_w, L0_xattn_ln1_b, L0_xattn_ln2_w, L0_xattn_ln2_b)
    x = x + _L0_ffn_ref(_layernorm(x, axis=-1), L0_ffn_gate_w, L0_ffn_w1, L0_ffn_b1, L0_ffn_w2, L0_ffn_b2, L0_ffn_gamma, L0_ffn_beta)
    x = x + _L1_xattn_ref(_layernorm(x, axis=-1), ctx_1024, mask_BxSxS2_bk0, L1_xattn_Wq, L1_xattn_Wkv, L1_xattn_Wproj, L1_xattn_bproj)
    x = x + _L1_ffn_ref(_layernorm(x, axis=-1), L1_ffn_W1, L1_ffn_b1, L1_ffn_quantum_phases, L1_ffn_quantum_weights_real, L1_ffn_quantum_weights_imag, L1_ffn_W2, L1_ffn_b2)
    return x

_drawn_inputs = setup_inputs


def setup_inputs(seed=0):
    import zlib

    import numpy as np

    out = dict(_drawn_inputs(seed))
    spreads = {'L0_xattn_ln1_w': (1.0, 0.6),
     'L0_xattn_ln1_b': (0.0, 0.38),
     'L0_xattn_ln2_w': (1.0, 0.2),
     'L0_xattn_ln2_b': (0.0, 0.1),
     'L0_ffn_b1': (0.0, 0.325),
     'L0_ffn_b2': (0.0, 0.1),
     'L0_ffn_gamma': (1.0, 0.2),
     'L0_ffn_beta': (0.0, 0.1),
     'L1_xattn_bproj': (0.0, 0.1),
     'L1_ffn_b1': (0.0, 0.1),
     'L1_ffn_b2': (0.0, 0.1)}
    factors = {'L1_ffn_quantum_phases': 29.837,
     'L1_ffn_quantum_weights_real': 64.0,
     'L1_ffn_quantum_weights_imag': 24.127}
    for name, (base, spread) in spreads.items():
        noise = np.random.default_rng([zlib.crc32(name.encode()), seed]).standard_normal(out[name].shape)
        drawn = base * np.exp(spread * noise) if base else spread * noise
        out[name] = jnp.asarray(drawn.astype(out[name].dtype))
    for name, factor in factors.items():
        out[name] = (out[name] * factor).astype(out[name].dtype)
    return out
```

```python
from contextlib import ExitStack

import numpy as np

import concourse.bass as bass
from concourse import mybir

P = 128
BATCH, TOK, D = 2, 1024, 256
CTX = 64
TILES = BATCH * TOK // P
TPB = TOK // P
DC = D // P
EPS = 1e-5

HEADS0, DH0 = 16, 64
INNER = HEADS0 * DH0
PAIRS = HEADS0 // 2
KEYS = TOK + CTX
KCH = TPB + 1
QUADS = 4
FF = 1024
E = 8
SLOT_TILES = 2 * (TILES + E // 2)
ROUND = 12582912.0
LEAD = 8
STEPS = 4 * QUADS

ALU = mybir.AluOpType
ACT = mybir.ActivationFunctionType
AX = mybir.AxisListType
F32 = mybir.dt.float32
I32 = mybir.dt.int32
U32 = mybir.dt.uint32
U8 = mybir.dt.uint8
ds = bass.ds


def layer_norm_transposed(nc, tag, x, h, ps, ident, affine, out_t, nested, add_residual, keep_rows=False):
    with ExitStack() as ctx:
        sb = lambda n, s, dt=F32: ctx.enter_context(nc.sbuf_tensor(f"{tag}_{n}", s, dt))
        sem = lambda n: ctx.enter_context(nc.semaphore(f"{tag}_{n}"))
        six = sb("six", [P, TILES, 6])
        mean, diff = sb("mean", [P, TILES]), sb("diff", [P, TILES])
        ve = sb("ve", [P, TILES])
        neghalf = sb("neghalf", [P, TILES])
        rstd = sb("rstd", [P, TILES])
        stage = sb("stage", [P, 4, D])
        stats_done, agg, rstd_ready = sem("stats_done"), sem("agg"), sem("rstd_ready")
        const_ready, staged, transposed, evacuated = sem("const_ready"), sem("staged"), sem("transposed"), sem("evacuated")
        resid = sem("resid")
        rounds = 2 if nested else 1
        block = ctx.enter_context(nc.Block())

        @block.vector
        def _(dve):
            def statistics(src, r):
                with dve.Fori(0, TILES) as t:
                    nc.vector.bn_stats(six[:, t, :], src[:, t, :]).then_inc(stats_done, 1)
                dve.wait_ge(stats_done, (2 * r + 1) * TILES)
                mean_e, mean_o, m2_e, m2_o = six[:, :, 1], six[:, :, 4], six[:, :, 2], six[:, :, 5]
                nc.vector.tensor_tensor(mean[:], mean_e, mean_o, ALU.add).then_inc(agg, 1)
                nc.vector.tensor_tensor(diff[:], mean_e, mean_o, ALU.subtract).then_inc(agg, 1)
                nc.vector.tensor_tensor(ve[:], m2_e, m2_o, ALU.add).then_inc(agg, 1)
                dve.wait_ge(agg, 7 * r + 3)
                nc.vector.tensor_scalar(mean[:], mean[:], 0.5, None, ALU.mult).then_inc(agg, 1)
                nc.vector.scalar_tensor_tensor(diff[:], diff[:], 0.25, diff[:], ALU.mult, ALU.mult).then_inc(agg, 1)
                nc.vector.tensor_scalar(ve[:], ve[:], 1.0 / D, EPS, ALU.mult, ALU.add).then_inc(agg, 1)
                dve.wait_ge(agg, 7 * r + 6)
                nc.vector.tensor_tensor(ve[:], ve[:], diff[:], ALU.add).then_inc(agg, 1)
                dve.wait_ge(agg, 7 * r + 7)
                dve.wait_ge(rstd_ready, r + 1)

            statistics(x, 0)
            if nested:
                with dve.Fori(0, TILES) as t:
                    nc.vector.tensor_scalar(h[:, t, :], x[:, t, :], mean[:, ds(t, 1)], rstd[:, ds(t, 1)],
                                            ALU.subtract, ALU.mult).then_inc(stats_done, 1)
                dve.wait_ge(stats_done, 2 * TILES)
                if add_residual:
                    nc.vector.tensor_tensor(x[:, :, :], x[:, :, :], h[:, :, :], ALU.add).then_inc(resid, 1)
                    dve.wait_ge(resid, 1)
                statistics(h, 1)
            src = h if nested else x
            with dve.Fori(0, TILES // 4) as g:
                dve.wait_ge(transposed, g * DC + LEAD)
                for j in range(4):
                    nc.vector.tensor_scalar(stage[:, j, :], src[:, g * 4 + j, :], mean[:, ds(g * 4 + j, 1)],
                                            rstd[:, ds(g * 4 + j, 1)], ALU.subtract, ALU.mult).then_inc(staged, 1)
                if keep_rows:
                    dve.wait_ge(staged, g * 4 + 4)
                    for j in range(4):
                        row = src[:, g * 4 + j, :]
                        nc.vector.tensor_scalar(row, row, mean[:, ds(g * 4 + j, 1)], rstd[:, ds(g * 4 + j, 1)],
                                                ALU.subtract, ALU.mult).then_inc(resid, 1)
            if keep_rows:
                dve.wait_ge(resid, TILES + (1 if add_residual else 0))

        @block.gpsimd
        def _(pool):
            nc.gpsimd.memset(neghalf[:], -0.5).then_inc(const_ready, 1)
            pool.wait_ge(const_ready, 1)
            for r in range(rounds):
                pool.wait_ge(agg, 7 * (r + 1))
                nc.gpsimd.tensor_tensor(rstd[:], ve[:], neghalf[:], ALU.pow).then_inc(rstd_ready, 1)

        @block.tensor
        def _(pe):
            pe.sem_inc(transposed, LEAD)
            with pe.Fori(0, TILES // 4) as g:
                pe.wait_ge(staged, g * 4 + 4)
                pe.wait_ge(evacuated, g * DC + LEAD)
                for c in range(DC):
                    for j in range(4):
                        mm = nc.tensor.transpose(ps[:, c, j * P:(j + 1) * P], stage[:, j, c * P:(c + 1) * P], ident[:])
                    mm.then_inc(transposed, 1)

        @block.scalar
        def _(act):
            act.sem_inc(evacuated, LEAD)
            with act.Fori(0, TILES // 4) as g:
                for c in range(DC):
                    act.wait_ge(transposed, g * DC + c + 1 + LEAD)
                    dst = out_t[:, c, ds(g * 4 * P, 4 * P)]
                    if affine is None:
                        nc.scalar.activation(dst, ps[:, c, :], ACT.Copy).then_inc(evacuated, 1)
                    else:
                        w, b = affine
                        nc.scalar.activation(dst, ps[:, c, :], ACT.Identity, bias=b[:, c:c + 1],
                                             scale=w[:, c:c + 1]).then_inc(evacuated, 1)
            act.wait_ge(evacuated, TILES // 4 * DC + LEAD)


VECTORS = [("L0_xattn_ln1_w", D), ("L0_xattn_ln1_b", D), ("L0_xattn_ln2_w", D), ("L0_xattn_ln2_b", D),
           ("L0_ffn_gamma", D), ("L0_ffn_beta", D), ("L1_ffn_b1", FF), ("L1_ffn_quantum_phases", FF),
           ("L1_ffn_quantum_weights_real", FF), ("L1_ffn_quantum_weights_imag", FF)]
VROWS = sum(n // P for _, n in VECTORS)


def vector_columns():
    at, out = 0, {}
    for name, n in VECTORS:
        out[name] = (at, at + n // P)
        at += n // P
    return out


def load_and_prepare(nc, a, x_sb, ctx_sb, ctx_t, ctx_ln_t, ident, ps, vecs):
    with ExitStack() as ctx:
        sb = lambda n, s, dt=F32: ctx.enter_context(nc.sbuf_tensor(f"prep_{n}", s, dt))
        sem = lambda n: ctx.enter_context(nc.semaphore(f"prep_{n}"))
        six, mv, ve, rstd, neghalf = sb("six", [P, 6]), sb("mv", [P, 2]), sb("ve", [P, 1]), sb("rstd", [P, 1]), sb("nh", [P, 1])
        cn = sb("cn", [P, D])
        vrows = sb("vrows", [VROWS, P])
        x_loaded, ctx_loaded, vec_loaded = sem("x_loaded"), sem("ctx_loaded"), sem("vec_loaded")
        id_zero, id_ready, step, pool_step = sem("id_zero"), sem("id_ready"), sem("step"), sem("pool_step")
        turned, evac = sem("turned"), sem("evac")
        block = ctx.enter_context(nc.Block())

        @block.sync
        def _(sp):
            sp.dma_start(ctx_sb[:], a["ctx_1024"].rearrange("b s d -> (b s) d")).then_inc(ctx_loaded, 16)
            sp.dma_start(x_sb[:], a["x"].rearrange("b (t p) d -> p (b t) d", p=P)).then_inc(x_loaded, 16)
            for name, (r0, r1) in vector_columns().items():
                sp.dma_start(vrows[r0:r1, :], a[name].rearrange("(c p) -> c p", p=P)).then_inc(vec_loaded, 16)
            sp.wait_ge(x_loaded, 16)

        @block.gpsimd
        def _(pool):
            nc.gpsimd.memset(ident[:], 0.0).then_inc(id_zero, 1)
            nc.gpsimd.memset(neghalf[:], -0.5).then_inc(id_zero, 1)
            pool.wait_ge(id_zero, 2)
            nc.gpsimd.affine_select(out=ident[:], in_=ident[:], compare_op=ALU.not_equal, fill=1.0, base=0,
                                    pattern=[[-1, P]], channel_multiplier=1).then_inc(id_ready, 1)
            pool.wait_ge(step, 3)
            nc.gpsimd.tensor_tensor(rstd[:], ve[:], neghalf[:], ALU.pow).then_inc(pool_step, 1)

        @block.vector
        def _(dve):
            dve.wait_ge(ctx_loaded, 16)
            nc.vector.bn_stats(six[:], ctx_sb[:]).then_inc(step, 1)
            dve.wait_ge(step, 1)
            nc.vector.bn_aggr(mv[:], six[:]).then_inc(step, 1)
            dve.wait_ge(step, 2)
            nc.vector.tensor_scalar(ve[:], mv[:, 1:2], EPS, None, ALU.add).then_inc(step, 1)
            dve.wait_ge(pool_step, 1)
            nc.vector.tensor_scalar(cn[:], ctx_sb[:], mv[:, 0:1], rstd[:, 0:1], ALU.subtract, ALU.mult).then_inc(step, 1)

        @block.tensor
        def _(pe):
            pe.wait_ge(id_ready, 1)
            pe.wait_ge(ctx_loaded, 16)
            for c in range(DC):
                nc.tensor.transpose(ps[:, 0, c * P:(c + 1) * P], ctx_sb[:, c * P:(c + 1) * P], ident[:]).then_inc(turned, 1)
            pe.wait_ge(vec_loaded, 16 * len(VECTORS))
            nc.tensor.transpose(ps[:, 2, 0:VROWS], vrows[:, :], ident[0:VROWS, 0:VROWS]).then_inc(turned, 1)
            pe.wait_ge(step, 4)
            for c in range(DC):
                nc.tensor.transpose(ps[:, 1, c * P:(c + 1) * P], cn[:, c * P:(c + 1) * P], ident[:]).then_inc(turned, 1)

        @block.scalar
        def _(act):
            act.wait_ge(turned, DC)
            for c in range(DC):
                nc.scalar.activation(ctx_t[:, c, :], ps[:, 0, c * P:(c + 1) * P], ACT.Copy).then_inc(evac, 1)
            act.wait_ge(turned, DC + 1)
            nc.scalar.activation(vecs[:, :], ps[:, 2, 0:VROWS], ACT.Copy).then_inc(evac, 1)
            act.wait_ge(evac, DC + 1)
            act.wait_ge(turned, 2 * DC + 1)
            w, b = (vecs[:, slice(*vector_columns()[n])] for n in ("L0_xattn_ln1_w", "L0_xattn_ln1_b"))
            for c in range(DC):
                nc.scalar.activation(ctx_ln_t[:, c, :], ps[:, 1, c * P:(c + 1) * P], ACT.Identity,
                                     bias=b[:, c:c + 1], scale=w[:, c:c + 1]).then_inc(evac, 1)
            act.wait_ge(evac, 2 * DC + 1)


def perceiver_attention(nc, a, x_sb, ln_t, ctx_ln_t, ident, ps):
    psf = ps[:, :, :].rearrange("p b n -> p (b n)")
    with ExitStack() as ctx:
        sb = lambda n, s, dt=F32: ctx.enter_context(nc.sbuf_tensor(f"at_{n}", s, dt))
        sem = lambda n: ctx.enter_context(nc.semaphore(f"at_{n}"))
        wq = sb("wq", [P, DC, INNER])
        wkv = sb("wkv", [P, DC, 2 * INNER])
        wo = sb("wo", [P, PAIRS, D])
        lnb = sb("lnb", [P, DC, KEYS])
        wst = sb("wst", [P, 3, DC, P])
        qt = sb("qt", [P, TOK])
        kt = sb("kt", [P, KEYS])
        vst = sb("vst", [P, KCH, 2, P])
        probs = sb("probs", [P, 2, KCH * P])
        pt = sb("pt", [P, 2, KCH, 4 * P])
        nmx = sb("nmx", [P, 2])
        recip = sb("recip", [DH0, 4 * P])
        ot = sb("ot", [P, PAIRS, TOK])
        w_loaded, ones_set, batch_copied, w_staged = sem("w_loaded"), sem("ones_set"), sem("batch_copied"), sem("w_staged")
        q_proj, k_proj, v_proj = sem("q_proj"), sem("k_proj"), sem("v_proj")
        qk_evac, v_evac = sem("qk_evac"), sem("v_evac")
        s_done, max_done, exp_done, t_done = sem("s_done"), sem("max_done"), sem("exp_done"), sem("t_done")
        pt_dve, pt_act, pv_done = sem("pt_dve"), sem("pt_act"), sem("pv_done")
        recip_done, norm_done = sem("recip_done"), sem("norm_done")
        wo_done, x_added = sem("wo_done"), sem("x_added")
        TB, OB = 6, 7
        block = ctx.enter_context(nc.Block())

        @block.sync
        def _(sp):
            sp.dma_start(wq[:], a["L0_xattn_Wq"].rearrange("(c p) n -> p c n", p=P)).then_inc(w_loaded, 16)
            sp.dma_start(wkv[:], a["L0_xattn_Wkv"].rearrange("(c p) n -> p c n", p=P)).then_inc(w_loaded, 16)
            sp.dma_start(wo[:], a["L0_xattn_Wo"].rearrange("(c p) n -> p c n", p=P)).then_inc(w_loaded, 16)

        @block.gpsimd
        def _(pool):
            nc.gpsimd.memset(vst[:, :, :, :], 1.0).then_inc(ones_set, 1)
            nc.gpsimd.memset(probs[:, :, KEYS:], 0.0).then_inc(ones_set, 1)
            pool.wait_ge(w_loaded, 48)
            with pool.Fori(0, BATCH) as b:
                pool.wait_ge(v_proj, b * (3 * PAIRS) + LEAD)
                nc.gpsimd.tensor_copy(lnb[:, :, 0:TOK], ln_t[:, :, ds(b * TOK, TOK)]).then_inc(batch_copied, 1)
                nc.gpsimd.tensor_copy(lnb[:, :, TOK:KEYS], ctx_ln_t[:, :, ds(b * CTX, CTX)]).then_inc(batch_copied, 1)
                with pool.Fori(0, PAIRS) as p:
                    it = b * PAIRS + p
                    pool.wait_ge(v_proj, it * 3 + LEAD)
                    nc.gpsimd.tensor_copy(wst[:, 0], wq[:, :, ds(p * P, P)]).then_inc(w_staged, 1)
                    nc.gpsimd.tensor_copy(wst[:, 1], wkv[:, :, ds(p * P, P)]).then_inc(w_staged, 1)
                    nc.gpsimd.tensor_copy(wst[:, 2], wkv[:, :, ds(p * P + INNER, P)]).then_inc(w_staged, 1)

        @block.tensor
        def _(pe):
            def scores(it, n, k0, k1):
                h, tile, base = n // 8, n % 8, 3 * (n % 2)
                hp = slice(DH0 * h, DH0 * h + DH0)
                for k in range(k0, k1):
                    w = min(512, KEYS - 512 * k)
                    mm = nc.tensor.matmul(ps[:, base + k, 0:w], qt[hp, tile * P:(tile + 1) * P],
                                          kt[hp, 512 * k:512 * k + w], start=True, stop=True)
                if k1 == 3:
                    mm.then_inc(s_done, 1)

            def turn(it, n, g):
                for c in range(4 * g, min(4 * g + 4, KCH)):
                    mm = nc.tensor.transpose(ps[:, TB, (c % 4) * P:(c % 4) * P + P],
                                             probs[:, n % 2, c * P:(c + 1) * P], ident[:])
                mm.then_inc(t_done, 1)

            def values(it, qd, c0, c1):
                for c in range(c0, c1):
                    w = min(P, KEYS - c * P)
                    mm = nc.tensor.matmul(ps[:, OB, :], vst[0:w, c, qd // 2, :], pt[0:w, qd % 2, c, :],
                                          start=(c == 0), stop=(c == KCH - 1))
                if c1 == KCH:
                    mm.then_inc(pv_done, 1)

            pe.wait_ge(w_loaded, 48)
            for s in (q_proj, k_proj, v_proj, s_done, t_done, pv_done, wo_done):
                pe.sem_inc(s, LEAD)
            pe.wait_ge(ones_set, 2)
            with pe.Fori(0, BATCH) as b:
                with pe.Fori(0, PAIRS) as p:
                    it = b * PAIRS + p
                    pe.wait_ge(batch_copied, b * 2 + 2)
                    pe.wait_ge(x_added, b * TPB + LEAD)
                    pe.wait_ge(w_staged, it * 3 + 3)
                    pe.wait_ge(exp_done, it * STEPS + LEAD)
                    pe.wait_ge(pt_dve, it * (2 * STEPS) + LEAD)
                    pe.wait_ge(norm_done, it * QUADS + LEAD)
                    for nb in range(2):
                        for c in range(DC):
                            mm = nc.tensor.matmul(ps[:, nb, :], wst[:, 0, c, :], lnb[:, c, nb * 512:(nb + 1) * 512],
                                                  start=(c == 0), stop=(c == DC - 1))
                    mm.then_inc(q_proj, 1)
                    for k in range(3):
                        w = min(512, KEYS - 512 * k)
                        for c in range(DC):
                            mm = nc.tensor.matmul(ps[:, 3 + k, 0:w], wst[:, 1, c, :], lnb[:, c, 512 * k:512 * k + w],
                                                  start=(c == 0), stop=(c == DC - 1))
                    mm.then_inc(k_proj, 1)
                    for g, bank in enumerate((2, TB, OB)):
                        for j in range(4 * g, min(4 * g + 4, KCH)):
                            w = min(P, KEYS - j * P)
                            for c in range(DC):
                                mm = nc.tensor.matmul(ps[0:w, bank, (j % 4) * P:(j % 4) * P + P],
                                                      lnb[:, c, j * P:j * P + w], wst[:, 2, c, :],
                                                      start=(c == 0), stop=(c == DC - 1))
                        mm.then_inc(v_proj, 1)
                    pe.wait_ge(qk_evac, it * 2 + 2 + LEAD)
                    pe.wait_ge(v_evac, it * 3 + 3 + LEAD)
                    scores(it, 0, 0, 3)
                    for n in range(STEPS + 1):
                        if n >= 1:
                            pe.wait_ge(exp_done, it * STEPS + n + LEAD)
                            pe.wait_ge(pt_dve, it * (2 * STEPS) + 2 * (n - 1) + LEAD)
                            turn(it, n - 1, 0)
                        if n + 1 < STEPS:
                            scores(it, n + 1, 0, 1)
                        if n >= 1:
                            pe.wait_ge(pt_dve, it * (2 * STEPS) + 2 * (n - 1) + 1 + LEAD)
                            turn(it, n - 1, 1)
                        if n + 1 < STEPS:
                            scores(it, n + 1, 1, 3)
                        if n >= 1:
                            pe.wait_ge(pt_act, it * STEPS + n + LEAD)
                            turn(it, n - 1, 2)
                        if n >= 5 and n % 4 != 0:
                            qd, part = (n - 5) // 4, (n - 5) % 4
                            if part == 0:
                                pe.wait_ge(pt_dve, it * (2 * STEPS) + 8 * (qd + 1) + LEAD)
                                pe.wait_ge(pt_act, it * STEPS + 4 * (qd + 1) + LEAD)
                                pe.wait_ge(norm_done, it * QUADS + qd + LEAD)
                            values(it, qd, 3 * part, 3 * part + 3)
                    pe.wait_ge(pt_dve, (it + 1) * (2 * STEPS) + LEAD)
                    pe.wait_ge(pt_act, (it + 1) * STEPS + LEAD)
                    pe.wait_ge(norm_done, it * QUADS + QUADS - 1 + LEAD)
                    values(it, QUADS - 1, 0, KCH)
                pe.wait_ge(norm_done, (b + 1) * (PAIRS * QUADS) + LEAD)
                pe.wait_ge(exp_done, (b + 1) * (PAIRS * STEPS) + LEAD)
                for i in range(TPB):
                    if i >= 4:
                        pe.wait_ge(x_added, b * TPB + i - 3 + LEAD)
                    for pr in range(PAIRS):
                        mm = nc.tensor.matmul(ps[:, i % 4, 0:D], ot[:, pr, i * P:(i + 1) * P], wo[:, pr, :],
                                              start=(pr == 0), stop=(pr == PAIRS - 1))
                    mm.then_inc(wo_done, 1)

        @block.scalar
        def _(act):
            for s in (qk_evac, exp_done, pt_act):
                act.sem_inc(s, LEAD)
            with act.Fori(0, BATCH) as b:
                with act.Fori(0, PAIRS) as p:
                    it = b * PAIRS + p
                    act.wait_ge(q_proj, it + 1 + LEAD)
                    act.wait_ge(s_done, it * STEPS + LEAD)
                    nc.scalar.activation(qt[:, :], psf[:, 0:TOK], ACT.Copy, scale=1.0 / 8.0).then_inc(qk_evac, 1)
                    act.wait_ge(k_proj, it + 1 + LEAD)
                    nc.scalar.activation(kt[:, :], psf[:, 3 * 512:3 * 512 + KEYS], ACT.Copy).then_inc(qk_evac, 1)
                    for n in range(STEPS + 1):
                        if n < STEPS:
                            act.wait_ge(max_done, it * STEPS + n + 1 + LEAD)
                            act.wait_ge(t_done, it * (3 * STEPS) + 3 * max(n - 1, 0) + LEAD)
                            lo = 3 * 512 * (n % 2)
                            nc.scalar.activation(probs[:, n % 2, 0:KEYS], psf[:, lo:lo + KEYS], ACT.Exp,
                                                 bias=nmx[:, n % 2:n % 2 + 1]).then_inc(exp_done, 1)
                        if n >= 1:
                            m = n - 1
                            act.wait_ge(t_done, it * (3 * STEPS) + 3 * m + 2 + LEAD)
                            act.wait_ge(pv_done, it * QUADS + max(m // 4 - 1, 0) + LEAD)
                            nc.scalar.activation(pt[:, (m // 4) % 2, 4:8, (m % 4) * P:(m % 4) * P + P],
                                                 ps[:, TB, :].rearrange("p (c q) -> p c q", c=4),
                                                 ACT.Copy).then_inc(pt_act, 1)

        @block.vector
        def _(dve):
            def row_max(it, n):
                dve.wait_ge(s_done, it * STEPS + n + 1 + LEAD)
                lo = 3 * 512 * (n % 2)
                nc.vector.tensor_reduce(nmx[:, n % 2:n % 2 + 1], psf[:, lo:lo + KEYS], AX.X, ALU.max,
                                        negate=True).then_inc(max_done, 1)

            def reciprocal(it, qd):
                dve.wait_ge(pv_done, it * QUADS + qd + 1 + LEAD)
                nc.vector.reciprocal(recip[:, :], ps[DH0:P, OB, :]).then_inc(recip_done, 1)

            def normalise(it, p, qd):
                dve.wait_ge(recip_done, it * QUADS + qd + 1 + LEAD)
                h = qd // 2
                nc.vector.tensor_tensor(ot[DH0 * h:DH0 * h + DH0, p, (qd % 2) * 512:(qd % 2) * 512 + 512],
                                        ps[0:DH0, OB, :], recip[:, :], ALU.mult).then_inc(norm_done, 1)

            dve.wait_ge(ones_set, 2)
            for s in (v_evac, max_done, pt_dve, recip_done, norm_done, x_added):
                dve.sem_inc(s, LEAD)
            with dve.Fori(0, BATCH) as b:
                with dve.Fori(0, PAIRS) as p:
                    it = b * PAIRS + p
                    dve.wait_ge(pv_done, it * QUADS + LEAD)
                    for g, bank in enumerate((2, TB, OB)):
                        n = min(4, KCH - 4 * g)
                        w = min(P, KEYS - 4 * g * P)
                        dve.wait_ge(v_proj, it * 3 + g + 1 + LEAD)
                        nc.vector.tensor_copy(vst[0:w, 4 * g:4 * g + n, :, 0:DH0],
                                              ps[0:w, bank, 0:n * P].rearrange("p (c h d) -> p c h d", h=2, d=DH0)
                                              ).then_inc(v_evac, 1)
                    row_max(it, 0)
                    for n in range(STEPS + 1):
                        if n >= 8 and n % 4 == 0:
                            reciprocal(it, n // 4 - 2)
                        if n >= 1:
                            m = n - 1
                            dst = pt[:, (m // 4) % 2, :, (m % 4) * P:(m % 4) * P + P]
                            dve.wait_ge(t_done, it * (3 * STEPS) + 3 * m + 1 + LEAD)
                            dve.wait_ge(pv_done, it * QUADS + max(m // 4 - 1, 0) + LEAD)
                            nc.vector.tensor_copy(dst[:, 0:4, :], ps[:, TB, :].rearrange("p (c q) -> p c q", c=4)
                                                  ).then_inc(pt_dve, 1)
                        if n + 1 < STEPS:
                            row_max(it, n + 1)
                        if n >= 1:
                            dve.wait_ge(t_done, it * (3 * STEPS) + 3 * m + 3 + LEAD)
                            nc.vector.tensor_copy(dst[0:CTX, 8, :], ps[0:CTX, TB, 0:P]).then_inc(pt_dve, 1)
                        if n >= 8 and n % 4 == 0:
                            normalise(it, p, n // 4 - 2)
                    reciprocal(it, QUADS - 1)
                    normalise(it, p, QUADS - 1)
                for i in range(TPB):
                    dve.wait_ge(wo_done, b * TPB + i + 1 + LEAD)
                    nc.vector.tensor_tensor(x_sb[:, b * TPB + i, :], ps[:, i % 4, 0:D], x_sb[:, b * TPB + i, :],
                                            ALU.add).then_inc(x_added, 1)
            dve.wait_ge(x_added, BATCH * TPB + LEAD)


def route(nc, a, outer, xn_t, h, ps):
    slots = nc.dram_tensor("slot_rows", [SLOT_TILES * P, D], F32, kind="Internal").ap()
    results = nc.dram_tensor("slot_results", [SLOT_TILES * P, D], F32, kind="Internal").ap()
    keep = lambda n, s, dt=F32: outer.enter_context(nc.sbuf_tensor(f"moe_{n}", s, dt, side="right"))
    slot = [keep(f"slot{k}", [P, TILES], U32) for k in range(2)]
    share = [keep(f"share{k}", [P, TILES]) for k in range(2)]
    tile_expert = keep("tile_expert", [P, SLOT_TILES], I32)
    gather_route(nc, a, xn_t, ps, slot, share, tile_expert)
    with ExitStack() as c1:
        zero = c1.enter_context(nc.sbuf_tensor("moe_zero", [P, D], F32))
        zeroed, zset, scattered = (c1.enter_context(nc.semaphore(f"moe_{n}")) for n in ("zeroed", "zset", "scattered"))
        block = c1.enter_context(nc.Block())

        @block.vector
        def _(dve):
            nc.vector.memset(zero[:], 0.0).then_inc(zset, 1)

        @block.sync
        def _(sp):
            sp.wait_ge(zset, 1)
            sp.dma_start(slots.rearrange("(t p) d -> p t d", p=P),
                         zero[:, :].unsqueeze(1).to_broadcast([P, SLOT_TILES, D])).then_inc(zeroed, 16)

        @block.gpsimd
        def _(pool):
            pool.wait_ge(zeroed, 16)
            for k in range(2):
                for t in range(TILES):
                    pool.indirect_dma_start(slots[:, :], bass.IndirectOffsetOnAxis(ap=slot[k][:, t:t + 1], axis=0),
                                            h[:, t, :], None).then_inc(scattered, 16)
            pool.wait_ge(scattered, 16 * 2 * TILES)
    return slots, results, slot, share, tile_expert


def run_experts(nc, a, x_sb, ident, ps, gamma, beta, tables):
    slots, results, slot, share, tile_expert = tables
    expert_tiles(nc, a, ident, ps, gamma, beta, slots, results, tile_expert)
    combine(nc, x_sb, slot, share, results)


def gather_route(nc, a, xn_t, ps, slot, share, tile_expert):
    with ExitStack() as ctx:
        sb = lambda n, s, dt=F32: ctx.enter_context(nc.sbuf_tensor(f"rt_{n}", s, dt))
        sem = lambda n: ctx.enter_context(nc.semaphore(f"rt_{n}"))
        gw = sb("gw", [P, DC, E])
        TE = [P, TILES, E]
        prob, work, ohs, one1, one2, base = (sb(n, TE) for n in ("prob", "work", "ohs", "one1", "one2", "base"))
        scan = [sb(f"scan{i}", TE) for i in range(2)]
        top1, top2, red = sb("top1", [P, TILES]), sb("top2", [P, TILES]), sb("red", [P, TILES])
        escan = [sb(f"escan{i}", [P, E]) for i in range(2)]
        padded, start = sb("padded", [P, E]), sb("start", [P, E])
        erank = sb("erank", [P, E])
        tstart = sb("tstart", [P, SLOT_TILES])
        cmp = sb("cmp", [P, SLOT_TILES, E])
        tsum = sb("tsum", [P, SLOT_TILES])
        lower, ones = sb("lower", [P, P]), sb("ones", [P, P])
        gw_loaded, const, logits_done, v, exped, counted = (sem(n) for n in ("gw", "const", "logits", "v", "exped", "counted"))
        block = ctx.enter_context(nc.Block())

        @block.sync
        def _(sp):
            sp.dma_start(gw[:], a["L0_ffn_gate_w"].rearrange("(c p) e -> p c e", p=P)).then_inc(gw_loaded, 16)

        @block.gpsimd
        def _(pool):
            nc.gpsimd.memset(ones[:], 1.0).then_inc(const, 1)
            nc.gpsimd.memset(lower[:], 1.0).then_inc(const, 1)
            nc.gpsimd.iota(erank[:], [[-1, E]], base=E, channel_multiplier=0,
                           allow_small_or_imprecise_dtypes=True).then_inc(const, 1)
            nc.gpsimd.iota(tstart[:], [[P, SLOT_TILES]], base=0, channel_multiplier=0,
                           allow_small_or_imprecise_dtypes=True).then_inc(const, 1)
            pool.wait_ge(const, 4)
            nc.gpsimd.affine_select(out=lower[:], in_=lower[:], compare_op=ALU.is_gt, fill=0.0, base=0,
                                    pattern=[[1, P]], channel_multiplier=-1).then_inc(const, 1)

        @block.tensor
        def _(pe):
            pe.wait_ge(gw_loaded, 16)
            for t in range(TILES):
                for c in range(DC):
                    mm = nc.tensor.matmul(ps[:, 0, t * E:(t + 1) * E], xn_t[:, c, t * P:(t + 1) * P], gw[:, c, :],
                                          start=(c == 0), stop=(c == DC - 1))
            mm.then_inc(logits_done, 1)
            pe.wait_ge(const, 5)
            pe.wait_ge(counted, 1)
            flat = ohs[:, :, :].rearrange("p t e -> p (t e)")
            nc.tensor.matmul(ps[:, 1, 0:TILES * E], lower[:], flat, start=True, stop=True).then_inc(counted, 1)
            nc.tensor.matmul(ps[:, 2, 0:TILES * E], ones[:], flat, start=True, stop=True).then_inc(counted, 1)

        @block.scalar
        def _(act):
            act.wait_ge(v, 2)
            nc.scalar.activation(prob[:, :, :], work[:, :, :], ACT.Exp).then_inc(exped, 1)

        @block.vector
        def _(dve):
            n = [0]

            def step(ins):
                n[0] += 1
                ins.then_inc(v, 1)
                dve.wait_ge(v, n[0])

            def bcast(x):
                return x[:, :].unsqueeze(2).to_broadcast(TE)

            V = nc.vector
            logits = ps[:, 0, 0:TILES * E].rearrange("p (t e) -> p t e", e=E)
            prefix = ps[:, 1, 0:TILES * E].rearrange("p (t e) -> p t e", e=E)
            total = ps[:, 2, 0:TILES * E].rearrange("p (t e) -> p t e", e=E)
            rank = erank[:, :].unsqueeze(1).to_broadcast(TE)
            dve.wait_ge(logits_done, 1)
            step(V.tensor_reduce(red[:], logits, AX.X, ALU.max))
            step(V.tensor_tensor(work[:], logits, bcast(red), ALU.subtract))
            dve.wait_ge(exped, 1)
            step(V.tensor_reduce(red[:], prob[:], AX.X, ALU.add))
            step(V.reciprocal(red[:], red[:]))
            step(V.tensor_tensor(prob[:], prob[:], bcast(red), ALU.mult))
            dve.wait_ge(const, 5)

            def pick(one, top):
                step(V.tensor_reduce(top[:], prob[:], AX.X, ALU.max))
                step(V.tensor_tensor(work[:], prob[:], bcast(top), ALU.is_equal))
                step(V.tensor_tensor(work[:], work[:], rank, ALU.mult))
                step(V.tensor_reduce(red[:], work[:], AX.X, ALU.max))
                step(V.tensor_tensor(one[:], bcast(red), rank, ALU.is_equal))

            pick(one1, top1)
            step(V.scalar_tensor_tensor(prob[:], one1[:], -4.0, prob[:], ALU.mult, ALU.add))
            pick(one2, top2)
            step(V.tensor_tensor(red[:], top1[:], top2[:], ALU.add))
            step(V.reciprocal(red[:], red[:]))
            step(V.tensor_tensor(share[0][:], top1[:], red[:], ALU.mult))
            step(V.tensor_tensor(share[1][:], top2[:], red[:], ALU.mult))
            V.tensor_tensor(ohs[:], one1[:], one2[:], ALU.add).then_inc(counted, 1)
            dve.wait_ge(counted, 3)
            step(V.tensor_copy(scan[0][:], total))
            src, s = 0, 1
            while s < TILES:
                step(V.tensor_copy(scan[1 - src][:, 0:s, :], scan[src][:, 0:s, :]))
                step(V.tensor_tensor(scan[1 - src][:, s:, :], scan[src][:, s:, :], scan[src][:, :TILES - s, :], ALU.add))
                src, s = 1 - src, 2 * s
            inclusive = scan[src]
            step(V.tensor_scalar(padded[:], inclusive[:, TILES - 1, :], 1.0 / P, 127.0 / P - 0.5 + 0.5 / P, ALU.mult, ALU.add))
            step(V.tensor_scalar(padded[:], padded[:], ROUND, None, ALU.add))
            step(V.tensor_scalar(padded[:], padded[:], ROUND, float(P), ALU.subtract, ALU.mult))
            step(V.tensor_copy(escan[0][:], padded[:]))
            es, s = 0, 1
            while s < E:
                step(V.tensor_copy(escan[1 - es][:, 0:s], escan[es][:, 0:s]))
                step(V.tensor_tensor(escan[1 - es][:, s:], escan[es][:, s:], escan[es][:, :E - s], ALU.add))
                es, s = 1 - es, 2 * s
            end = escan[es]
            step(V.tensor_tensor(start[:], end[:], padded[:], ALU.subtract))
            step(V.tensor_tensor(base[:], inclusive[:], total, ALU.subtract))
            step(V.tensor_tensor(base[:], base[:], prefix, ALU.add))
            step(V.tensor_tensor(base[:], base[:], start[:, :].unsqueeze(1).to_broadcast(TE), ALU.add))
            for k, one in enumerate((one1, one2)):
                step(V.tensor_tensor(work[:], one[:], base[:], ALU.mult))
                step(V.tensor_reduce(red[:], work[:], AX.X, ALU.add))
                step(V.tensor_copy(slot[k][:], red[:]))
            SE = [P, SLOT_TILES, E]
            step(V.tensor_tensor(cmp[:], end[:, :].unsqueeze(1).to_broadcast(SE), tstart[:, :].unsqueeze(2).to_broadcast(SE),
                                 ALU.is_le))
            step(V.tensor_reduce(tsum[:], cmp[:], AX.X, ALU.add))
            step(V.tensor_scalar(tile_expert[:], tsum[:], float(E - 1), None, ALU.min))


def expert_tiles(nc, a, ident, ps, gamma, beta, slots, results, tile_expert):
    with ExitStack() as ctx:
        sb = lambda n, s, dt=F32: ctx.enter_context(nc.sbuf_tensor(f"ex_{n}", s, dt))
        sem = lambda n: ctx.enter_context(nc.semaphore(f"ex_{n}"))
        FC = FF // P
        w1 = sb("w1", [P, E * DC * FF])
        w2 = sb("w2", [P, E * FC * D])
        rows = sb("rows", [P, 2, D])
        b1r = sb("b1r", [P, 2, FF])
        b2r = sb("b2r", [P, 2, D])
        xt = sb("xt", [P, 2, DC, P])
        hid = sb("hid", [P, 2, FF])
        hid_t = sb("hid_t", [P, 2, FC, P])
        y = sb("y", [P, 2, D])
        w_loaded = sem("w_loaded")
        rows_loaded, b1_loaded, b2_loaded, stored = ([sem(f"{n}{j}") for j in range(2)]
                                                     for n in ("rows_loaded", "b1_loaded", "b2_loaded", "stored"))
        x_turned, x_evac, h_done, h_biased, h_act = (sem(n) for n in ("x_turned", "x_evac", "h_done", "h_biased", "h_act"))
        g_turned, g_evac_act, g_evac_dve, y_done, y_biased = (sem(n) for n in ("g_turned", "g_evac_act", "g_evac_dve", "y_done", "y_biased"))
        XB, HB, TB, YB = 0, 1, 5, 7
        NT = SLOT_TILES
        block = ctx.enter_context(nc.Block())

        @block.sync
        def _(sp):
            for s in rows_loaded + b1_loaded + b2_loaded + stored:
                sp.sem_inc(s, LEAD)
            w1_src = a["L0_ffn_w1"].rearrange("e (c p) h -> p e c h", p=P)
            w2_src = a["L0_ffn_w2"].rearrange("e (f p) d -> p e f d", p=P)
            w1_dst = w1[:, :].rearrange("p (e c h) -> p e c h", e=E, c=DC)
            w2_dst = w2[:, :].rearrange("p (e f d) -> p e f d", e=E, f=FC)
            for e in range(E):
                sp.dma_start(w1_dst[:, e], w1_src[:, e]).then_inc(w_loaded, 16)
                sp.dma_start(w2_dst[:, e], w2_src[:, e]).then_inc(w_loaded, 16)
            def load(s, j, store):
                e = sp.value_load(tile_expert[0:1, ds(s, 1)], min_val=0, max_val=E - 1)
                sp.wait_ge(x_turned, s - 1 + LEAD)
                sp.dma_start(rows[:, j, :], slots[ds(s * P, P), :]).then_inc(rows_loaded[j], 16)
                sp.wait_ge(h_biased, s - 1 + LEAD)
                sp.dma_start(b1r[:, j, :], a["L0_ffn_b1"][ds(e, 1), :].partition_broadcast(P)).then_inc(b1_loaded[j], 16)
                sp.wait_ge(y_biased, s - 1 + LEAD)
                sp.dma_start(b2r[:, j, :], a["L0_ffn_b2"][ds(e, 1), :].partition_broadcast(P)).then_inc(b2_loaded[j], 16)
                if store:
                    sp.dma_start(results[ds((s - 2) * P, P), :], y[:, j, :]).then_inc(stored[j], 16)

            for j in range(2):
                load(j, j, False)
            with sp.Fori(1, NT // 2) as u:
                for j in range(2):
                    load(u * 2 + j, j, True)
            for j in range(2):
                sp.wait_ge(y_biased, NT - 1 + j + LEAD)
                sp.dma_start(results[(NT - 2 + j) * P:(NT - 1 + j) * P, :], y[:, j, :]).then_inc(stored[j], 16)
            for j in range(2):
                sp.wait_ge(stored[j], NT // 2 * 16 + LEAD)

        @block.tensor
        def _(pe):
            for s in (x_turned, h_done, g_turned, y_done):
                pe.sem_inc(s, LEAD)

            def turn_rows(s, u, j):
                pe.wait_ge(rows_loaded[j], (u + 1) * 16 + LEAD)
                pe.wait_ge(x_evac, s * DC + LEAD)
                for c in range(DC):
                    mm = nc.tensor.transpose(ps[:, XB, c * P:(c + 1) * P], rows[:, j, c * P:(c + 1) * P], ident[:])
                mm.then_inc(x_turned, 1)

            def first_layer(s, j):
                e = pe.value_load(tile_expert[0:1, ds(s, 1)], min_val=0, max_val=E - 1)
                pe.wait_ge(x_evac, s * DC + DC + LEAD)
                pe.wait_ge(h_biased, s - 1 + LEAD)
                for nb in range(2):
                    for c in range(DC):
                        mm = nc.tensor.matmul(ps[:, HB + 2 * j + nb, :], xt[:, j, c, :],
                                              w1[:, ds(e * (DC * FF) + (c * FF + nb * 512), 512)],
                                              start=(c == 0), stop=(c == DC - 1))
                mm.then_inc(h_done, 1)

            def turn_hidden(s, j):
                pe.wait_ge(h_act, s + 1 + LEAD)
                pe.wait_ge(g_evac_act, s + LEAD)
                pe.wait_ge(g_evac_dve, s + LEAD)
                for f in range(FC):
                    mm = nc.tensor.transpose(ps[:, TB + f // 4, (f % 4) * P:(f % 4) * P + P],
                                             hid[:, j, f * P:(f + 1) * P], ident[:])
                    if f % 4 == 3:
                        mm.then_inc(g_turned, 1)

            def second_layer(s, j):
                e = pe.value_load(tile_expert[0:1, ds(s, 1)], min_val=0, max_val=E - 1)
                pe.wait_ge(g_evac_act, s + 1 + LEAD)
                pe.wait_ge(g_evac_dve, s + 1 + LEAD)
                pe.wait_ge(y_biased, s + LEAD)
                for f in range(FC):
                    mm = nc.tensor.matmul(ps[:, YB, 0:D], hid_t[:, j, f, :], w2[:, ds(e * (FC * D) + f * D, D)],
                                          start=(f == 0), stop=(f == FC - 1))
                mm.then_inc(y_done, 1)

            def step(s, j, nxt):
                if nxt:
                    turn_rows(*nxt)
                turn_hidden(s, j)
                if nxt:
                    first_layer(nxt[0], nxt[2])
                second_layer(s, j)

            turn_rows(0, 0, 0)
            pe.wait_ge(w_loaded, 32 * E)
            first_layer(0, 0)
            with pe.Fori(0, NT // 2 - 1) as u:
                step(u * 2, 0, (u * 2 + 1, u, 1))
                step(u * 2 + 1, 1, (u * 2 + 2, u + 1, 0))
            step(NT - 2, 0, (NT - 1, NT // 2 - 1, 1))
            step(NT - 1, 1, None)

        @block.scalar
        def _(act):
            for s in (x_evac, h_act, g_evac_act):
                act.sem_inc(s, LEAD)

            def rows_out(s, j):
                act.wait_ge(x_turned, s + 1 + LEAD)
                act.wait_ge(h_done, s - 1 + LEAD)
                for c in range(DC):
                    nc.scalar.activation(xt[:, j, c, :], ps[:, XB, c * P:(c + 1) * P], ACT.Identity,
                                         bias=beta[:, c:c + 1], scale=gamma[:, c:c + 1]).then_inc(x_evac, 1)

            def gelu(s, j):
                act.wait_ge(h_biased, s + 1 + LEAD)
                nc.scalar.activation(hid[:, j, :], hid[:, j, :], ACT.Gelu).then_inc(h_act, 1)

            def hidden_out(s, j):
                act.wait_ge(g_turned, s * 2 + 1 + LEAD)
                act.wait_ge(y_done, s - 1 + LEAD)
                nc.scalar.activation(hid_t[:, j, 0:4, :], ps[:, TB, :].rearrange("p (f q) -> p f q", f=4),
                                     ACT.Copy).then_inc(g_evac_act, 1)

            def step(s, j, nxt):
                if nxt:
                    rows_out(nxt[0], nxt[1])
                hidden_out(s, j)
                if nxt:
                    gelu(nxt[0], nxt[1])

            rows_out(0, 0)
            gelu(0, 0)
            with act.Fori(0, NT // 2 - 1) as u:
                step(u * 2, 0, (u * 2 + 1, 1))
                step(u * 2 + 1, 1, (u * 2 + 2, 0))
            step(NT - 2, 0, (NT - 1, 1))
            step(NT - 1, 1, None)

        @block.vector
        def _(dve):
            for s in (h_biased, g_evac_dve, y_biased):
                dve.sem_inc(s, LEAD)

            def add_b1(s, u, j):
                dve.wait_ge(h_done, s + 1 + LEAD)
                dve.wait_ge(b1_loaded[j], (u + 1) * 16 + LEAD)
                dve.wait_ge(g_turned, s * 2 - 2 + LEAD)
                nc.vector.tensor_tensor(hid[:, j, :].rearrange("p (b n) -> p b n", b=2), ps[:, HB + 2 * j:HB + 2 * j + 2, :],
                                        b1r[:, j, :].rearrange("p (b n) -> p b n", b=2), ALU.add).then_inc(h_biased, 1)

            def hidden_out(s, j):
                dve.wait_ge(g_turned, s * 2 + 2 + LEAD)
                dve.wait_ge(y_done, s - 1 + LEAD)
                nc.vector.tensor_copy(hid_t[:, j, 4:8, :], ps[:, TB + 1, :].rearrange("p (f q) -> p f q", f=4)
                                      ).then_inc(g_evac_dve, 1)

            def add_b2(s, u, j):
                dve.wait_ge(y_done, s + 1 + LEAD)
                dve.wait_ge(b2_loaded[j], (u + 1) * 16 + LEAD)
                dve.wait_ge(stored[j], u * 16 + LEAD)
                nc.vector.tensor_tensor(y[:, j, :], ps[:, YB, 0:D], b2r[:, j, :], ALU.add).then_inc(y_biased, 1)

            def step(s, u, j, nxt):
                hidden_out(s, j)
                if nxt:
                    add_b1(*nxt)
                add_b2(s, u, j)

            add_b1(0, 0, 0)
            with dve.Fori(0, NT // 2 - 1) as u:
                step(u * 2, u, 0, (u * 2 + 1, u, 1))
                step(u * 2 + 1, u, 1, (u * 2 + 2, u + 1, 0))
            step(NT - 2, NT // 2 - 1, 0, (NT - 1, NT // 2 - 1, 1))
            step(NT - 1, NT // 2 - 1, 1, None)


def combine(nc, x_sb, slot, share, results):
    with ExitStack() as ctx:
        NBUF = 4
        got = ctx.enter_context(nc.sbuf_tensor("cb_got", [P, NBUF, D], F32))
        gathered = [ctx.enter_context(nc.semaphore(f"cb_gathered{i}")) for i in range(NBUF)]
        added = ctx.enter_context(nc.semaphore("cb_added"))
        block = ctx.enter_context(nc.Block())

        @block.gpsimd
        def _(pool):
            for n in range(2 * TILES):
                if n >= NBUF:
                    pool.wait_ge(added, n - NBUF + 1)
                pool.indirect_dma_start(got[:, n % NBUF, :], None, results[:, :],
                                        bass.IndirectOffsetOnAxis(ap=slot[n % 2][:, n // 2:n // 2 + 1], axis=0)
                                        ).then_inc(gathered[n % NBUF], 16)

        @block.vector
        def _(dve):
            for n in range(2 * TILES):
                t = n // 2
                dve.wait_ge(gathered[n % NBUF], 16 * (n // NBUF + 1))
                if n % 2:
                    dve.wait_ge(added, n)
                nc.vector.scalar_tensor_tensor(x_sb[:, t, :], got[:, n % NBUF, :], share[n % 2][:, t:t + 1],
                                               x_sb[:, t, :], ALU.mult, ALU.add).then_inc(added, 1)
            dve.wait_ge(added, 2 * TILES)


def masked_attention(nc, a, x_sb, h_t, ctx_t, ident, ps):
    HEADS, DH, HALF = 16, 16, 8
    with ExitStack() as ctx:
        sb = lambda n, s, dt=F32: ctx.enter_context(nc.sbuf_tensor(f"ma_{n}", s, dt))
        sem = lambda n: ctx.enter_context(nc.semaphore(f"ma_{n}"))
        wq, wkv, wp = sb("wq", [P, DC, D]), sb("wkv", [P, DC, 2 * D]), sb("wp", [P, DC, D])
        bproj = sb("bproj", [P, D])
        mask = sb("mask", [P, TILES, CTX // 4], I32)
        cap = sb("cap", [P, TILES, CTX])
        hmask = sb("hmask", [P, HALF])
        ctx2 = sb("ctx2", [P, DC, BATCH, 2, CTX])
        k_diag = sb("k_diag", [P, BATCH * 2 * HALF * CTX])
        kt = sb("kt", [P, 2, P])
        v_diag = sb("v_diag", [P, BATCH, HEADS // 2, P])
        vb = sb("vb", [P, HEADS // 2, P])
        qt = sb("qt", [P, 2, 512])
        score = sb("score", [P, 2, HEADS, CTX])
        top, negtop, den = sb("top", [P, 2, HEADS]), sb("negtop", [P, 2, HEADS]), sb("den", [P, 2, HEADS])
        etop = sb("etop", [P, 2, HEADS])
        pt = sb("pt", [P, HEADS // 2, 4 * P])
        ot = sb("ot", [P, 2, 4 * P])
        w_loaded, m_loaded, const, dupd, kv_done, k_out, v_out, prep = (sem(n) for n in (
            "w_loaded", "m_loaded", "const", "dupd", "kv_done", "k_out", "v_out", "prep"))
        vb_ready, q_done, q_evac, s_done, capped, shifted, exped, rec, summed, normed, t_done = (sem(n) for n in (
            "vb_ready", "q_done", "q_evac", "s_done", "capped", "shifted", "exped", "rec", "summed", "normed", "t_done"))
        t_act, t_dve, o_done, o_evac, p_done, x_added, etop_done = (sem(n) for n in (
            "t_act", "t_dve", "o_done", "o_evac", "p_done", "x_added", "etop_done"))
        FMAX = float(np.finfo(np.float32).max)
        block = ctx.enter_context(nc.Block())

        @block.sync
        def _(sp):
            sp.dma_start(wkv[:], a["L1_xattn_Wkv"].rearrange("(c p) n -> p c n", p=P)).then_inc(w_loaded, 16)
            sp.dma_start(wq[:], a["L1_xattn_Wq"].rearrange("(c p) n -> p c n", p=P)).then_inc(w_loaded, 16)
            sp.dma_start(wp[:], a["L1_xattn_Wproj"].rearrange("(c p) n -> p c n", p=P)).then_inc(w_loaded, 16)
            sp.dma_start(mask[:], a["mask_BxSxS2_bk0"].rearrange("b (t p) k -> p (b t) k", p=P)).then_inc(m_loaded, 16)
            sp.dma_start(bproj[:], a["L1_xattn_bproj"].partition_broadcast(P)).then_inc(m_loaded, 16)

        @block.gpsimd
        def _(pool):
            pool.sem_inc(normed, LEAD)
            pool.sem_inc(vb_ready, LEAD)
            nc.gpsimd.memset(hmask[:], 1.0).then_inc(const, 1)
            nc.gpsimd.memset(v_diag[:, :, :, :], 0.0).then_inc(const, 1)
            pool.wait_ge(const, 2)
            nc.gpsimd.affine_select(out=hmask[:], in_=hmask[:], compare_op=ALU.is_ge, fill=0.0, base=0,
                                    pattern=[[-DH, HALF]], channel_multiplier=1).then_inc(const, 1)
            pool.wait_ge(const, 3)
            nc.gpsimd.affine_select(out=hmask[:], in_=hmask[:], compare_op=ALU.is_ge, fill=0.0, base=DH - 1,
                                    pattern=[[DH, HALF]], channel_multiplier=-1).then_inc(const, 1)
            pool.wait_ge(v_out, BATCH * HEADS)
            with pool.Fori(0, BATCH) as b:
                pool.wait_ge(o_done, b * 2 + LEAD)
                nc.gpsimd.tensor_copy(vb[:, :, :], v_diag[:, b, :, :]).then_inc(vb_ready, 1)
                with pool.Fori(0, 2) as g2:
                    for j in range(4):
                        n = (b * 2 + g2) * 4 + j
                        pool.wait_ge(summed, n + 1 + LEAD)
                        nc.gpsimd.tensor_tensor(score[:, j % 2], score[:, j % 2],
                                                den[:, j % 2, :].unsqueeze(2).to_broadcast([P, HEADS, CTX]),
                                                ALU.mult).then_inc(normed, 1)

        @block.tensor
        def _(pe):
            for s in (q_done, s_done, t_done, o_done, p_done):
                pe.sem_inc(s, LEAD)
            pe.wait_ge(w_loaded, 48)
            for m in range(2):
                for c in range(DC):
                    mm = nc.tensor.matmul(ps[:, 0, m * P:(m + 1) * P], wkv[:, c, m * P:(m + 1) * P], ctx_t[:, c, :],
                                          start=(c == 0), stop=(c == DC - 1))
            mm.then_inc(kv_done, 1)
            pe.wait_ge(dupd, DC)
            for b in range(BATCH):
                for c in range(DC):
                    mm = nc.tensor.matmul(ps[:, 1 + b, 0:D], ctx2[:, c, b, :, :].rearrange("p r k -> p (r k)"),
                                          wkv[:, c, D:2 * D], start=(c == 0), stop=(c == DC - 1))
            mm.then_inc(kv_done, 1)
            pe.wait_ge(k_out, 5)
            pe.wait_ge(v_out, BATCH * HEADS)

            with pe.Fori(0, BATCH) as b:
                with pe.Fori(0, 2) as g2:
                    g = b * 2 + g2

                    def scores(j):
                        n = g * 4 + j
                        pe.wait_ge(capped, n - 1 + LEAD)
                        for m in range(2):
                            mm = nc.tensor.matmul(ps[:, 2 + 2 * (j % 2) + m, :], qt[:, m, j * P:(j + 1) * P],
                                                  k_diag[:, ds(b * (2 * HALF * CTX) + m * (HALF * CTX), HALF * CTX)],
                                                  start=True, stop=True)
                        mm.then_inc(s_done, 1)

                    pe.wait_ge(o_evac, g * 2 + LEAD)
                    pe.wait_ge(vb_ready, b + 1 + LEAD)
                    for m in range(2):
                        for c in range(DC):
                            mm = nc.tensor.matmul(ps[:, m, :], wq[:, c, m * P:(m + 1) * P], h_t[:, c, ds(g * 512, 512)],
                                                  start=(c == 0), stop=(c == DC - 1))
                    mm.then_inc(q_done, 1)
                    pe.wait_ge(q_evac, g + 1 + LEAD)
                    scores(0)
                    scores(1)
                    for j in range(4):
                        n = g * 4 + j
                        pe.wait_ge(normed, n + 1 + LEAD)
                        pe.wait_ge(t_act, n + LEAD)
                        pe.wait_ge(t_dve, n + LEAD)
                        pe.wait_ge(x_added, g * 4 + LEAD)
                        for k in range(HEADS // 2):
                            mm = nc.tensor.transpose(ps[:, 6 + k // 4, (k % 4) * P:(k % 4) * P + P],
                                                     score[:, j % 2, 2 * k:2 * k + 2, :].rearrange("p h k -> p (h k)"), ident[:])
                        mm.then_inc(t_done, 1)
                        if j + 2 < 4:
                            scores(j + 2)
                    pe.wait_ge(t_act, g * 4 + 4 + LEAD)
                    pe.wait_ge(t_dve, g * 4 + 4 + LEAD)
                    for k in range(HEADS // 2):
                        mm = nc.tensor.matmul(ps[:, k // 4, :], vb[:, k, :], pt[:, k, :], start=(k % 4 == 0), stop=(k % 4 == 3))
                    mm.then_inc(o_done, 1)
                    pe.wait_ge(o_evac, g * 2 + 2 + LEAD)
                    for j in range(4):
                        if j >= 2:
                            pe.wait_ge(x_added, g * 4 + j - 1 + LEAD)
                        for c in range(DC):
                            mm = nc.tensor.matmul(ps[:, 6 + j % 2, 0:D], ot[:, c, j * P:(j + 1) * P], wp[:, c, :],
                                                  start=(c == 0), stop=(c == DC - 1))
                        mm.then_inc(p_done, 1)

        @block.scalar
        def _(act):
            for s in (q_evac, exped, etop_done, t_act, o_evac):
                act.sem_inc(s, LEAD)
            for c in range(DC):
                nc.scalar.activation(ctx2[:, c], ctx_t[:, c, :].rearrange("p (b k) -> p b k", b=BATCH).unsqueeze(2)
                                     .to_broadcast([P, BATCH, 2, CTX]), ACT.Copy).then_inc(dupd, 1)
            act.wait_ge(kv_done, 1)
            nc.scalar.activation(kt[:, :, :], ps[:, 0, 0:2 * P].rearrange("p (m k) -> p m k", m=2), ACT.Copy).then_inc(k_out, 1)
            with act.Fori(0, BATCH) as b:
                with act.Fori(0, 2) as g2:
                    g = b * 2 + g2
                    act.wait_ge(q_done, g + 1 + LEAD)
                    act.wait_ge(s_done, g * 4 + LEAD)
                    nc.scalar.activation(qt[:, :, :], ps[:, 0:2, :], ACT.Copy).then_inc(q_evac, 1)
                    for j in range(4):
                        n = g * 4 + j
                        act.wait_ge(shifted, n + 1 + LEAD)
                        nc.scalar.activation(score[:, j % 2], score[:, j % 2], ACT.Exp, scale=0.25).then_inc(exped, 1)
                        nc.scalar.activation(etop[:, j % 2, :], top[:, j % 2, :], ACT.Exp, scale=-0.25).then_inc(etop_done, 1)
                        act.wait_ge(t_done, n + 1 + LEAD)
                        act.wait_ge(o_done, g + LEAD)
                        nc.scalar.activation(pt[:, 0:4, j * P:(j + 1) * P], ps[:, 6, :].rearrange("p (k q) -> p k q", k=4),
                                             ACT.Copy).then_inc(t_act, 1)
                    act.wait_ge(o_done, g + 1 + LEAD)
                    act.wait_ge(p_done, g * 4 + LEAD)
                    for c in range(2):
                        nc.scalar.activation(ot[:, c, :], ps[:, c, :], ACT.Copy).then_inc(o_evac, 1)

        @block.vector
        def _(dve):
            for s in (capped, shifted, summed, t_dve, x_added):
                dve.sem_inc(s, LEAD)
            V = nc.vector
            dve.wait_ge(m_loaded, 32)
            V.tensor_scalar(cap[:, :, :], mask[:, :, :].bitcast(U8), -2.0, 1.0, ALU.mult, ALU.add).then_inc(prep, 1)
            V.tensor_tensor(x_sb[:, :, :], x_sb[:, :, :], bproj[:, :].unsqueeze(1).to_broadcast([P, TILES, D]),
                            ALU.add).then_inc(prep, 1)
            dve.wait_ge(prep, 2)
            V.tensor_scalar(cap[:, :, :], cap[:, :, :], FMAX, None, ALU.mult).then_inc(prep, 1)
            dve.wait_ge(prep, 3)
            dve.wait_ge(k_out, 1)
            dve.wait_ge(const, 4)
            for b in range(BATCH):
                for m in range(2):
                    o = (b * 2 + m) * HALF * CTX
                    V.tensor_tensor(k_diag[:, o:o + HALF * CTX].rearrange("p (h k) -> p h k", h=HALF),
                                    kt[:, m, b * CTX:(b + 1) * CTX].unsqueeze(1).to_broadcast([P, HALF, CTX]),
                                    hmask[:, :].unsqueeze(2).to_broadcast([P, HALF, CTX]), ALU.mult).then_inc(k_out, 1)
            dve.wait_ge(kv_done, 2)
            for b in range(BATCH):
                for h in range(HEADS):
                    r = slice(CTX * (h % 2), CTX * (h % 2) + CTX)
                    col = (h % HALF) * DH
                    V.tensor_copy(v_diag[r, b, h // 2, col:col + DH], ps[r, 1 + b, h * DH:(h + 1) * DH]).then_inc(v_out, 1)

            with dve.Fori(0, BATCH) as b:
                with dve.Fori(0, 2) as g2:
                    g = b * 2 + g2

                    def shift(j):
                        n = g * 4 + j
                        sc = score[:, j % 2]
                        dve.wait_ge(s_done, n + 1 + LEAD)
                        dve.wait_ge(t_done, n - 1 + LEAD)
                        V.tensor_tensor(sc, ps[:, 2 + 2 * (j % 2):4 + 2 * (j % 2), :].rearrange("p m (h k) -> p (m h) k", k=CTX),
                                        cap[:, ds(g * 4 + j, 1), :].to_broadcast([P, HEADS, CTX]), ALU.min).then_inc(capped, 1)
                        dve.wait_ge(capped, n + 1 + LEAD)
                        V.tensor_reduce(top[:, j % 2, :], sc, AX.X, ALU.max).then_inc(rec, 1)
                        dve.wait_ge(rec, n * 4 + 1)
                        V.tensor_scalar(top[:, j % 2, :], top[:, j % 2, :], 0.0, None, ALU.max).then_inc(rec, 1)
                        dve.wait_ge(rec, n * 4 + 2)
                        V.tensor_tensor(sc, sc, top[:, j % 2, :].unsqueeze(2).to_broadcast([P, HEADS, CTX]),
                                        ALU.subtract).then_inc(shifted, 1)

                    def total(j):
                        n = g * 4 + j
                        dve.wait_ge(exped, n + 1 + LEAD)
                        V.tensor_reduce(den[:, j % 2, :], score[:, j % 2], AX.X, ALU.add).then_inc(rec, 1)
                        dve.wait_ge(etop_done, n + 1 + LEAD)
                        dve.wait_ge(rec, n * 4 + 3)
                        V.tensor_tensor(den[:, j % 2, :], den[:, j % 2, :], etop[:, j % 2, :], ALU.add).then_inc(rec, 1)
                        dve.wait_ge(rec, n * 4 + 4)
                        V.reciprocal(den[:, j % 2, :], den[:, j % 2, :]).then_inc(summed, 1)

                    for j in range(4):
                        n = g * 4 + j
                        shift(j)
                        total(j)
                        dve.wait_ge(t_done, n + 1 + LEAD)
                        dve.wait_ge(o_done, g + LEAD)
                        V.tensor_copy(pt[:, 4:8, j * P:(j + 1) * P], ps[:, 7, :].rearrange("p (k q) -> p k q", k=4)).then_inc(t_dve, 1)
                    for j in range(4):
                        dve.wait_ge(p_done, g * 4 + j + 1 + LEAD)
                        row = x_sb[:, ds(g * 4 + j, 1), :]
                        V.tensor_tensor(row, ps[:, 6 + j % 2, 0:D].unsqueeze(1), row, ALU.add).then_inc(x_added, 1)
            dve.wait_ge(x_added, TILES + LEAD)


def phase_ffn(nc, a, x_sb, h_t, vecs, ps):
    FC, SLOTS, G = FF // P, 4, TILES // 4
    INV2PI = float(np.float32(1 / (2 * np.pi)))
    TWO_PI_HI = 6.28125
    TWO_PI_LO = 2 * np.pi - TWO_PI_HI
    PI_IN = float(np.nextafter(np.float32(np.pi), np.float32(0)))
    b1, theta, wr, wi = (vecs[n] for n in ("L1_ffn_b1", "L1_ffn_quantum_phases", "L1_ffn_quantum_weights_real",
                                           "L1_ffn_quantum_weights_imag"))
    with ExitStack() as ctx:
        sb = lambda n, s, dt=F32: ctx.enter_context(nc.sbuf_tensor(f"ff_{n}", s, dt))
        sem = lambda n: ctx.enter_context(nc.semaphore(f"ff_{n}"))
        w1, w2, b2 = sb("w1", [P, DC, FF]), sb("w2", [P, FC, D]), sb("b2", [P, D])
        red, cosv, sinv, coef = (sb(n, [P, FC]) for n in ("red", "cosv", "sinv", "coef"))
        hid, arg, turns, mixed = (sb(n, [P, SLOTS, 512]) for n in ("hid", "arg", "turns", "mixed"))
        w_loaded, small, s_act = sem("w_loaded"), sem("small"), sem("s_act")
        h_done, h_out, arg_done, k_rough, k_done, r_step, r_done, sin_done, q_done, relu_done, y_done, x_added = (
            sem(n) for n in ("h_done", "h_out", "arg_done", "k_rough", "k_done", "r_step", "r_done", "sin_done",
                             "q_done", "relu_done", "y_done", "x_added"))
        block = ctx.enter_context(nc.Block())

        @block.sync
        def _(sp):
            sp.dma_start(w1[:], a["L1_ffn_W1"].rearrange("(c p) n -> p c n", p=P)).then_inc(w_loaded, 16)
            sp.dma_start(w2[:], a["L1_ffn_W2"].rearrange("(f p) n -> p f n", p=P)).then_inc(w_loaded, 16)
            sp.dma_start(b2[:], a["L1_ffn_b2"].partition_broadcast(P)).then_inc(w_loaded, 16)

        @block.tensor
        def _(pe):
            for s in (h_done, y_done):
                pe.sem_inc(s, LEAD)
            pe.wait_ge(w_loaded, 48)
            with pe.Fori(0, G) as g:
                for n in range(FC + 4):
                    if n < FC:
                        pe.wait_ge(h_out, g * FC + (n - 3) + LEAD)
                        for c in range(DC):
                            mm = nc.tensor.matmul(ps[:, n % 4, :], w1[:, c, n * P:(n + 1) * P], h_t[:, c, ds(g * 512, 512)],
                                                  start=(c == 0), stop=(c == DC - 1))
                        mm.then_inc(h_done, 1)
                    if n >= 4:
                        f = n - 4
                        pe.wait_ge(relu_done, g * FC + f + 1 + LEAD)
                        if f == 0:
                            pe.wait_ge(x_added, g * 4 + LEAD)
                        for j in range(4):
                            mm = nc.tensor.matmul(ps[:, 4 + j, 0:D], mixed[:, f % SLOTS, j * P:(j + 1) * P], w2[:, f, :],
                                                  start=(f == 0), stop=(f == FC - 1))
                        mm.then_inc(y_done, 1)

        @block.scalar
        def _(act):
            for s in (h_out, k_done, sin_done, relu_done):
                act.sem_inc(s, LEAD)
            act.wait_ge(small, 6)
            nc.scalar.activation(sinv[:], red[:], ACT.Sin).then_inc(s_act, 1)
            nc.scalar.activation(cosv[:], cosv[:], ACT.Sin).then_inc(s_act, 1)
            with act.Fori(0, G) as g:
                for n in range(FC + 3):
                    if n < FC:
                        act.wait_ge(h_done, g * FC + n + 1 + LEAD)
                        act.wait_ge(q_done, g * FC + n - 3 + LEAD)
                        nc.scalar.activation(hid[:, n % SLOTS, :], ps[:, n % 4, :], ACT.Identity,
                                             bias=b1[:, n:n + 1]).then_inc(h_out, 1)
                    if 1 <= n <= FC:
                        f = n - 1
                        act.wait_ge(k_rough, g * FC + f + 1 + LEAD)
                        nc.scalar.activation(turns[:, f % SLOTS, :], turns[:, f % SLOTS, :], ACT.Copy,
                                             bias=-ROUND).then_inc(k_done, 1)
                    if 2 <= n <= FC + 1:
                        f = n - 2
                        act.wait_ge(r_done, g * FC + f + 1 + LEAD)
                        nc.scalar.activation(arg[:, f % SLOTS, :], arg[:, f % SLOTS, :], ACT.Sin).then_inc(sin_done, 1)
                    if n >= 3:
                        f = n - 3
                        act.wait_ge(q_done, g * FC + f + 1 + LEAD)
                        nc.scalar.activation(mixed[:, f % SLOTS, :], mixed[:, f % SLOTS, :], ACT.Relu).then_inc(relu_done, 1)

        @block.vector
        def _(dve):
            for s in (arg_done, k_rough, r_step, r_done, q_done, x_added):
                dve.sem_inc(s, LEAD)
            V = nc.vector
            n_small = [0]

            def step(ins):
                n_small[0] += 1
                ins.then_inc(small, 1)
                dve.wait_ge(small, n_small[0])

            step(V.tensor_scalar(red[:], theta, INV2PI, ROUND, ALU.mult, ALU.add))
            step(V.tensor_scalar(red[:], red[:], ROUND, None, ALU.subtract))
            step(V.scalar_tensor_tensor(coef[:], red[:], -TWO_PI_HI, theta, ALU.mult, ALU.add))
            step(V.scalar_tensor_tensor(red[:], red[:], -TWO_PI_LO, coef[:], ALU.mult, ALU.add))
            step(V.tensor_scalar(red[:], red[:], -PI_IN, PI_IN, ALU.max, ALU.min))
            V.tensor_scalar(coef[:], red[:], -1.0, None, ALU.mult).then_inc(s_act, 1)
            dve.wait_ge(s_act, 1)
            V.tensor_tensor(cosv[:], coef[:], red[:], ALU.min).then_inc(s_act, 1)
            dve.wait_ge(s_act, 2)
            step(V.tensor_scalar(cosv[:], cosv[:], float(np.pi / 2), None, ALU.add))
            dve.wait_ge(s_act, 4)
            step(V.tensor_tensor(cosv[:], cosv[:], wr, ALU.mult))
            step(V.tensor_tensor(sinv[:], sinv[:], wi, ALU.mult))
            step(V.tensor_tensor(coef[:], cosv[:], sinv[:], ALU.add))
            step(V.scalar_tensor_tensor(coef[:], coef[:], 0.1, wi, ALU.mult, ALU.mult))
            dve.wait_ge(w_loaded, 48)
            step(V.tensor_tensor(x_sb[:, :, :], x_sb[:, :, :], b2[:, :].unsqueeze(1).to_broadcast([P, TILES, D]), ALU.add))
            with dve.Fori(0, G) as g:
                for n in range(FC + 3):
                    if n < FC:
                        s = n % SLOTS
                        dve.wait_ge(h_out, g * FC + n + 1 + LEAD)
                        V.tensor_scalar(arg[:, s, :], hid[:, s, :], 0.1, theta[:, n:n + 1], ALU.mult, ALU.add).then_inc(arg_done, 1)
                        dve.wait_ge(arg_done, g * FC + n + 1 + LEAD)
                        V.tensor_scalar(turns[:, s, :], arg[:, s, :], INV2PI, ROUND, ALU.mult, ALU.add).then_inc(k_rough, 1)
                    if 1 <= n <= FC:
                        f = n - 1
                        s = f % SLOTS
                        dve.wait_ge(k_done, g * FC + f + 1 + LEAD)
                        V.scalar_tensor_tensor(arg[:, s, :], turns[:, s, :], -TWO_PI_HI, arg[:, s, :], ALU.mult, ALU.add).then_inc(r_step, 1)
                        dve.wait_ge(r_step, g * (2 * FC) + 2 * f + 1 + LEAD)
                        V.scalar_tensor_tensor(arg[:, s, :], turns[:, s, :], -TWO_PI_LO, arg[:, s, :], ALU.mult, ALU.add).then_inc(r_step, 1)
                        dve.wait_ge(r_step, g * (2 * FC) + 2 * f + 2 + LEAD)
                        V.tensor_scalar(arg[:, s, :], arg[:, s, :], -PI_IN, PI_IN, ALU.max, ALU.min).then_inc(r_done, 1)
                    if n >= 3:
                        f = n - 3
                        s = f % SLOTS
                        dve.wait_ge(sin_done, g * FC + f + 1 + LEAD)
                        dve.wait_ge(y_done, g * FC + f - 3 + LEAD)
                        V.scalar_tensor_tensor(mixed[:, s, :], arg[:, s, :], coef[:, f:f + 1], hid[:, s, :], ALU.mult,
                                               ALU.add).then_inc(q_done, 1)
                for j in range(4):
                    dve.wait_ge(y_done, g * FC + FC + LEAD)
                    row = x_sb[:, ds(g * 4 + j, 1), :]
                    V.tensor_tensor(row, ps[:, 4 + j, 0:D].unsqueeze(1), row, ALU.add).then_inc(x_added, 1)
            dve.wait_ge(x_added, TILES + LEAD)


def store_out(nc, out, x_sb):
    with ExitStack() as ctx:
        stored = ctx.enter_context(nc.semaphore("stored"))
        block = ctx.enter_context(nc.Block())

        @block.sync
        def _(sp):
            sp.dma_start(out.rearrange("b (t p) d -> p (b t) d", p=P), x_sb[:]).then_inc(stored, 16)
            sp.wait_ge(stored, 16)


def build(nc, a, out):
    with ExitStack() as ctx:
        sb = lambda n, s, dt=F32: ctx.enter_context(nc.sbuf_tensor(n, s, dt))
        ps = ctx.enter_context(nc.psum_tensor("ps", [P, 8, 512], F32))
        ident = sb("ident", [P, P])
        x_sb = sb("x_sb", [P, TILES, D])
        ctx_sb = sb("ctx_sb", [P, D])
        ctx_t = sb("ctx_t", [P, DC, P])
        vecs = sb("vecs", [P, VROWS])
        aff = {n: vecs[:, r0:r1] for n, (r0, r1) in vector_columns().items()}
        with ExitStack() as c0:
            ctx_ln_t = c0.enter_context(nc.sbuf_tensor("ctx_ln_t", [P, DC, P], F32))
            ln_t = c0.enter_context(nc.sbuf_tensor("ln_t", [P, DC, TILES * P], F32))
            load_and_prepare(nc, a, x_sb, ctx_sb, ctx_t, ctx_ln_t, ident, ps, vecs)
            with nc.sbuf_tensor("h0", [P, TILES, D], F32) as h:
                layer_norm_transposed(nc, "ln0", x_sb, h, ps, ident, (aff["L0_xattn_ln2_w"], aff["L0_xattn_ln2_b"]),
                                      ln_t, nested=True, add_residual=False)
            perceiver_attention(nc, a, x_sb, ln_t, ctx_ln_t, ident, ps)
        with ExitStack() as c1:
            with nc.sbuf_tensor("h1", [P, TILES, D], F32) as h, nc.sbuf_tensor("xn_t", [P, DC, TILES * P], F32) as xn_t:
                layer_norm_transposed(nc, "ln1", x_sb, h, ps, ident, (aff["L0_ffn_gamma"], aff["L0_ffn_beta"]), xn_t,
                                      nested=True, add_residual=True, keep_rows=True)
                tables = route(nc, a, c1, xn_t, h, ps)
            run_experts(nc, a, x_sb, ident, ps, aff["L0_ffn_gamma"], aff["L0_ffn_beta"], tables)
        with nc.sbuf_tensor("h2_t", [P, DC, TILES * P], F32) as h_t:
            layer_norm_transposed(nc, "ln2", x_sb, None, ps, ident, None, h_t, nested=False, add_residual=False)
            masked_attention(nc, a, x_sb, h_t, ctx_t, ident, ps)
        with nc.sbuf_tensor("h3_t", [P, DC, TILES * P], F32) as h_t:
            layer_norm_transposed(nc, "ln3", x_sb, None, ps, ident, None, h_t, nested=False, add_residual=False)
            phase_ffn(nc, a, x_sb, h_t, aff, ps)
        store_out(nc, out, x_sb)


NAMES = ['x', 'ctx_1024', 'mask_BxSxS2_bk0', 'L0_xattn_Wq', 'L0_xattn_Wkv', 'L0_xattn_Wo', 'L0_xattn_ln1_w',
         'L0_xattn_ln1_b', 'L0_xattn_ln2_w', 'L0_xattn_ln2_b', 'L0_ffn_gate_w', 'L0_ffn_w1', 'L0_ffn_b1', 'L0_ffn_w2',
         'L0_ffn_b2', 'L0_ffn_gamma', 'L0_ffn_beta', 'L1_xattn_Wq', 'L1_xattn_Wkv', 'L1_xattn_Wproj', 'L1_xattn_bproj',
         'L1_ffn_W1', 'L1_ffn_b1', 'L1_ffn_quantum_phases', 'L1_ffn_quantum_weights_real',
         'L1_ffn_quantum_weights_imag', 'L1_ffn_W2', 'L1_ffn_b2']


def kernel(**inputs):
    import concourse.bacc as bacc
    from concourse.bass_utils import run_bass_kernel_spmd

    nc = bacc.Bacc("TRN2", target_bir_lowering=False, num_devices=1)
    arrays, handles = {}, {}
    for name in NAMES:
        v = np.ascontiguousarray(inputs[name])
        if v.dtype == np.bool_:
            v = v.view(np.int32)
        arrays[f"in_{name}"] = v
        handles[name] = nc.dram_tensor(f"in_{name}", v.shape, mybir.dt.from_np(v.dtype), kind="ExternalInput").ap()
    out = nc.dram_tensor("out_0", (BATCH, TOK, D), F32, kind="ExternalOutput").ap()
    build(nc, handles, out)
    r = run_bass_kernel_spmd(nc, [arrays], core_ids=[0])
    return r.results[0]["out_0"]
```

```python
from contextlib import ExitStack

import numpy as np

import concourse.bass as bass
from concourse import mybir

P = 128
BATCH, TOK, D = 2, 1024, 256
CTX = 64
TILES = BATCH * TOK // P
TPB = TOK // P
DC = D // P
EPS = 1e-5

HEADS0, DH0 = 16, 64
INNER = HEADS0 * DH0
PAIRS = HEADS0 // 2
KEYS = TOK + CTX
KCH = TPB + 1
FF = 1024
E = 8
SLOT_TILES = 2 * (TILES + E // 2)
ROUND = 12582912.0
LEAD = 8

ALU = mybir.AluOpType
ACT = mybir.ActivationFunctionType
AX = mybir.AxisListType
F32 = mybir.dt.float32
F32R = mybir.dt.float32r
I32 = mybir.dt.int32
U32 = mybir.dt.uint32
U8 = mybir.dt.uint8
ds = bass.ds


def layer_norm_transposed(nc, tag, x, h, ps, ident, affine, out_t, nested, add_residual, keep_rows=False,
                          prefetch=None):
    with ExitStack() as ctx:
        sb = lambda n, s, dt=F32: ctx.enter_context(nc.sbuf_tensor(f"{tag}_{n}", s, dt))
        sem = lambda n: ctx.enter_context(nc.semaphore(f"{tag}_{n}"))
        six = sb("six", [P, TILES, 6])
        mean, diff = sb("mean", [P, TILES]), sb("diff", [P, TILES])
        ve = sb("ve", [P, TILES])
        neghalf = sb("neghalf", [P, TILES])
        rstd = sb("rstd", [P, TILES])
        stage = sb("stage", [P, 4, D])
        stats_done, agg, rstd_ready = sem("stats_done"), sem("agg"), sem("rstd_ready")
        const_ready, staged, transposed, evacuated = sem("const_ready"), sem("staged"), sem("transposed"), sem("evacuated")
        resid = sem("resid")
        rounds = 2 if nested else 1
        block = ctx.enter_context(nc.Block())

        if prefetch:
            @block.sync
            def _(sp):
                prefetch(sp)

        @block.vector
        def _(dve):
            def statistics(src, r):
                with dve.Fori(0, TILES // 4) as g:
                    for j in range(4):
                        t = g * 4 + j
                        nc.vector.bn_stats(six[:, t, :], src[:, t, :]).then_inc(stats_done, 1)
                dve.wait_ge(stats_done, (2 * r + 1) * TILES)
                mean_e, mean_o, m2_e, m2_o = six[:, :, 1], six[:, :, 4], six[:, :, 2], six[:, :, 5]
                nc.vector.tensor_tensor(mean[:], mean_e, mean_o, ALU.add).then_inc(agg, 1)
                nc.vector.tensor_tensor(diff[:], mean_e, mean_o, ALU.subtract).then_inc(agg, 1)
                nc.vector.tensor_tensor(ve[:], m2_e, m2_o, ALU.add).then_inc(agg, 1)
                dve.wait_ge(agg, 7 * r + 3)
                nc.vector.tensor_scalar(mean[:], mean[:], 0.5, None, ALU.mult).then_inc(agg, 1)
                nc.vector.scalar_tensor_tensor(diff[:], diff[:], 0.25, diff[:], ALU.mult, ALU.mult).then_inc(agg, 1)
                nc.vector.tensor_scalar(ve[:], ve[:], 1.0 / D, EPS, ALU.mult, ALU.add).then_inc(agg, 1)
                dve.wait_ge(agg, 7 * r + 6)
                nc.vector.tensor_tensor(ve[:], ve[:], diff[:], ALU.add).then_inc(agg, 1)
                dve.wait_ge(agg, 7 * r + 7)
                dve.wait_ge(rstd_ready, r + 1)

            statistics(x, 0)
            if nested:
                with dve.Fori(0, TILES // 4) as g:
                    for j in range(4):
                        t = g * 4 + j
                        nc.vector.tensor_scalar(h[:, t, :], x[:, t, :], mean[:, ds(t, 1)], rstd[:, ds(t, 1)],
                                                ALU.subtract, ALU.mult).then_inc(stats_done, 1)
                dve.wait_ge(stats_done, 2 * TILES)
                if add_residual:
                    nc.vector.tensor_tensor(x[:, :, :], x[:, :, :], h[:, :, :], ALU.add).then_inc(resid, 1)
                    dve.wait_ge(resid, 1)
                statistics(h, 1)
            src = h if nested else x
            with dve.Fori(0, TILES // 4) as g:
                dve.wait_ge(transposed, g * DC + LEAD)
                for j in range(4):
                    nc.vector.tensor_scalar(stage[:, j, :], src[:, g * 4 + j, :], mean[:, ds(g * 4 + j, 1)],
                                            rstd[:, ds(g * 4 + j, 1)], ALU.subtract, ALU.mult).then_inc(staged, 1)
                if keep_rows:
                    dve.wait_ge(staged, g * 4 + 4)
                    for j in range(4):
                        row = src[:, g * 4 + j, :]
                        nc.vector.tensor_scalar(row, row, mean[:, ds(g * 4 + j, 1)], rstd[:, ds(g * 4 + j, 1)],
                                                ALU.subtract, ALU.mult).then_inc(resid, 1)
            if keep_rows:
                dve.wait_ge(resid, TILES + (1 if add_residual else 0))

        @block.gpsimd
        def _(pool):
            nc.gpsimd.memset(neghalf[:], -0.5).then_inc(const_ready, 1)
            pool.wait_ge(const_ready, 1)
            for r in range(rounds):
                pool.wait_ge(agg, 7 * (r + 1))
                nc.gpsimd.tensor_tensor(rstd[:], ve[:], neghalf[:], ALU.pow).then_inc(rstd_ready, 1)

        @block.tensor
        def _(pe):
            pe.sem_inc(transposed, LEAD)
            with pe.Fori(0, TILES // 4) as g:
                pe.wait_ge(staged, g * 4 + 4)
                pe.wait_ge(evacuated, g * DC + LEAD)
                for c in range(DC):
                    for j in range(4):
                        mm = nc.tensor.transpose(ps[:, c, j * P:(j + 1) * P], stage[:, j, c * P:(c + 1) * P], ident[:])
                    mm.then_inc(transposed, 1)

        @block.scalar
        def _(act):
            act.sem_inc(evacuated, LEAD)
            with act.Fori(0, TILES // 4) as g:
                for c in range(DC):
                    act.wait_ge(transposed, g * DC + c + 1 + LEAD)
                    dst = out_t[:, c, ds(g * 4 * P, 4 * P)]
                    if affine is None:
                        nc.scalar.activation(dst, ps[:, c, :], ACT.Copy).then_inc(evacuated, 1)
                    else:
                        w, b = affine
                        nc.scalar.activation(dst, ps[:, c, :], ACT.Identity, bias=b[:, c:c + 1],
                                             scale=w[:, c:c + 1]).then_inc(evacuated, 1)
            act.wait_ge(evacuated, TILES // 4 * DC + LEAD)


VECTORS = [("L0_xattn_ln1_w", D), ("L0_xattn_ln1_b", D), ("L0_xattn_ln2_w", D), ("L0_xattn_ln2_b", D),
           ("L0_ffn_gamma", D), ("L0_ffn_beta", D), ("L1_ffn_b1", FF), ("L1_ffn_quantum_phases", FF),
           ("L1_ffn_quantum_weights_real", FF), ("L1_ffn_quantum_weights_imag", FF)]
VROWS = sum(n // P for _, n in VECTORS)


def vector_columns():
    at, out = 0, {}
    for name, n in VECTORS:
        out[name] = (at, at + n // P)
        at += n // P
    return out


def load_and_prepare(nc, a, x_sb, ctx_sb, ctx_t, ctx_ln_t, ident, ps, vecs):
    with ExitStack() as ctx:
        sb = lambda n, s, dt=F32: ctx.enter_context(nc.sbuf_tensor(f"prep_{n}", s, dt))
        sem = lambda n: ctx.enter_context(nc.semaphore(f"prep_{n}"))
        six, mv, ve, rstd, neghalf = sb("six", [P, 6]), sb("mv", [P, 2]), sb("ve", [P, 1]), sb("rstd", [P, 1]), sb("nh", [P, 1])
        cn = sb("cn", [P, D])
        vrows = sb("vrows", [VROWS, P])
        x_loaded, ctx_loaded, vec_loaded = sem("x_loaded"), sem("ctx_loaded"), sem("vec_loaded")
        id_zero, id_ready, step, pool_step = sem("id_zero"), sem("id_ready"), sem("step"), sem("pool_step")
        turned, evac = sem("turned"), sem("evac")
        block = ctx.enter_context(nc.Block())

        @block.sync
        def _(sp):
            sp.dma_start(ctx_sb[:], a["ctx_1024"].rearrange("b s d -> (b s) d")).then_inc(ctx_loaded, 16)
            sp.dma_start(x_sb[:], a["x"].rearrange("b (t p) d -> p (b t) d", p=P)).then_inc(x_loaded, 16)
            for name, (r0, r1) in vector_columns().items():
                sp.dma_start(vrows[r0:r1, :], a[name].rearrange("(c p) -> c p", p=P)).then_inc(vec_loaded, 16)
            sp.wait_ge(x_loaded, 16)

        @block.gpsimd
        def _(pool):
            nc.gpsimd.memset(ident[:], 0.0).then_inc(id_zero, 1)
            nc.gpsimd.memset(neghalf[:], -0.5).then_inc(id_zero, 1)
            pool.wait_ge(id_zero, 2)
            nc.gpsimd.affine_select(out=ident[:], in_=ident[:], compare_op=ALU.not_equal, fill=1.0, base=0,
                                    pattern=[[-1, P]], channel_multiplier=1).then_inc(id_ready, 1)
            pool.wait_ge(step, 3)
            nc.gpsimd.tensor_tensor(rstd[:], ve[:], neghalf[:], ALU.pow).then_inc(pool_step, 1)

        @block.vector
        def _(dve):
            dve.wait_ge(ctx_loaded, 16)
            nc.vector.bn_stats(six[:], ctx_sb[:]).then_inc(step, 1)
            dve.wait_ge(step, 1)
            nc.vector.bn_aggr(mv[:], six[:]).then_inc(step, 1)
            dve.wait_ge(step, 2)
            nc.vector.tensor_scalar(ve[:], mv[:, 1:2], EPS, None, ALU.add).then_inc(step, 1)
            dve.wait_ge(pool_step, 1)
            nc.vector.tensor_scalar(cn[:], ctx_sb[:], mv[:, 0:1], rstd[:, 0:1], ALU.subtract, ALU.mult).then_inc(step, 1)

        @block.tensor
        def _(pe):
            pe.wait_ge(id_ready, 1)
            pe.wait_ge(ctx_loaded, 16)
            for c in range(DC):
                nc.tensor.transpose(ps[:, 0, c * P:(c + 1) * P], ctx_sb[:, c * P:(c + 1) * P], ident[:]).then_inc(turned, 1)
            pe.wait_ge(vec_loaded, 16 * len(VECTORS))
            nc.tensor.transpose(ps[:, 2, 0:VROWS], vrows[:, :], ident[0:VROWS, 0:VROWS]).then_inc(turned, 1)
            pe.wait_ge(step, 4)
            for c in range(DC):
                nc.tensor.transpose(ps[:, 1, c * P:(c + 1) * P], cn[:, c * P:(c + 1) * P], ident[:]).then_inc(turned, 1)

        @block.scalar
        def _(act):
            act.wait_ge(turned, DC)
            for c in range(DC):
                nc.scalar.activation(ctx_t[:, c, :], ps[:, 0, c * P:(c + 1) * P], ACT.Copy).then_inc(evac, 1)
            act.wait_ge(turned, DC + 1)
            nc.scalar.activation(vecs[:, :], ps[:, 2, 0:VROWS], ACT.Copy).then_inc(evac, 1)
            act.wait_ge(evac, DC + 1)
            act.wait_ge(turned, 2 * DC + 1)
            w, b = (vecs[:, slice(*vector_columns()[n])] for n in ("L0_xattn_ln1_w", "L0_xattn_ln1_b"))
            for c in range(DC):
                nc.scalar.activation(ctx_ln_t[:, c, :], ps[:, 1, c * P:(c + 1) * P], ACT.Identity,
                                     bias=b[:, c:c + 1], scale=w[:, c:c + 1]).then_inc(evac, 1)
            act.wait_ge(evac, 2 * DC + 1)


def perceiver_attention(nc, a, x_sb, ln_t, ctx_ln_t, ident, ps):
    NQ, SLOTS = TPB, 4
    LAG = 2
    KPAD = TOK + P
    Q_PIECES = [(0, 0, 512), (1, 512, 512)]
    K_PIECES = [(2, 0, 512), (3, 512, 512), (6, TOK, CTX)]
    V_PIECES = [(4, 0, 4), (5, 4, 4), (6, 8, 1)]
    SPLITS = len(Q_PIECES) + len(K_PIECES)
    TB, CB, OB = 4, 6, 7
    psf = ps[:, :, :].rearrange("p b n -> p (b n)")
    with ExitStack() as ctx:
        sb = lambda n, s, dt=F32: ctx.enter_context(nc.sbuf_tensor(f"at_{n}", s, dt))
        sem = lambda n: ctx.enter_context(nc.semaphore(f"at_{n}"))
        w_pair = sb("w_pair", [P, 3, DC, P])
        wo = sb("wo", [P, PAIRS, D])
        lnb = sb("lnb", [P, DC, KPAD])
        q_split = sb("q_split", [P, 2, TOK], F32R)
        k_split = sb("k_split", [P, 2, KEYS], F32R)
        v_split = sb("v_split", [P, 2, KCH, 2, DH0], F32R)
        q_st = sb("q_st", [P, 2, TOK], F32R)
        k_st = sb("k_st", [P, 2, 2, KEYS], F32R)
        v_st = sb("v_st", [P, 2, KCH, 2, DH0], F32R)
        probs = sb("probs", [P, SLOTS, KPAD])
        pt = sb("pt", [P, 2, 2, KCH, 2 * P], F32R)
        s_ctx = sb("s_ctx", [P, NQ, CTX])
        ctx_nmx = sb("ctx_nmx", [P, NQ])
        tok_nmx, nmx = sb("tok_nmx", [P, SLOTS]), sb("nmx", [P, SLOTS])
        den, rden = sb("den", [P, 2, SLOTS]), sb("rden", [P, SLOTS])
        o_low = sb("o_low", [DH0, 2 * P])
        ot = sb("ot", [P, PAIRS, TOK])
        pads_zero, w_loaded, wo_loaded, lnb_loaded = sem("pads_zero"), sem("w_loaded"), sem("wo_loaded"), sem("lnb_loaded")
        qk_proj, v_proj, qk_high, qk_low, v_high, v_low = (
            sem(n) for n in ("qk_proj", "v_proj", "qk_high", "qk_low", "v_high", "v_low"))
        a_stacked, b_stacked, va_stacked, vb_stacked = (sem(n) for n in ("a_stacked", "b_stacked", "va_stacked", "vb_stacked"))
        s_done, max_done, exp_done, rden_done, normed = (sem(n) for n in ("s_done", "max_done", "exp_done", "rden_done", "normed"))
        t_done, pt_high, pt_low, pv_done, o_low_done, o_done = (
            sem(n) for n in ("t_done", "pt_high", "pt_low", "pv_done", "o_low_done", "o_done"))
        wo_done, x_added = sem("wo_done"), sem("x_added")
        c_done, c_copied, c_max, tok_max, den_sum = (sem(n) for n in ("c_done", "c_copied", "c_max", "tok_max", "den_sum"))
        block = ctx.enter_context(nc.Block())

        def pt_group(part, n, g):
            bank = TB + g
            buf = (n // 2) % 2
            if g < 2:
                cols = slice((n % 2) * P, (n % 2) * P + P)
                return pt[:, part, buf, 4 * g:4 * g + 4, cols], ps[:, bank, :].rearrange("p (c q) -> p c q", c=4)
            return pt[:, part, buf, KCH - 1, :], ps[:, bank, 0:2 * P]

        @block.sync
        def _(sp):
            for s in (a_stacked, b_stacked, va_stacked, vb_stacked):
                sp.sem_inc(s, LEAD)

            def load_weights(p):
                for i, (name, at) in enumerate((("L0_xattn_Wq", 0), ("L0_xattn_Wkv", 0), ("L0_xattn_Wkv", INNER))):
                    sp.dma_start(w_pair[:, i], a[name].rearrange("(c p) n -> p c n", p=P)[:, :, ds(p * P + at, P)]
                                 ).then_inc(w_loaded, 16)

            def stack(h, done):
                rows = slice(DH0 * h, DH0 * h + DH0)
                for half in range(2):
                    to = slice(DH0 * half, DH0 * half + DH0)
                    sp.dma_start(q_st[to, h, :].bitcast(F32), q_split[rows, half, :].bitcast(F32)).then_inc(done, 16)
                    sp.dma_start(k_st[to, h, :, :].bitcast(F32), k_split[rows, :, :].bitcast(F32)).then_inc(done, 16)

            with sp.Fori(0, BATCH) as b:
                sp.wait_ge(v_proj, b * (PAIRS * 3) + LEAD)
                sp.dma_start(lnb[:, :, 0:TOK], ln_t[:, :, ds(b * TOK, TOK)]).then_inc(lnb_loaded, 16)
                for i in range(2):
                    at = TOK + i * CTX
                    sp.dma_start(lnb[:, :, at:at + CTX], ctx_ln_t[:, :, ds(b * CTX, CTX)]).then_inc(lnb_loaded, 16)
                with sp.Fori(0, PAIRS) as p:
                    k = b * PAIRS + p
                    sp.wait_ge(v_proj, k * 3 + LEAD)
                    load_weights(p)
                    sp.wait_ge(qk_low, (k + 1) * SPLITS + LEAD)
                    stack(0, a_stacked)
                    sp.wait_ge(v_low, (k + 1) * 3 + LEAD)
                    sp.wait_ge(pv_done, k * 8 - 4 + LEAD)
                    sp.dma_start(v_st[:, 0].bitcast(F32), v_split[:, 0].bitcast(F32)).then_inc(va_stacked, 16)
                    sp.wait_ge(s_done, k * 16 + LEAD)
                    stack(1, b_stacked)
                    sp.wait_ge(pv_done, k * 8 + LEAD)
                    sp.dma_start(v_st[:, 1].bitcast(F32), v_split[:, 1].bitcast(F32)).then_inc(vb_stacked, 16)
            sp.wait_ge(v_proj, BATCH * PAIRS * 3 + LEAD)
            load_weights(0)

        @block.gpsimd
        def _(pool):
            nc.gpsimd.memset(probs[:, :, KEYS:], 0.0).then_inc(pads_zero, 1)
            pool.dma_start(wo[:], a["L0_xattn_Wo"].rearrange("(c p) n -> p c n", p=P)).then_inc(wo_loaded, 16)
            with pool.Fori(0, BATCH * HEADS0 * NQ // SLOTS) as g:
                for i in range(SLOTS):
                    pool.wait_ge(rden_done, g * SLOTS + i + 1)
                    cols = probs[:, i, 0:KEYS]
                    nc.gpsimd.tensor_tensor(cols, cols, rden[:, i:i + 1].to_broadcast([P, KEYS]), ALU.mult).then_inc(normed, 1)

        @block.tensor
        def _(pe):
            for s in (qk_proj, v_proj, s_done, c_done, t_done, pv_done, wo_done):
                pe.sem_inc(s, LEAD)

            def scores(u, n, h):
                pe.wait_ge(exp_done, u * NQ + n - 1 + LEAD)
                for part in range(2):
                    for i in range(2):
                        mm = nc.tensor.matmul(ps[:, 2 * (n % 2) + i, :], q_st[:, h, (n % NQ) * P:(n % NQ) * P + P],
                                              k_st[:, h, part, i * 512:i * 512 + 512], start=(part == 0), stop=(part == 1))
                mm.then_inc(s_done, 1)

            def context_scores(u, n, h):
                pe.wait_ge(pt_low, u * (5 * NQ // 2) + 5 * max(n - LAG, 0) // 2 + LEAD)
                for t in range(NQ):
                    for part in range(2):
                        mm = nc.tensor.matmul(ps[:, CB, t * CTX:(t + 1) * CTX], q_st[:, h, t * P:(t + 1) * P],
                                              k_st[:, h, part, TOK:KEYS], start=(part == 0), stop=(part == 1))
                mm.then_inc(c_done, 1)

            def turn(u, n, g, len_heads):
                gi = 5 * (n // 2) + 2 * (n % 2) + g
                if g == 0:
                    pe.wait_ge(normed, u * NQ + n + 1)
                last = 5 * (n // 2) - 1 if g == 2 else gi - (2 if n % 2 else 3)
                pe.wait_ge(pt_low, u * (5 * NQ // 2) + last + 1 + LEAD)
                if g == 2:
                    pe.wait_ge(c_copied, u + min((n + LAG) // NQ, len_heads - 1) + 1 + LEAD)
                pieces = [(n, 4 * g + i) for i in range(4)] if g < 2 else [(n - 1, KCH - 1), (n, KCH - 1)]
                for i, (m, c) in enumerate(pieces):
                    mm = nc.tensor.transpose(ps[:, TB + g, i * P:(i + 1) * P], probs[:, m % SLOTS, c * P:(c + 1) * P],
                                             ident[:])
                mm.then_inc(t_done, 1)

            def values(u, j, h, c0, c1):
                if c0 == 0:
                    pe.wait_ge(pt_low, u * (5 * NQ // 2) + j * 5 + 5 + LEAD)
                    pe.wait_ge(o_done, u * (NQ // 2) + j + LEAD)
                for c in range(c0, c1):
                    for part in range(2):
                        mm = nc.tensor.matmul(ps[:, OB, 0:2 * P], v_st[:, h, c].rearrange("p l d -> p (l d)"),
                                              pt[:, part, j % 2, c, :], start=(c == 0 and part == 0),
                                              stop=(c == KCH - 1 and part == 1))
                if c1 == KCH:
                    mm.then_inc(pv_done, 1)

            def project_qk(which, pieces):
                for bank, at, w in pieces:
                    for c in range(DC):
                        mm = nc.tensor.matmul(ps[:, bank, 0:w], w_pair[:, which, c, :], lnb[:, c, at:at + w],
                                              start=(c == 0), stop=(c == DC - 1))
                    mm.then_inc(qk_proj, 1)

            def project_v():
                for bank, c0, n in V_PIECES:
                    for c in range(n):
                        for f in range(DC):
                            mm = nc.tensor.matmul(ps[:, bank, c * P:(c + 1) * P], lnb[:, f, (c0 + c) * P:(c0 + c + 1) * P],
                                                  w_pair[:, 2, f, :], start=(f == 0), stop=(f == DC - 1))
                    mm.then_inc(v_proj, 1)

            def phase(u, k, heads, project, own_values):
                nt = NQ * len(heads)
                pe.wait_ge(qk_low, (k + 1) * SPLITS + LEAD)
                for n in range(nt + LAG):
                    m = n - LAG
                    if n < nt:
                        h, dk = heads[n // NQ]
                        if n % NQ == 0:
                            pe.wait_ge(b_stacked if h else a_stacked, (k + dk + 1) * 64 + LEAD)
                        scores(u, n, h)
                        if n % NQ == 0:
                            context_scores(u, n, h)
                    if n == 1 and own_values:
                        pe.wait_ge(pt_low, u * (5 * NQ // 2) + LEAD)
                        pe.wait_ge(c_copied, u + 1 + LEAD)
                        project_v()
                    cuts = []
                    if m >= 2:
                        j, cuts = (m - 2) // 2, ([0, 2, 5], [5, 7, 9])[m % 2]
                        h, dk = heads[j // (NQ // 2)]
                        if m % 2 == 0 and j % (NQ // 2) == 0:
                            pe.wait_ge(vb_stacked if h else va_stacked, (k + dk + 1) * 16 + LEAD)
                    if m >= 0:
                        if m == 0 and own_values:
                            pe.wait_ge(v_low, (k + 1) * 3 + LEAD)
                        turn(u, m, 0, len(heads))
                        turn(u, m, 1, len(heads))
                        if m % 2 == 1:
                            turn(u, m, 2, len(heads))
                        if cuts:
                            values(u, j, h, cuts[0], cuts[2])
                    if n == nt and project:
                        pe.wait_ge(w_loaded, (k + 2) * 48)
                        pe.wait_ge(exp_done, u * NQ + nt - 1 + LEAD)
                        project_qk(0, Q_PIECES)
                    if n == nt + 1 and project:
                        pe.wait_ge(exp_done, u * NQ + nt + LEAD)
                        project_qk(1, K_PIECES[:2])
                h, dk = heads[-1]
                values(u, nt // 2 - 1, h, 0, KCH)
                if project:
                    pe.wait_ge(pt_low, u * (5 * NQ // 2) + 5 * nt // 2 + LEAD)
                    project_qk(1, K_PIECES[2:])

            pe.wait_ge(w_loaded, 48)
            pe.wait_ge(lnb_loaded, 48)
            project_qk(0, Q_PIECES)
            project_qk(1, K_PIECES)
            with pe.Fori(0, BATCH) as b:
                pe.wait_ge(x_added, b * TPB + LEAD)
                phase(b * HEADS0, b * PAIRS, [(0, 0)], True, True)
                with pe.Fori(1, PAIRS) as p:
                    k = b * PAIRS + p
                    pe.wait_ge(lnb_loaded, b * 48 + 48)
                    phase(k * 2 - 1, k, [(1, -1), (0, 0)], True, True)
                phase(b * HEADS0 + (HEADS0 - 1), b * PAIRS + PAIRS, [(1, -1)], False, False)
                pe.wait_ge(wo_loaded, 16)
                pe.wait_ge(o_done, (b + 1) * (HEADS0 * NQ // 2) + LEAD)
                for i in range(TPB):
                    if i >= 4:
                        pe.wait_ge(x_added, b * TPB + i - 3 + LEAD)
                    for pr in range(PAIRS):
                        mm = nc.tensor.matmul(ps[:, i % 4, 0:D], ot[:, pr, i * P:(i + 1) * P], wo[:, pr, :],
                                              start=(pr == 0), stop=(pr == PAIRS - 1))
                    mm.then_inc(wo_done, 1)

        @block.scalar
        def _(act):
            for s in (qk_high, v_high, c_copied, exp_done, pt_high, o_low_done):
                act.sem_inc(s, LEAD)

            def high_qk(k, which, pieces, i0):
                dst, scale = ((q_split, 1.0 / 8.0), (k_split, 1.0))[which]
                for i, (bank, at, w) in enumerate(pieces):
                    act.wait_ge(qk_proj, k * SPLITS + i0 + i + 1 + LEAD)
                    if i0 + i == 0:
                        act.wait_ge(a_stacked, k * 64 + LEAD)
                        act.wait_ge(b_stacked, k * 64 + LEAD)
                    nc.scalar.activation(dst[:, 0, at:at + w], ps[:, bank, 0:w], ACT.Copy, scale=scale).then_inc(qk_high, 1)

            def high_v(k):
                for i, (bank, c0, n) in enumerate(V_PIECES):
                    act.wait_ge(v_proj, k * 3 + i + 1 + LEAD)
                    if i == 0:
                        act.wait_ge(va_stacked, k * 16 + LEAD)
                        act.wait_ge(vb_stacked, k * 16 + LEAD)
                    nc.scalar.activation(v_split[:, :, c0:c0 + n, 0, :],
                                         ps[:, bank, 0:n * P].rearrange("p (c h d) -> p h c d", h=2, d=DH0),
                                         ACT.Copy).then_inc(v_high, 1)

            def copy_context(u, n):
                act.wait_ge(c_done, u + n // NQ + 1 + LEAD)
                act.wait_ge(exp_done, u * NQ + n + LEAD)
                nc.scalar.activation(s_ctx[:, :, :], ps[:, CB, :].rearrange("p (t c) -> p t c", c=CTX),
                                     ACT.Copy).then_inc(c_copied, 1)

            def exponential(u, n):
                slot = n % SLOTS
                act.wait_ge(max_done, u * NQ + n + 1 + LEAD)
                act.wait_ge(t_done, u * (5 * NQ // 2) + 5 * (n // 2 - 1) + LEAD)
                nc.scalar.activation(probs[:, slot, TOK:KEYS], s_ctx[:, n % NQ, :], ACT.Exp, bias=nmx[:, slot:slot + 1],
                                     accum_out=den[:, 1, slot:slot + 1])
                nc.scalar.activation(probs[:, slot, 0:TOK], psf[:, 1024 * (n % 2):1024 * (n % 2) + TOK], ACT.Exp,
                                     bias=nmx[:, slot:slot + 1], accum_out=den[:, 0, slot:slot + 1]).then_inc(exp_done, 1)

            def high_pt(u, n, g):
                gi = 5 * (n // 2) + 2 * (n % 2) + g
                act.wait_ge(t_done, u * (5 * NQ // 2) + gi + 1 + LEAD)
                if g == 0:
                    act.wait_ge(pv_done, u * (NQ // 2) + n // 2 - 1 + LEAD)
                dst, src = pt_group(0, n, g)
                nc.scalar.activation(dst, src, ACT.Copy).then_inc(pt_high, 1)

            def low_rows(u, j):
                act.wait_ge(pv_done, u * (NQ // 2) + j + 1 + LEAD)
                nc.scalar.activation(o_low[:, :], ps[DH0:P, OB, 0:2 * P], ACT.Copy).then_inc(o_low_done, 1)

            def phase(u, k, heads, project, own_values):
                nt = NQ * len(heads)
                for n in range(nt + LAG + 3):
                    m = n - LAG
                    if m >= 4 and m % 2 == 0:
                        low_rows(u, (m - 4) // 2)
                    if n < nt and n % NQ == 0:
                        copy_context(u, n)
                    if 0 <= m < nt:
                        high_pt(u, m, 0)
                        high_pt(u, m, 1)
                        if m % 2 == 1:
                            high_pt(u, m, 2)
                    if n < nt:
                        exponential(u, n)
                    if n == 1 and own_values:
                        high_v(k)
                    if n == nt and project:
                        high_qk(k + 1, 0, Q_PIECES, 0)
                    if n == nt + 1 and project:
                        high_qk(k + 1, 1, K_PIECES[:2], len(Q_PIECES))
                if project:
                    high_qk(k + 1, 1, K_PIECES[2:], SPLITS - 1)

            high_qk(0, 0, Q_PIECES, 0)
            high_qk(0, 1, K_PIECES, len(Q_PIECES))
            with act.Fori(0, BATCH) as b:
                phase(b * HEADS0, b * PAIRS, [(0, 0)], True, True)
                with act.Fori(1, PAIRS) as p:
                    k = b * PAIRS + p
                    phase(k * 2 - 1, k, [(1, -1), (0, 0)], True, True)
                phase(b * HEADS0 + (HEADS0 - 1), b * PAIRS + PAIRS, [(1, -1)], False, False)

        @block.vector
        def _(dve):
            for s in (qk_low, v_low, c_max, tok_max, max_done, den_sum, pt_low, o_done, x_added):
                dve.sem_inc(s, LEAD)

            def low_qk(k, which, pieces, i0):
                dst, scale = ((q_split, 1.0 / 8.0), (k_split, 1.0))[which]
                for i, (bank, at, w) in enumerate(pieces):
                    dve.wait_ge(qk_high, k * SPLITS + i0 + i + 1 + LEAD)
                    nc.vector.scalar_tensor_tensor(dst[:, 1, at:at + w], ps[:, bank, 0:w], scale, dst[:, 0, at:at + w],
                                                   ALU.mult, ALU.subtract).then_inc(qk_low, 1)

            def low_v(k):
                for i, (bank, c0, n) in enumerate(V_PIECES):
                    dve.wait_ge(v_high, k * 3 + i + 1 + LEAD)
                    nc.vector.tensor_tensor(v_split[:, :, c0:c0 + n, 1, :],
                                            ps[:, bank, 0:n * P].rearrange("p (c h d) -> p h c d", h=2, d=DH0),
                                            v_split[:, :, c0:c0 + n, 0, :], ALU.subtract).then_inc(v_low, 1)

            def context_max(u, n):
                dve.wait_ge(c_copied, u + n // NQ + 1 + LEAD)
                dve.wait_ge(max_done, u * NQ + n + LEAD)
                nc.vector.tensor_reduce(ctx_nmx[:, :], s_ctx[:, :, :], AX.X, ALU.max, negate=True).then_inc(c_max, 1)

            def row_max(u, n):
                s, slot = u * NQ + n, n % SLOTS
                dve.wait_ge(s_done, s + 1 + LEAD)
                nc.vector.tensor_reduce(tok_nmx[:, slot:slot + 1], psf[:, 1024 * (n % 2):1024 * (n % 2) + TOK], AX.X,
                                        ALU.max, negate=True).then_inc(tok_max, 1)
                if n % NQ == 0:
                    context_max(u, n)
                    dve.wait_ge(c_max, u + n // NQ + 1 + LEAD)
                dve.wait_ge(tok_max, s + 1 + LEAD)
                nc.vector.tensor_tensor(nmx[:, slot:slot + 1], tok_nmx[:, slot:slot + 1], ctx_nmx[:, n % NQ:n % NQ + 1],
                                        ALU.min).then_inc(max_done, 1)

            def reciprocal(u, n):
                s, slot = u * NQ + n, n % SLOTS
                dve.wait_ge(exp_done, s + 1 + LEAD)
                nc.vector.tensor_tensor(den[:, 0, slot:slot + 1], den[:, 0, slot:slot + 1], den[:, 1, slot:slot + 1],
                                        ALU.add).then_inc(den_sum, 1)
                dve.wait_ge(den_sum, s + 1 + LEAD)
                nc.vector.reciprocal(rden[:, slot:slot + 1], den[:, 0, slot:slot + 1]).then_inc(rden_done, 1)

            def low_pt(u, n, g):
                dve.wait_ge(pt_high, u * (5 * NQ // 2) + 5 * (n // 2) + 2 * (n % 2) + g + 1 + LEAD)
                dst, src = pt_group(1, n, g)
                nc.vector.tensor_tensor(dst, src, pt_group(0, n, g)[0], ALU.subtract).then_inc(pt_low, 1)

            def join(u, j, h, pair):
                dve.wait_ge(o_low_done, u * (NQ // 2) + j + 1 + LEAD)
                cols = slice((j % (NQ // 2)) * 2 * P, (j % (NQ // 2)) * 2 * P + 2 * P)
                nc.vector.tensor_tensor(ot[DH0 * h:DH0 * h + DH0, pair, cols], ps[0:DH0, OB, 0:2 * P], o_low[:, :],
                                        ALU.add).then_inc(o_done, 1)

            def phase(u, k, heads, pairs, project, own_values):
                nt = NQ * len(heads)
                for n in range(nt + LAG + 3):
                    m = n - LAG
                    if m >= 4 and m % 2 == 0:
                        j = (m - 4) // 2
                        join(u, j, heads[j // (NQ // 2)][0], pairs[j // (NQ // 2)])
                    if 1 <= n <= nt:
                        reciprocal(u, n - 1)
                    if n < nt:
                        row_max(u, n)
                    if n == 1 and own_values:
                        low_v(k)
                    if 0 <= m < nt:
                        low_pt(u, m, 0)
                        low_pt(u, m, 1)
                        if m % 2 == 1:
                            low_pt(u, m, 2)
                    if n == nt and project:
                        low_qk(k + 1, 0, Q_PIECES, 0)
                    if n == nt + 1 and project:
                        low_qk(k + 1, 1, K_PIECES[:2], len(Q_PIECES))
                if project:
                    low_qk(k + 1, 1, K_PIECES[2:], SPLITS - 1)

            low_qk(0, 0, Q_PIECES, 0)
            low_qk(0, 1, K_PIECES, len(Q_PIECES))
            with dve.Fori(0, BATCH) as b:
                phase(b * HEADS0, b * PAIRS, [(0, 0)], [0], True, True)
                with dve.Fori(1, PAIRS) as p:
                    k = b * PAIRS + p
                    phase(k * 2 - 1, k, [(1, -1), (0, 0)], [p - 1, p], True, True)
                phase(b * HEADS0 + (HEADS0 - 1), b * PAIRS + PAIRS, [(1, -1)], [PAIRS - 1], False, False)
                for i in range(TPB):
                    dve.wait_ge(wo_done, b * TPB + i + 1 + LEAD)
                    nc.vector.tensor_tensor(x_sb[:, b * TPB + i, :], ps[:, i % 4, 0:D], x_sb[:, b * TPB + i, :],
                                            ALU.add).then_inc(x_added, 1)
            dve.wait_ge(x_added, BATCH * TPB + LEAD)


def route(nc, a, outer, xn_t, h, ps):
    slots = nc.dram_tensor("slot_rows", [SLOT_TILES * P, D], F32, kind="Internal").ap()
    results = nc.dram_tensor("slot_results", [SLOT_TILES * P, D], F32, kind="Internal").ap()
    keep = lambda n, s, dt=F32: outer.enter_context(nc.sbuf_tensor(f"moe_{n}", s, dt, side="right"))
    slot = [keep(f"slot{k}", [P, TILES], U32) for k in range(2)]
    share = [keep(f"share{k}", [P, TILES]) for k in range(2)]
    tile_expert = keep("tile_expert", [P, SLOT_TILES], I32)
    gather_route(nc, a, xn_t, ps, slot, share, tile_expert)
    with ExitStack() as c1:
        zero = c1.enter_context(nc.sbuf_tensor("moe_zero", [P, D], F32))
        zeroed, zset, scattered = (c1.enter_context(nc.semaphore(f"moe_{n}")) for n in ("zeroed", "zset", "scattered"))
        block = c1.enter_context(nc.Block())

        @block.vector
        def _(dve):
            nc.vector.memset(zero[:], 0.0).then_inc(zset, 1)

        @block.sync
        def _(sp):
            sp.wait_ge(zset, 1)
            sp.dma_start(slots.rearrange("(t p) d -> p t d", p=P),
                         zero[:, :].unsqueeze(1).to_broadcast([P, SLOT_TILES, D])).then_inc(zeroed, 16)

        @block.gpsimd
        def _(pool):
            pool.wait_ge(zeroed, 16)
            for k in range(2):
                for t in range(TILES):
                    pool.indirect_dma_start(slots[:, :], bass.IndirectOffsetOnAxis(ap=slot[k][:, t:t + 1], axis=0),
                                            h[:, t, :], None).then_inc(scattered, 16)
            pool.wait_ge(scattered, 16 * 2 * TILES)
    return slots, results, slot, share, tile_expert


def run_experts(nc, a, x_sb, ident, ps, gamma, beta, tables, weights):
    slots, results, slot, share, tile_expert = tables
    expert_tiles(nc, a, ident, ps, gamma, beta, slots, results, tile_expert, weights)
    combine(nc, x_sb, slot, share, results)


def gather_route(nc, a, xn_t, ps, slot, share, tile_expert):
    with ExitStack() as ctx:
        sb = lambda n, s, dt=F32: ctx.enter_context(nc.sbuf_tensor(f"rt_{n}", s, dt))
        sem = lambda n: ctx.enter_context(nc.semaphore(f"rt_{n}"))
        gw = sb("gw", [P, DC, E])
        TE = [P, TILES, E]
        prob, work, ohs, one1, one2, base = (sb(n, TE) for n in ("prob", "work", "ohs", "one1", "one2", "base"))
        scan = [sb(f"scan{i}", TE) for i in range(2)]
        top1, top2, red = sb("top1", [P, TILES]), sb("top2", [P, TILES]), sb("red", [P, TILES])
        escan = [sb(f"escan{i}", [P, E]) for i in range(2)]
        padded, start = sb("padded", [P, E]), sb("start", [P, E])
        erank = sb("erank", [P, E])
        tstart = sb("tstart", [P, SLOT_TILES])
        cmp = sb("cmp", [P, SLOT_TILES, E])
        tsum = sb("tsum", [P, SLOT_TILES])
        lower, ones = sb("lower", [P, P]), sb("ones", [P, P])
        gw_loaded, const, logits_done, v, exped, counted = (sem(n) for n in ("gw", "const", "logits", "v", "exped", "counted"))
        block = ctx.enter_context(nc.Block())

        @block.sync
        def _(sp):
            sp.dma_start(gw[:], a["L0_ffn_gate_w"].rearrange("(c p) e -> p c e", p=P)).then_inc(gw_loaded, 16)

        @block.gpsimd
        def _(pool):
            nc.gpsimd.memset(ones[:], 1.0).then_inc(const, 1)
            nc.gpsimd.memset(lower[:], 1.0).then_inc(const, 1)
            nc.gpsimd.iota(erank[:], [[-1, E]], base=E, channel_multiplier=0,
                           allow_small_or_imprecise_dtypes=True).then_inc(const, 1)
            nc.gpsimd.iota(tstart[:], [[P, SLOT_TILES]], base=0, channel_multiplier=0,
                           allow_small_or_imprecise_dtypes=True).then_inc(const, 1)
            pool.wait_ge(const, 4)
            nc.gpsimd.affine_select(out=lower[:], in_=lower[:], compare_op=ALU.is_gt, fill=0.0, base=0,
                                    pattern=[[1, P]], channel_multiplier=-1).then_inc(const, 1)

        @block.tensor
        def _(pe):
            pe.wait_ge(gw_loaded, 16)
            for t in range(TILES):
                for c in range(DC):
                    mm = nc.tensor.matmul(ps[:, 0, t * E:(t + 1) * E], xn_t[:, c, t * P:(t + 1) * P], gw[:, c, :],
                                          start=(c == 0), stop=(c == DC - 1))
            mm.then_inc(logits_done, 1)
            pe.wait_ge(const, 5)
            pe.wait_ge(counted, 1)
            flat = ohs[:, :, :].rearrange("p t e -> p (t e)")
            nc.tensor.matmul(ps[:, 1, 0:TILES * E], lower[:], flat, start=True, stop=True).then_inc(counted, 1)
            nc.tensor.matmul(ps[:, 2, 0:TILES * E], ones[:], flat, start=True, stop=True).then_inc(counted, 1)

        @block.scalar
        def _(act):
            act.wait_ge(v, 2)
            nc.scalar.activation(prob[:, :, :], work[:, :, :], ACT.Exp).then_inc(exped, 1)

        @block.vector
        def _(dve):
            n = [0]

            def step(ins):
                n[0] += 1
                ins.then_inc(v, 1)
                dve.wait_ge(v, n[0])

            def bcast(x):
                return x[:, :].unsqueeze(2).to_broadcast(TE)

            V = nc.vector
            logits = ps[:, 0, 0:TILES * E].rearrange("p (t e) -> p t e", e=E)
            prefix = ps[:, 1, 0:TILES * E].rearrange("p (t e) -> p t e", e=E)
            total = ps[:, 2, 0:TILES * E].rearrange("p (t e) -> p t e", e=E)
            rank = erank[:, :].unsqueeze(1).to_broadcast(TE)
            dve.wait_ge(logits_done, 1)
            step(V.tensor_reduce(red[:], logits, AX.X, ALU.max))
            step(V.tensor_tensor(work[:], logits, bcast(red), ALU.subtract))
            dve.wait_ge(exped, 1)
            step(V.tensor_reduce(red[:], prob[:], AX.X, ALU.add))
            step(V.reciprocal(red[:], red[:]))
            step(V.tensor_tensor(prob[:], prob[:], bcast(red), ALU.mult))
            dve.wait_ge(const, 5)

            def pick(one, top):
                step(V.tensor_reduce(top[:], prob[:], AX.X, ALU.max))
                step(V.tensor_tensor(work[:], prob[:], bcast(top), ALU.is_equal))
                step(V.tensor_tensor(work[:], work[:], rank, ALU.mult))
                step(V.tensor_reduce(red[:], work[:], AX.X, ALU.max))
                step(V.tensor_tensor(one[:], bcast(red), rank, ALU.is_equal))

            pick(one1, top1)
            step(V.scalar_tensor_tensor(prob[:], one1[:], -4.0, prob[:], ALU.mult, ALU.add))
            pick(one2, top2)
            step(V.tensor_tensor(red[:], top1[:], top2[:], ALU.add))
            step(V.reciprocal(red[:], red[:]))
            step(V.tensor_tensor(share[0][:], top1[:], red[:], ALU.mult))
            step(V.tensor_tensor(share[1][:], top2[:], red[:], ALU.mult))
            V.tensor_tensor(ohs[:], one1[:], one2[:], ALU.add).then_inc(counted, 1)
            dve.wait_ge(counted, 3)
            step(V.tensor_copy(scan[0][:], total))
            src, s = 0, 1
            while s < TILES:
                step(V.tensor_copy(scan[1 - src][:, 0:s, :], scan[src][:, 0:s, :]))
                step(V.tensor_tensor(scan[1 - src][:, s:, :], scan[src][:, s:, :], scan[src][:, :TILES - s, :], ALU.add))
                src, s = 1 - src, 2 * s
            inclusive = scan[src]
            step(V.tensor_scalar(padded[:], inclusive[:, TILES - 1, :], 1.0 / P, 127.0 / P - 0.5 + 0.5 / P, ALU.mult, ALU.add))
            step(V.tensor_scalar(padded[:], padded[:], ROUND, None, ALU.add))
            step(V.tensor_scalar(padded[:], padded[:], ROUND, float(P), ALU.subtract, ALU.mult))
            step(V.tensor_copy(escan[0][:], padded[:]))
            es, s = 0, 1
            while s < E:
                step(V.tensor_copy(escan[1 - es][:, 0:s], escan[es][:, 0:s]))
                step(V.tensor_tensor(escan[1 - es][:, s:], escan[es][:, s:], escan[es][:, :E - s], ALU.add))
                es, s = 1 - es, 2 * s
            end = escan[es]
            step(V.tensor_tensor(start[:], end[:], padded[:], ALU.subtract))
            step(V.tensor_tensor(base[:], inclusive[:], total, ALU.subtract))
            step(V.tensor_tensor(base[:], base[:], prefix, ALU.add))
            step(V.tensor_tensor(base[:], base[:], start[:, :].unsqueeze(1).to_broadcast(TE), ALU.add))
            for k, one in enumerate((one1, one2)):
                step(V.tensor_tensor(work[:], one[:], base[:], ALU.mult))
                step(V.tensor_reduce(red[:], work[:], AX.X, ALU.add))
                step(V.tensor_copy(slot[k][:], red[:]))
            SE = [P, SLOT_TILES, E]
            step(V.tensor_tensor(cmp[:], end[:, :].unsqueeze(1).to_broadcast(SE), tstart[:, :].unsqueeze(2).to_broadcast(SE),
                                 ALU.is_le))
            step(V.tensor_reduce(tsum[:], cmp[:], AX.X, ALU.add))
            step(V.tensor_scalar(tile_expert[:], tsum[:], float(E - 1), None, ALU.min))


def expert_tiles(nc, a, ident, ps, gamma, beta, slots, results, tile_expert, weights):
    w1, w2, w_loaded = weights
    with ExitStack() as ctx:
        sb = lambda n, s, dt=F32: ctx.enter_context(nc.sbuf_tensor(f"ex_{n}", s, dt))
        sem = lambda n: ctx.enter_context(nc.semaphore(f"ex_{n}"))
        FC = FF // P
        rows = sb("rows", [P, 2, D])
        b1r = sb("b1r", [P, 2, FF])
        b2r = sb("b2r", [P, 2, D])
        xt = sb("xt", [P, 2, DC, P])
        hid = sb("hid", [P, 2, FF])
        hid_t = sb("hid_t", [P, 2, FC, P])
        y = sb("y", [P, 2, D])
        rows_loaded, b1_loaded, b2_loaded, stored = ([sem(f"{n}{j}") for j in range(2)]
                                                     for n in ("rows_loaded", "b1_loaded", "b2_loaded", "stored"))
        x_turned, x_evac, h_done, h_biased, h_act = (sem(n) for n in ("x_turned", "x_evac", "h_done", "h_biased", "h_act"))
        g_turned, g_evac_act, g_evac_dve, y_done, y_biased = (sem(n) for n in ("g_turned", "g_evac_act", "g_evac_dve", "y_done", "y_biased"))
        XB, HB, TB, YB = 0, 1, 5, 7
        NT = SLOT_TILES
        block = ctx.enter_context(nc.Block())

        @block.sync
        def _(sp):
            for s in rows_loaded + b1_loaded + b2_loaded + stored:
                sp.sem_inc(s, LEAD)

            def load(s, j, store):
                e = sp.value_load(tile_expert[0:1, ds(s, 1)], min_val=0, max_val=E - 1)
                sp.wait_ge(x_turned, s - 1 + LEAD)
                sp.dma_start(rows[:, j, :], slots[ds(s * P, P), :]).then_inc(rows_loaded[j], 16)
                sp.wait_ge(h_biased, s - 1 + LEAD)
                sp.dma_start(b1r[:, j, :], a["L0_ffn_b1"][ds(e, 1), :].partition_broadcast(P)).then_inc(b1_loaded[j], 16)
                sp.wait_ge(y_biased, s - 1 + LEAD)
                sp.dma_start(b2r[:, j, :], a["L0_ffn_b2"][ds(e, 1), :].partition_broadcast(P)).then_inc(b2_loaded[j], 16)
                if store:
                    sp.dma_start(results[ds((s - 2) * P, P), :], y[:, j, :]).then_inc(stored[j], 16)

            for j in range(2):
                load(j, j, False)
            with sp.Fori(1, NT // 2) as u:
                for j in range(2):
                    load(u * 2 + j, j, True)
            for j in range(2):
                sp.wait_ge(y_biased, NT - 1 + j + LEAD)
                sp.dma_start(results[(NT - 2 + j) * P:(NT - 1 + j) * P, :], y[:, j, :]).then_inc(stored[j], 16)
            for j in range(2):
                sp.wait_ge(stored[j], NT // 2 * 16 + LEAD)

        @block.tensor
        def _(pe):
            for s in (x_turned, h_done, g_turned, y_done):
                pe.sem_inc(s, LEAD)

            def turn_rows(s, u, j):
                pe.wait_ge(rows_loaded[j], (u + 1) * 16 + LEAD)
                pe.wait_ge(x_evac, s * DC + LEAD)
                for c in range(DC):
                    mm = nc.tensor.transpose(ps[:, XB, c * P:(c + 1) * P], rows[:, j, c * P:(c + 1) * P], ident[:])
                mm.then_inc(x_turned, 1)

            def first_layer(s, j):
                e = pe.value_load(tile_expert[0:1, ds(s, 1)], min_val=0, max_val=E - 1)
                pe.wait_ge(x_evac, s * DC + DC + LEAD)
                pe.wait_ge(h_biased, s - 1 + LEAD)
                for nb in range(2):
                    for c in range(DC):
                        mm = nc.tensor.matmul(ps[:, HB + 2 * j + nb, :], xt[:, j, c, :],
                                              w1[:, ds(e * (DC * FF) + (c * FF + nb * 512), 512)],
                                              start=(c == 0), stop=(c == DC - 1))
                mm.then_inc(h_done, 1)

            def turn_hidden(s, j):
                pe.wait_ge(h_act, s + 1 + LEAD)
                pe.wait_ge(g_evac_act, s + LEAD)
                pe.wait_ge(g_evac_dve, s + LEAD)
                for f in range(FC):
                    mm = nc.tensor.transpose(ps[:, TB + f // 4, (f % 4) * P:(f % 4) * P + P],
                                             hid[:, j, f * P:(f + 1) * P], ident[:])
                    if f % 4 == 3:
                        mm.then_inc(g_turned, 1)

            def second_layer(s, j):
                e = pe.value_load(tile_expert[0:1, ds(s, 1)], min_val=0, max_val=E - 1)
                pe.wait_ge(g_evac_act, s + 1 + LEAD)
                pe.wait_ge(g_evac_dve, s + 1 + LEAD)
                pe.wait_ge(y_biased, s + LEAD)
                for f in range(FC):
                    mm = nc.tensor.matmul(ps[:, YB, 0:D], hid_t[:, j, f, :], w2[:, ds(e * (FC * D) + f * D, D)],
                                          start=(f == 0), stop=(f == FC - 1))
                mm.then_inc(y_done, 1)

            def step(s, j, nxt):
                if nxt:
                    turn_rows(*nxt)
                turn_hidden(s, j)
                if nxt:
                    first_layer(nxt[0], nxt[2])
                second_layer(s, j)

            turn_rows(0, 0, 0)
            pe.wait_ge(w_loaded, 32 * E)
            first_layer(0, 0)
            with pe.Fori(0, NT // 2 - 1) as u:
                step(u * 2, 0, (u * 2 + 1, u, 1))
                step(u * 2 + 1, 1, (u * 2 + 2, u + 1, 0))
            step(NT - 2, 0, (NT - 1, NT // 2 - 1, 1))
            step(NT - 1, 1, None)

        @block.scalar
        def _(act):
            for s in (x_evac, h_act, g_evac_act):
                act.sem_inc(s, LEAD)

            def rows_out(s, j):
                act.wait_ge(x_turned, s + 1 + LEAD)
                act.wait_ge(h_done, s - 1 + LEAD)
                for c in range(DC):
                    nc.scalar.activation(xt[:, j, c, :], ps[:, XB, c * P:(c + 1) * P], ACT.Identity,
                                         bias=beta[:, c:c + 1], scale=gamma[:, c:c + 1]).then_inc(x_evac, 1)

            def gelu(s, j):
                act.wait_ge(h_biased, s + 1 + LEAD)
                nc.scalar.activation(hid[:, j, :], hid[:, j, :], ACT.Gelu).then_inc(h_act, 1)

            def hidden_out(s, j):
                act.wait_ge(g_turned, s * 2 + 1 + LEAD)
                act.wait_ge(y_done, s - 1 + LEAD)
                nc.scalar.activation(hid_t[:, j, 0:4, :], ps[:, TB, :].rearrange("p (f q) -> p f q", f=4),
                                     ACT.Copy).then_inc(g_evac_act, 1)

            def step(s, j, nxt):
                if nxt:
                    rows_out(nxt[0], nxt[1])
                hidden_out(s, j)
                if nxt:
                    gelu(nxt[0], nxt[1])

            rows_out(0, 0)
            gelu(0, 0)
            with act.Fori(0, NT // 2 - 1) as u:
                step(u * 2, 0, (u * 2 + 1, 1))
                step(u * 2 + 1, 1, (u * 2 + 2, 0))
            step(NT - 2, 0, (NT - 1, 1))
            step(NT - 1, 1, None)

        @block.vector
        def _(dve):
            for s in (h_biased, g_evac_dve, y_biased):
                dve.sem_inc(s, LEAD)

            def add_b1(s, u, j):
                dve.wait_ge(h_done, s + 1 + LEAD)
                dve.wait_ge(b1_loaded[j], (u + 1) * 16 + LEAD)
                dve.wait_ge(g_turned, s * 2 - 2 + LEAD)
                nc.vector.tensor_tensor(hid[:, j, :].rearrange("p (b n) -> p b n", b=2), ps[:, HB + 2 * j:HB + 2 * j + 2, :],
                                        b1r[:, j, :].rearrange("p (b n) -> p b n", b=2), ALU.add).then_inc(h_biased, 1)

            def hidden_out(s, j):
                dve.wait_ge(g_turned, s * 2 + 2 + LEAD)
                dve.wait_ge(y_done, s - 1 + LEAD)
                nc.vector.tensor_copy(hid_t[:, j, 4:8, :], ps[:, TB + 1, :].rearrange("p (f q) -> p f q", f=4)
                                      ).then_inc(g_evac_dve, 1)

            def add_b2(s, u, j):
                dve.wait_ge(y_done, s + 1 + LEAD)
                dve.wait_ge(b2_loaded[j], (u + 1) * 16 + LEAD)
                dve.wait_ge(stored[j], u * 16 + LEAD)
                nc.vector.tensor_tensor(y[:, j, :], ps[:, YB, 0:D], b2r[:, j, :], ALU.add).then_inc(y_biased, 1)

            def step(s, u, j, nxt):
                hidden_out(s, j)
                if nxt:
                    add_b1(*nxt)
                add_b2(s, u, j)

            add_b1(0, 0, 0)
            with dve.Fori(0, NT // 2 - 1) as u:
                step(u * 2, u, 0, (u * 2 + 1, u, 1))
                step(u * 2 + 1, u, 1, (u * 2 + 2, u + 1, 0))
            step(NT - 2, NT // 2 - 1, 0, (NT - 1, NT // 2 - 1, 1))
            step(NT - 1, NT // 2 - 1, 1, None)


def combine(nc, x_sb, slot, share, results):
    with ExitStack() as ctx:
        NBUF = 4
        got = ctx.enter_context(nc.sbuf_tensor("cb_got", [P, NBUF, D], F32))
        gathered = [ctx.enter_context(nc.semaphore(f"cb_gathered{i}")) for i in range(NBUF)]
        added = ctx.enter_context(nc.semaphore("cb_added"))
        block = ctx.enter_context(nc.Block())

        @block.gpsimd
        def _(pool):
            for n in range(2 * TILES):
                if n >= NBUF:
                    pool.wait_ge(added, n - NBUF + 1)
                pool.indirect_dma_start(got[:, n % NBUF, :], None, results[:, :],
                                        bass.IndirectOffsetOnAxis(ap=slot[n % 2][:, n // 2:n // 2 + 1], axis=0)
                                        ).then_inc(gathered[n % NBUF], 16)

        @block.vector
        def _(dve):
            for n in range(2 * TILES):
                t = n // 2
                dve.wait_ge(gathered[n % NBUF], 16 * (n // NBUF + 1))
                if n % 2:
                    dve.wait_ge(added, n)
                nc.vector.scalar_tensor_tensor(x_sb[:, t, :], got[:, n % NBUF, :], share[n % 2][:, t:t + 1],
                                               x_sb[:, t, :], ALU.mult, ALU.add).then_inc(added, 1)
            dve.wait_ge(added, 2 * TILES)


def masked_attention(nc, a, x_sb, h_t, ctx_t, ident, ps):
    HEADS, DH, HALF = 16, 16, 8
    with ExitStack() as ctx:
        sb = lambda n, s, dt=F32: ctx.enter_context(nc.sbuf_tensor(f"ma_{n}", s, dt))
        sem = lambda n: ctx.enter_context(nc.semaphore(f"ma_{n}"))
        wq, wkv, wp = sb("wq", [P, DC, D]), sb("wkv", [P, DC, 2 * D]), sb("wp", [P, DC, D])
        bproj = sb("bproj", [P, D])
        mask = sb("mask", [P, TILES, CTX // 4], I32)
        cap = sb("cap", [P, TILES, CTX])
        hmask = sb("hmask", [P, HALF])
        ctx2 = sb("ctx2", [P, DC, BATCH, 2, CTX])
        k_diag = sb("k_diag", [P, BATCH * 2 * HALF * CTX])
        kt = sb("kt", [P, 2, P])
        v_diag = sb("v_diag", [P, BATCH, HEADS // 2, P])
        vb = sb("vb", [P, HEADS // 2, P])
        qt = sb("qt", [P, 2, 512])
        score = sb("score", [P, 2, HEADS, CTX])
        top, negtop, den = sb("top", [P, 2, HEADS]), sb("negtop", [P, 2, HEADS]), sb("den", [P, 2, HEADS])
        etop = sb("etop", [P, 2, HEADS])
        pt = sb("pt", [P, HEADS // 2, 4 * P])
        ot = sb("ot", [P, 2, 4 * P])
        w_loaded, m_loaded, const, dupd, kv_done, k_out, v_out, prep = (sem(n) for n in (
            "w_loaded", "m_loaded", "const", "dupd", "kv_done", "k_out", "v_out", "prep"))
        vb_ready, q_done, q_evac, s_done, capped, shifted, exped, rec, summed, normed, t_done = (sem(n) for n in (
            "vb_ready", "q_done", "q_evac", "s_done", "capped", "shifted", "exped", "rec", "summed", "normed", "t_done"))
        t_act, t_dve, o_done, o_evac, p_done, x_added, etop_done = (sem(n) for n in (
            "t_act", "t_dve", "o_done", "o_evac", "p_done", "x_added", "etop_done"))
        FMAX = float(np.finfo(np.float32).max)
        block = ctx.enter_context(nc.Block())

        @block.sync
        def _(sp):
            sp.dma_start(wkv[:], a["L1_xattn_Wkv"].rearrange("(c p) n -> p c n", p=P)).then_inc(w_loaded, 16)
            sp.dma_start(wq[:], a["L1_xattn_Wq"].rearrange("(c p) n -> p c n", p=P)).then_inc(w_loaded, 16)
            sp.dma_start(wp[:], a["L1_xattn_Wproj"].rearrange("(c p) n -> p c n", p=P)).then_inc(w_loaded, 16)
            sp.dma_start(mask[:], a["mask_BxSxS2_bk0"].rearrange("b (t p) k -> p (b t) k", p=P)).then_inc(m_loaded, 16)
            sp.dma_start(bproj[:], a["L1_xattn_bproj"].partition_broadcast(P)).then_inc(m_loaded, 16)

        @block.gpsimd
        def _(pool):
            pool.sem_inc(normed, LEAD)
            pool.sem_inc(vb_ready, LEAD)
            nc.gpsimd.memset(hmask[:], 1.0).then_inc(const, 1)
            nc.gpsimd.memset(v_diag[:, :, :, :], 0.0).then_inc(const, 1)
            pool.wait_ge(const, 2)
            nc.gpsimd.affine_select(out=hmask[:], in_=hmask[:], compare_op=ALU.is_ge, fill=0.0, base=0,
                                    pattern=[[-DH, HALF]], channel_multiplier=1).then_inc(const, 1)
            pool.wait_ge(const, 3)
            nc.gpsimd.affine_select(out=hmask[:], in_=hmask[:], compare_op=ALU.is_ge, fill=0.0, base=DH - 1,
                                    pattern=[[DH, HALF]], channel_multiplier=-1).then_inc(const, 1)
            pool.wait_ge(v_out, BATCH * HEADS)
            with pool.Fori(0, BATCH) as b:
                pool.wait_ge(o_done, b * 2 + LEAD)
                nc.gpsimd.tensor_copy(vb[:, :, :], v_diag[:, b, :, :]).then_inc(vb_ready, 1)
                with pool.Fori(0, 2) as g2:
                    for j in range(4):
                        n = (b * 2 + g2) * 4 + j
                        pool.wait_ge(summed, n + 1 + LEAD)
                        nc.gpsimd.tensor_tensor(score[:, j % 2], score[:, j % 2],
                                                den[:, j % 2, :].unsqueeze(2).to_broadcast([P, HEADS, CTX]),
                                                ALU.mult).then_inc(normed, 1)

        @block.tensor
        def _(pe):
            for s in (q_done, s_done, t_done, o_done, p_done):
                pe.sem_inc(s, LEAD)
            pe.wait_ge(w_loaded, 48)
            for m in range(2):
                for c in range(DC):
                    mm = nc.tensor.matmul(ps[:, 0, m * P:(m + 1) * P], wkv[:, c, m * P:(m + 1) * P], ctx_t[:, c, :],
                                          start=(c == 0), stop=(c == DC - 1))
            mm.then_inc(kv_done, 1)
            pe.wait_ge(dupd, DC)
            for b in range(BATCH):
                for c in range(DC):
                    mm = nc.tensor.matmul(ps[:, 1 + b, 0:D], ctx2[:, c, b, :, :].rearrange("p r k -> p (r k)"),
                                          wkv[:, c, D:2 * D], start=(c == 0), stop=(c == DC - 1))
            mm.then_inc(kv_done, 1)
            pe.wait_ge(k_out, 5)
            pe.wait_ge(v_out, BATCH * HEADS)

            with pe.Fori(0, BATCH) as b:
                with pe.Fori(0, 2) as g2:
                    g = b * 2 + g2

                    def scores(j):
                        n = g * 4 + j
                        pe.wait_ge(capped, n - 1 + LEAD)
                        for m in range(2):
                            mm = nc.tensor.matmul(ps[:, 2 + 2 * (j % 2) + m, :], qt[:, m, j * P:(j + 1) * P],
                                                  k_diag[:, ds(b * (2 * HALF * CTX) + m * (HALF * CTX), HALF * CTX)],
                                                  start=True, stop=True)
                        mm.then_inc(s_done, 1)

                    pe.wait_ge(o_evac, g * 2 + LEAD)
                    pe.wait_ge(vb_ready, b + 1 + LEAD)
                    for m in range(2):
                        for c in range(DC):
                            mm = nc.tensor.matmul(ps[:, m, :], wq[:, c, m * P:(m + 1) * P], h_t[:, c, ds(g * 512, 512)],
                                                  start=(c == 0), stop=(c == DC - 1))
                    mm.then_inc(q_done, 1)
                    pe.wait_ge(q_evac, g + 1 + LEAD)
                    scores(0)
                    scores(1)
                    for j in range(4):
                        n = g * 4 + j
                        pe.wait_ge(normed, n + 1 + LEAD)
                        pe.wait_ge(t_act, n + LEAD)
                        pe.wait_ge(t_dve, n + LEAD)
                        pe.wait_ge(x_added, g * 4 + LEAD)
                        for k in range(HEADS // 2):
                            mm = nc.tensor.transpose(ps[:, 6 + k // 4, (k % 4) * P:(k % 4) * P + P],
                                                     score[:, j % 2, 2 * k:2 * k + 2, :].rearrange("p h k -> p (h k)"), ident[:])
                        mm.then_inc(t_done, 1)
                        if j + 2 < 4:
                            scores(j + 2)
                    pe.wait_ge(t_act, g * 4 + 4 + LEAD)
                    pe.wait_ge(t_dve, g * 4 + 4 + LEAD)
                    for k in range(HEADS // 2):
                        mm = nc.tensor.matmul(ps[:, k // 4, :], vb[:, k, :], pt[:, k, :], start=(k % 4 == 0), stop=(k % 4 == 3))
                    mm.then_inc(o_done, 1)
                    pe.wait_ge(o_evac, g * 2 + 2 + LEAD)
                    for j in range(4):
                        if j >= 2:
                            pe.wait_ge(x_added, g * 4 + j - 1 + LEAD)
                        for c in range(DC):
                            mm = nc.tensor.matmul(ps[:, 6 + j % 2, 0:D], ot[:, c, j * P:(j + 1) * P], wp[:, c, :],
                                                  start=(c == 0), stop=(c == DC - 1))
                        mm.then_inc(p_done, 1)

        @block.scalar
        def _(act):
            for s in (q_evac, exped, etop_done, t_act, o_evac):
                act.sem_inc(s, LEAD)
            for c in range(DC):
                nc.scalar.activation(ctx2[:, c], ctx_t[:, c, :].rearrange("p (b k) -> p b k", b=BATCH).unsqueeze(2)
                                     .to_broadcast([P, BATCH, 2, CTX]), ACT.Copy).then_inc(dupd, 1)
            act.wait_ge(kv_done, 1)
            nc.scalar.activation(kt[:, :, :], ps[:, 0, 0:2 * P].rearrange("p (m k) -> p m k", m=2), ACT.Copy).then_inc(k_out, 1)
            with act.Fori(0, BATCH) as b:
                with act.Fori(0, 2) as g2:
                    g = b * 2 + g2
                    act.wait_ge(q_done, g + 1 + LEAD)
                    act.wait_ge(s_done, g * 4 + LEAD)
                    nc.scalar.activation(qt[:, :, :], ps[:, 0:2, :], ACT.Copy).then_inc(q_evac, 1)
                    for j in range(4):
                        n = g * 4 + j
                        act.wait_ge(shifted, n + 1 + LEAD)
                        nc.scalar.activation(score[:, j % 2], score[:, j % 2], ACT.Exp, scale=0.25).then_inc(exped, 1)
                        nc.scalar.activation(etop[:, j % 2, :], top[:, j % 2, :], ACT.Exp, scale=-0.25).then_inc(etop_done, 1)
                        act.wait_ge(t_done, n + 1 + LEAD)
                        act.wait_ge(o_done, g + LEAD)
                        nc.scalar.activation(pt[:, 0:4, j * P:(j + 1) * P], ps[:, 6, :].rearrange("p (k q) -> p k q", k=4),
                                             ACT.Copy).then_inc(t_act, 1)
                    act.wait_ge(o_done, g + 1 + LEAD)
                    act.wait_ge(p_done, g * 4 + LEAD)
                    for c in range(2):
                        nc.scalar.activation(ot[:, c, :], ps[:, c, :], ACT.Copy).then_inc(o_evac, 1)

        @block.vector
        def _(dve):
            for s in (capped, shifted, summed, t_dve, x_added):
                dve.sem_inc(s, LEAD)
            V = nc.vector
            dve.wait_ge(m_loaded, 32)
            V.tensor_scalar(cap[:, :, :], mask[:, :, :].bitcast(U8), -2.0, 1.0, ALU.mult, ALU.add).then_inc(prep, 1)
            V.tensor_tensor(x_sb[:, :, :], x_sb[:, :, :], bproj[:, :].unsqueeze(1).to_broadcast([P, TILES, D]),
                            ALU.add).then_inc(prep, 1)
            dve.wait_ge(prep, 2)
            V.tensor_scalar(cap[:, :, :], cap[:, :, :], FMAX, None, ALU.mult).then_inc(prep, 1)
            dve.wait_ge(prep, 3)
            dve.wait_ge(k_out, 1)
            dve.wait_ge(const, 4)
            for b in range(BATCH):
                for m in range(2):
                    o = (b * 2 + m) * HALF * CTX
                    V.tensor_tensor(k_diag[:, o:o + HALF * CTX].rearrange("p (h k) -> p h k", h=HALF),
                                    kt[:, m, b * CTX:(b + 1) * CTX].unsqueeze(1).to_broadcast([P, HALF, CTX]),
                                    hmask[:, :].unsqueeze(2).to_broadcast([P, HALF, CTX]), ALU.mult).then_inc(k_out, 1)
            dve.wait_ge(kv_done, 2)
            for b in range(BATCH):
                for h in range(HEADS):
                    r = slice(CTX * (h % 2), CTX * (h % 2) + CTX)
                    col = (h % HALF) * DH
                    V.tensor_copy(v_diag[r, b, h // 2, col:col + DH], ps[r, 1 + b, h * DH:(h + 1) * DH]).then_inc(v_out, 1)

            with dve.Fori(0, BATCH) as b:
                with dve.Fori(0, 2) as g2:
                    g = b * 2 + g2

                    def shift(j):
                        n = g * 4 + j
                        sc = score[:, j % 2]
                        dve.wait_ge(s_done, n + 1 + LEAD)
                        dve.wait_ge(t_done, n - 1 + LEAD)
                        V.tensor_tensor(sc, ps[:, 2 + 2 * (j % 2):4 + 2 * (j % 2), :].rearrange("p m (h k) -> p (m h) k", k=CTX),
                                        cap[:, ds(g * 4 + j, 1), :].to_broadcast([P, HEADS, CTX]), ALU.min).then_inc(capped, 1)
                        dve.wait_ge(capped, n + 1 + LEAD)
                        V.tensor_reduce(top[:, j % 2, :], sc, AX.X, ALU.max).then_inc(rec, 1)
                        dve.wait_ge(rec, n * 4 + 1)
                        V.tensor_scalar(top[:, j % 2, :], top[:, j % 2, :], 0.0, None, ALU.max).then_inc(rec, 1)
                        dve.wait_ge(rec, n * 4 + 2)
                        V.tensor_tensor(sc, sc, top[:, j % 2, :].unsqueeze(2).to_broadcast([P, HEADS, CTX]),
                                        ALU.subtract).then_inc(shifted, 1)

                    def total(j):
                        n = g * 4 + j
                        dve.wait_ge(exped, n + 1 + LEAD)
                        V.tensor_reduce(den[:, j % 2, :], score[:, j % 2], AX.X, ALU.add).then_inc(rec, 1)
                        dve.wait_ge(etop_done, n + 1 + LEAD)
                        dve.wait_ge(rec, n * 4 + 3)
                        V.tensor_tensor(den[:, j % 2, :], den[:, j % 2, :], etop[:, j % 2, :], ALU.add).then_inc(rec, 1)
                        dve.wait_ge(rec, n * 4 + 4)
                        V.reciprocal(den[:, j % 2, :], den[:, j % 2, :]).then_inc(summed, 1)

                    for j in range(4):
                        n = g * 4 + j
                        shift(j)
                        total(j)
                        dve.wait_ge(t_done, n + 1 + LEAD)
                        dve.wait_ge(o_done, g + LEAD)
                        V.tensor_copy(pt[:, 4:8, j * P:(j + 1) * P], ps[:, 7, :].rearrange("p (k q) -> p k q", k=4)).then_inc(t_dve, 1)
                    for j in range(4):
                        dve.wait_ge(p_done, g * 4 + j + 1 + LEAD)
                        row = x_sb[:, ds(g * 4 + j, 1), :]
                        V.tensor_tensor(row, ps[:, 6 + j % 2, 0:D].unsqueeze(1), row, ALU.add).then_inc(x_added, 1)
            dve.wait_ge(x_added, TILES + LEAD)


def phase_ffn(nc, a, x_sb, h_t, vecs, ps):
    FC, SLOTS, G = FF // P, 4, TILES // 4
    INV2PI = float(np.float32(1 / (2 * np.pi)))
    TWO_PI_HI = 6.28125
    TWO_PI_LO = 2 * np.pi - TWO_PI_HI
    PI_IN = float(np.nextafter(np.float32(np.pi), np.float32(0)))
    b1, theta, wr, wi = (vecs[n] for n in ("L1_ffn_b1", "L1_ffn_quantum_phases", "L1_ffn_quantum_weights_real",
                                           "L1_ffn_quantum_weights_imag"))
    with ExitStack() as ctx:
        sb = lambda n, s, dt=F32: ctx.enter_context(nc.sbuf_tensor(f"ff_{n}", s, dt))
        sem = lambda n: ctx.enter_context(nc.semaphore(f"ff_{n}"))
        w1, w2, b2 = sb("w1", [P, DC, FF]), sb("w2", [P, FC, D]), sb("b2", [P, D])
        red, cosv, sinv, coef = (sb(n, [P, FC]) for n in ("red", "cosv", "sinv", "coef"))
        hid, arg, turns, mixed = (sb(n, [P, SLOTS, 512]) for n in ("hid", "arg", "turns", "mixed"))
        w_loaded, small, s_act = sem("w_loaded"), sem("small"), sem("s_act")
        h_done, h_out, arg_done, k_rough, k_done, r_step, r_done, sin_done, q_done, relu_done, y_done, x_added = (
            sem(n) for n in ("h_done", "h_out", "arg_done", "k_rough", "k_done", "r_step", "r_done", "sin_done",
                             "q_done", "relu_done", "y_done", "x_added"))
        block = ctx.enter_context(nc.Block())

        @block.sync
        def _(sp):
            sp.dma_start(w1[:], a["L1_ffn_W1"].rearrange("(c p) n -> p c n", p=P)).then_inc(w_loaded, 16)
            sp.dma_start(w2[:], a["L1_ffn_W2"].rearrange("(f p) n -> p f n", p=P)).then_inc(w_loaded, 16)
            sp.dma_start(b2[:], a["L1_ffn_b2"].partition_broadcast(P)).then_inc(w_loaded, 16)

        @block.tensor
        def _(pe):
            for s in (h_done, y_done):
                pe.sem_inc(s, LEAD)
            pe.wait_ge(w_loaded, 48)
            with pe.Fori(0, G) as g:
                for n in range(FC + 4):
                    if n < FC:
                        pe.wait_ge(h_out, g * FC + (n - 3) + LEAD)
                        for c in range(DC):
                            mm = nc.tensor.matmul(ps[:, n % 4, :], w1[:, c, n * P:(n + 1) * P], h_t[:, c, ds(g * 512, 512)],
                                                  start=(c == 0), stop=(c == DC - 1))
                        mm.then_inc(h_done, 1)
                    if n >= 4:
                        f = n - 4
                        pe.wait_ge(relu_done, g * FC + f + 1 + LEAD)
                        if f == 0:
                            pe.wait_ge(x_added, g * 4 + LEAD)
                        for j in range(4):
                            mm = nc.tensor.matmul(ps[:, 4 + j, 0:D], mixed[:, f % SLOTS, j * P:(j + 1) * P], w2[:, f, :],
                                                  start=(f == 0), stop=(f == FC - 1))
                        mm.then_inc(y_done, 1)

        @block.scalar
        def _(act):
            for s in (h_out, k_done, sin_done, relu_done):
                act.sem_inc(s, LEAD)
            act.wait_ge(small, 6)
            nc.scalar.activation(sinv[:], red[:], ACT.Sin).then_inc(s_act, 1)
            nc.scalar.activation(cosv[:], cosv[:], ACT.Sin).then_inc(s_act, 1)
            with act.Fori(0, G) as g:
                for n in range(FC + 3):
                    if n < FC:
                        act.wait_ge(h_done, g * FC + n + 1 + LEAD)
                        act.wait_ge(q_done, g * FC + n - 3 + LEAD)
                        nc.scalar.activation(hid[:, n % SLOTS, :], ps[:, n % 4, :], ACT.Identity,
                                             bias=b1[:, n:n + 1]).then_inc(h_out, 1)
                    if 1 <= n <= FC:
                        f = n - 1
                        act.wait_ge(k_rough, g * FC + f + 1 + LEAD)
                        nc.scalar.activation(turns[:, f % SLOTS, :], turns[:, f % SLOTS, :], ACT.Copy,
                                             bias=-ROUND).then_inc(k_done, 1)
                    if 2 <= n <= FC + 1:
                        f = n - 2
                        act.wait_ge(r_done, g * FC + f + 1 + LEAD)
                        nc.scalar.activation(arg[:, f % SLOTS, :], arg[:, f % SLOTS, :], ACT.Sin).then_inc(sin_done, 1)
                    if n >= 3:
                        f = n - 3
                        act.wait_ge(q_done, g * FC + f + 1 + LEAD)
                        nc.scalar.activation(mixed[:, f % SLOTS, :], mixed[:, f % SLOTS, :], ACT.Relu).then_inc(relu_done, 1)

        @block.vector
        def _(dve):
            for s in (arg_done, k_rough, r_step, r_done, q_done, x_added):
                dve.sem_inc(s, LEAD)
            V = nc.vector
            n_small = [0]

            def step(ins):
                n_small[0] += 1
                ins.then_inc(small, 1)
                dve.wait_ge(small, n_small[0])

            step(V.tensor_scalar(red[:], theta, INV2PI, ROUND, ALU.mult, ALU.add))
            step(V.tensor_scalar(red[:], red[:], ROUND, None, ALU.subtract))
            step(V.scalar_tensor_tensor(coef[:], red[:], -TWO_PI_HI, theta, ALU.mult, ALU.add))
            step(V.scalar_tensor_tensor(red[:], red[:], -TWO_PI_LO, coef[:], ALU.mult, ALU.add))
            step(V.tensor_scalar(red[:], red[:], -PI_IN, PI_IN, ALU.max, ALU.min))
            V.tensor_scalar(coef[:], red[:], -1.0, None, ALU.mult).then_inc(s_act, 1)
            dve.wait_ge(s_act, 1)
            V.tensor_tensor(cosv[:], coef[:], red[:], ALU.min).then_inc(s_act, 1)
            dve.wait_ge(s_act, 2)
            step(V.tensor_scalar(cosv[:], cosv[:], float(np.pi / 2), None, ALU.add))
            dve.wait_ge(s_act, 4)
            step(V.tensor_tensor(cosv[:], cosv[:], wr, ALU.mult))
            step(V.tensor_tensor(sinv[:], sinv[:], wi, ALU.mult))
            step(V.tensor_tensor(coef[:], cosv[:], sinv[:], ALU.add))
            step(V.scalar_tensor_tensor(coef[:], coef[:], 0.1, wi, ALU.mult, ALU.mult))
            dve.wait_ge(w_loaded, 48)
            step(V.tensor_tensor(x_sb[:, :, :], x_sb[:, :, :], b2[:, :].unsqueeze(1).to_broadcast([P, TILES, D]), ALU.add))
            with dve.Fori(0, G) as g:
                for n in range(FC + 3):
                    if n < FC:
                        s = n % SLOTS
                        dve.wait_ge(h_out, g * FC + n + 1 + LEAD)
                        V.tensor_scalar(arg[:, s, :], hid[:, s, :], 0.1, theta[:, n:n + 1], ALU.mult, ALU.add).then_inc(arg_done, 1)
                        dve.wait_ge(arg_done, g * FC + n + 1 + LEAD)
                        V.tensor_scalar(turns[:, s, :], arg[:, s, :], INV2PI, ROUND, ALU.mult, ALU.add).then_inc(k_rough, 1)
                    if 1 <= n <= FC:
                        f = n - 1
                        s = f % SLOTS
                        dve.wait_ge(k_done, g * FC + f + 1 + LEAD)
                        V.scalar_tensor_tensor(arg[:, s, :], turns[:, s, :], -TWO_PI_HI, arg[:, s, :], ALU.mult, ALU.add).then_inc(r_step, 1)
                        dve.wait_ge(r_step, g * (2 * FC) + 2 * f + 1 + LEAD)
                        V.scalar_tensor_tensor(arg[:, s, :], turns[:, s, :], -TWO_PI_LO, arg[:, s, :], ALU.mult, ALU.add).then_inc(r_step, 1)
                        dve.wait_ge(r_step, g * (2 * FC) + 2 * f + 2 + LEAD)
                        V.tensor_scalar(arg[:, s, :], arg[:, s, :], -PI_IN, PI_IN, ALU.max, ALU.min).then_inc(r_done, 1)
                    if n >= 3:
                        f = n - 3
                        s = f % SLOTS
                        dve.wait_ge(sin_done, g * FC + f + 1 + LEAD)
                        dve.wait_ge(y_done, g * FC + f - 3 + LEAD)
                        V.scalar_tensor_tensor(mixed[:, s, :], arg[:, s, :], coef[:, f:f + 1], hid[:, s, :], ALU.mult,
                                               ALU.add).then_inc(q_done, 1)
                for j in range(4):
                    dve.wait_ge(y_done, g * FC + FC + LEAD)
                    row = x_sb[:, ds(g * 4 + j, 1), :]
                    V.tensor_tensor(row, ps[:, 4 + j, 0:D].unsqueeze(1), row, ALU.add).then_inc(x_added, 1)
            dve.wait_ge(x_added, TILES + LEAD)


def store_out(nc, out, x_sb):
    with ExitStack() as ctx:
        stored = ctx.enter_context(nc.semaphore("stored"))
        block = ctx.enter_context(nc.Block())

        @block.sync
        def _(sp):
            sp.dma_start(out.rearrange("b (t p) d -> p (b t) d", p=P), x_sb[:]).then_inc(stored, 16)
            sp.wait_ge(stored, 16)


def build(nc, a, out):
    with ExitStack() as ctx:
        sb = lambda n, s, dt=F32: ctx.enter_context(nc.sbuf_tensor(n, s, dt))
        ps = ctx.enter_context(nc.psum_tensor("ps", [P, 8, 512], F32))
        ident = sb("ident", [P, P])
        x_sb = sb("x_sb", [P, TILES, D])
        ctx_sb = sb("ctx_sb", [P, D])
        ctx_t = sb("ctx_t", [P, DC, P])
        vecs = sb("vecs", [P, VROWS])
        aff = {n: vecs[:, r0:r1] for n, (r0, r1) in vector_columns().items()}
        with ExitStack() as c0:
            ctx_ln_t = c0.enter_context(nc.sbuf_tensor("ctx_ln_t", [P, DC, P], F32))
            ln_t = c0.enter_context(nc.sbuf_tensor("ln_t", [P, DC, TILES * P], F32))
            load_and_prepare(nc, a, x_sb, ctx_sb, ctx_t, ctx_ln_t, ident, ps, vecs)
            with nc.sbuf_tensor("h0", [P, TILES, D], F32) as h:
                layer_norm_transposed(nc, "ln0", x_sb, h, ps, ident, (aff["L0_xattn_ln2_w"], aff["L0_xattn_ln2_b"]),
                                      ln_t, nested=True, add_residual=False)
            perceiver_attention(nc, a, x_sb, ln_t, ctx_ln_t, ident, ps)
        with ExitStack() as c1:
            w1 = c1.enter_context(nc.sbuf_tensor("ex_w1", [P, E * DC * FF], F32))
            w2 = c1.enter_context(nc.sbuf_tensor("ex_w2", [P, E * FF // P * D], F32))
            w_loaded = c1.enter_context(nc.semaphore("ex_w_loaded"))

            def load_experts(sp):
                w1_src = a["L0_ffn_w1"].rearrange("e (c p) h -> p e c h", p=P)
                w2_src = a["L0_ffn_w2"].rearrange("e (f p) d -> p e f d", p=P)
                w1_dst = w1[:, :].rearrange("p (e c h) -> p e c h", e=E, c=DC)
                w2_dst = w2[:, :].rearrange("p (e f d) -> p e f d", e=E, f=FF // P)
                for e in range(E):
                    sp.dma_start(w1_dst[:, e], w1_src[:, e]).then_inc(w_loaded, 16)
                    sp.dma_start(w2_dst[:, e], w2_src[:, e]).then_inc(w_loaded, 16)

            with nc.sbuf_tensor("h1", [P, TILES, D], F32) as h, nc.sbuf_tensor("xn_t", [P, DC, TILES * P], F32) as xn_t:
                layer_norm_transposed(nc, "ln1", x_sb, h, ps, ident, (aff["L0_ffn_gamma"], aff["L0_ffn_beta"]), xn_t,
                                      nested=True, add_residual=True, keep_rows=True, prefetch=load_experts)
                tables = route(nc, a, c1, xn_t, h, ps)
            run_experts(nc, a, x_sb, ident, ps, aff["L0_ffn_gamma"], aff["L0_ffn_beta"], tables, (w1, w2, w_loaded))
        with nc.sbuf_tensor("h2_t", [P, DC, TILES * P], F32) as h_t:
            layer_norm_transposed(nc, "ln2", x_sb, None, ps, ident, None, h_t, nested=False, add_residual=False)
            masked_attention(nc, a, x_sb, h_t, ctx_t, ident, ps)
        with nc.sbuf_tensor("h3_t", [P, DC, TILES * P], F32) as h_t:
            layer_norm_transposed(nc, "ln3", x_sb, None, ps, ident, None, h_t, nested=False, add_residual=False)
            phase_ffn(nc, a, x_sb, h_t, aff, ps)
        store_out(nc, out, x_sb)


NAMES = ['x', 'ctx_1024', 'mask_BxSxS2_bk0', 'L0_xattn_Wq', 'L0_xattn_Wkv', 'L0_xattn_Wo', 'L0_xattn_ln1_w',
         'L0_xattn_ln1_b', 'L0_xattn_ln2_w', 'L0_xattn_ln2_b', 'L0_ffn_gate_w', 'L0_ffn_w1', 'L0_ffn_b1', 'L0_ffn_w2',
         'L0_ffn_b2', 'L0_ffn_gamma', 'L0_ffn_beta', 'L1_xattn_Wq', 'L1_xattn_Wkv', 'L1_xattn_Wproj', 'L1_xattn_bproj',
         'L1_ffn_W1', 'L1_ffn_b1', 'L1_ffn_quantum_phases', 'L1_ffn_quantum_weights_real',
         'L1_ffn_quantum_weights_imag', 'L1_ffn_W2', 'L1_ffn_b2']


def kernel(**inputs):
    import concourse.bacc as bacc
    from concourse.bass_utils import run_bass_kernel_spmd

    nc = bacc.Bacc("TRN2", target_bir_lowering=False, num_devices=1)
    arrays, handles = {}, {}
    for name in NAMES:
        v = np.ascontiguousarray(inputs[name])
        if v.dtype == np.bool_:
            v = v.view(np.int32)
        arrays[f"in_{name}"] = v
        handles[name] = nc.dram_tensor(f"in_{name}", v.shape, mybir.dt.from_np(v.dtype), kind="ExternalInput").ap()
    out = nc.dram_tensor("out_0", (BATCH, TOK, D), F32, kind="ExternalOutput").ap()
    build(nc, handles, out)
    r = run_bass_kernel_spmd(nc, [arrays], core_ids=[0])
    return r.results[0]["out_0"]
```

```python
from contextlib import ExitStack

import numpy as np

import concourse.bass as bass
from concourse import mybir

P = 128
BATCH, TOK, D = 2, 1024, 256
CTX = 64
TILES = BATCH * TOK // P
TPB = TOK // P
DC = D // P
EPS = 1e-5

HEADS0, DH0 = 16, 64
INNER = HEADS0 * DH0
PAIRS = HEADS0 // 2
KEYS = TOK + CTX
KCH = TPB + 1
FF = 1024
E = 8
SLOT_TILES = 2 * (TILES + E // 2)
ROUND = 12582912.0
LEAD = 8

ALU = mybir.AluOpType
ACT = mybir.ActivationFunctionType
AX = mybir.AxisListType
F32 = mybir.dt.float32
F32R = mybir.dt.float32r
I32 = mybir.dt.int32
U32 = mybir.dt.uint32
U8 = mybir.dt.uint8
ds = bass.ds


def layer_norm_transposed(nc, tag, x, h, ps, ident, affine, out_t, nested, add_residual, keep_rows=False,
                          prefetch=None):
    with ExitStack() as ctx:
        sb = lambda n, s, dt=F32: ctx.enter_context(nc.sbuf_tensor(f"{tag}_{n}", s, dt))
        sem = lambda n: ctx.enter_context(nc.semaphore(f"{tag}_{n}"))
        six = sb("six", [P, TILES, 6])
        mean, diff = sb("mean", [P, TILES]), sb("diff", [P, TILES])
        ve = sb("ve", [P, TILES])
        neghalf = sb("neghalf", [P, TILES])
        rstd = sb("rstd", [P, TILES])
        stage = sb("stage", [P, 4, D])
        stats_done, agg, rstd_ready = sem("stats_done"), sem("agg"), sem("rstd_ready")
        const_ready, staged, transposed, evacuated = sem("const_ready"), sem("staged"), sem("transposed"), sem("evacuated")
        resid = sem("resid")
        rounds = 2 if nested else 1
        block = ctx.enter_context(nc.Block())

        if prefetch:
            @block.sync
            def _(sp):
                prefetch(sp)

        @block.vector
        def _(dve):
            def statistics(src, r):
                with dve.Fori(0, TILES // 4) as g:
                    for j in range(4):
                        t = g * 4 + j
                        nc.vector.bn_stats(six[:, t, :], src[:, t, :]).then_inc(stats_done, 1)
                dve.wait_ge(stats_done, (2 * r + 1) * TILES)
                mean_e, mean_o, m2_e, m2_o = six[:, :, 1], six[:, :, 4], six[:, :, 2], six[:, :, 5]
                nc.vector.tensor_tensor(mean[:], mean_e, mean_o, ALU.add).then_inc(agg, 1)
                nc.vector.tensor_tensor(diff[:], mean_e, mean_o, ALU.subtract).then_inc(agg, 1)
                nc.vector.tensor_tensor(ve[:], m2_e, m2_o, ALU.add).then_inc(agg, 1)
                dve.wait_ge(agg, 7 * r + 3)
                nc.vector.tensor_scalar(mean[:], mean[:], 0.5, None, ALU.mult).then_inc(agg, 1)
                nc.vector.scalar_tensor_tensor(diff[:], diff[:], 0.25, diff[:], ALU.mult, ALU.mult).then_inc(agg, 1)
                nc.vector.tensor_scalar(ve[:], ve[:], 1.0 / D, EPS, ALU.mult, ALU.add).then_inc(agg, 1)
                dve.wait_ge(agg, 7 * r + 6)
                nc.vector.tensor_tensor(ve[:], ve[:], diff[:], ALU.add).then_inc(agg, 1)
                dve.wait_ge(agg, 7 * r + 7)
                dve.wait_ge(rstd_ready, r + 1)

            statistics(x, 0)
            if nested:
                with dve.Fori(0, TILES // 4) as g:
                    for j in range(4):
                        t = g * 4 + j
                        nc.vector.tensor_scalar(h[:, t, :], x[:, t, :], mean[:, ds(t, 1)], rstd[:, ds(t, 1)],
                                                ALU.subtract, ALU.mult).then_inc(stats_done, 1)
                dve.wait_ge(stats_done, 2 * TILES)
                if add_residual:
                    nc.vector.tensor_tensor(x[:, :, :], x[:, :, :], h[:, :, :], ALU.add).then_inc(resid, 1)
                    dve.wait_ge(resid, 1)
                statistics(h, 1)
            src = h if nested else x
            with dve.Fori(0, TILES // 4) as g:
                dve.wait_ge(transposed, g * DC + LEAD)
                for j in range(4):
                    nc.vector.tensor_scalar(stage[:, j, :], src[:, g * 4 + j, :], mean[:, ds(g * 4 + j, 1)],
                                            rstd[:, ds(g * 4 + j, 1)], ALU.subtract, ALU.mult).then_inc(staged, 1)
                if keep_rows:
                    dve.wait_ge(staged, g * 4 + 4)
                    for j in range(4):
                        row = src[:, g * 4 + j, :]
                        nc.vector.tensor_scalar(row, row, mean[:, ds(g * 4 + j, 1)], rstd[:, ds(g * 4 + j, 1)],
                                                ALU.subtract, ALU.mult).then_inc(resid, 1)
            if keep_rows:
                dve.wait_ge(resid, TILES + (1 if add_residual else 0))

        @block.gpsimd
        def _(pool):
            nc.gpsimd.memset(neghalf[:], -0.5).then_inc(const_ready, 1)
            pool.wait_ge(const_ready, 1)
            for r in range(rounds):
                pool.wait_ge(agg, 7 * (r + 1))
                nc.gpsimd.tensor_tensor(rstd[:], ve[:], neghalf[:], ALU.pow).then_inc(rstd_ready, 1)

        @block.tensor
        def _(pe):
            pe.sem_inc(transposed, LEAD)
            with pe.Fori(0, TILES // 4) as g:
                pe.wait_ge(staged, g * 4 + 4)
                pe.wait_ge(evacuated, g * DC + LEAD)
                for c in range(DC):
                    for j in range(4):
                        mm = nc.tensor.transpose(ps[:, c, j * P:(j + 1) * P], stage[:, j, c * P:(c + 1) * P], ident[:])
                    mm.then_inc(transposed, 1)

        @block.scalar
        def _(act):
            act.sem_inc(evacuated, LEAD)
            with act.Fori(0, TILES // 4) as g:
                for c in range(DC):
                    act.wait_ge(transposed, g * DC + c + 1 + LEAD)
                    dst = out_t[:, c, ds(g * 4 * P, 4 * P)]
                    if affine is None:
                        nc.scalar.activation(dst, ps[:, c, :], ACT.Copy).then_inc(evacuated, 1)
                    else:
                        w, b = affine
                        nc.scalar.activation(dst, ps[:, c, :], ACT.Identity, bias=b[:, c:c + 1],
                                             scale=w[:, c:c + 1]).then_inc(evacuated, 1)
            act.wait_ge(evacuated, TILES // 4 * DC + LEAD)


VECTORS = [("L0_xattn_ln1_w", D), ("L0_xattn_ln1_b", D), ("L0_xattn_ln2_w", D), ("L0_xattn_ln2_b", D),
           ("L0_ffn_gamma", D), ("L0_ffn_beta", D), ("L1_ffn_b1", FF), ("L1_ffn_quantum_phases", FF),
           ("L1_ffn_quantum_weights_real", FF), ("L1_ffn_quantum_weights_imag", FF)]
VROWS = sum(n // P for _, n in VECTORS)


def vector_columns():
    at, out = 0, {}
    for name, n in VECTORS:
        out[name] = (at, at + n // P)
        at += n // P
    return out


def load_and_prepare(nc, a, x_sb, ctx_sb, ctx_t, ctx_ln_t, ident, ps, vecs, zero):
    with ExitStack() as ctx:
        sb = lambda n, s, dt=F32: ctx.enter_context(nc.sbuf_tensor(f"prep_{n}", s, dt))
        sem = lambda n: ctx.enter_context(nc.semaphore(f"prep_{n}"))
        six, mv, ve, rstd, neghalf = sb("six", [P, 6]), sb("mv", [P, 2]), sb("ve", [P, 1]), sb("rstd", [P, 1]), sb("nh", [P, 1])
        cn = sb("cn", [P, D])
        vrows = sb("vrows", [VROWS, P])
        x_loaded, ctx_loaded, vec_loaded = sem("x_loaded"), sem("ctx_loaded"), sem("vec_loaded")
        id_zero, id_ready, step, pool_step = sem("id_zero"), sem("id_ready"), sem("step"), sem("pool_step")
        turned, evac = sem("turned"), sem("evac")
        block = ctx.enter_context(nc.Block())

        @block.sync
        def _(sp):
            sp.dma_start(ctx_sb[:], a["ctx_1024"].rearrange("b s d -> (b s) d")).then_inc(ctx_loaded, 16)
            sp.dma_start(x_sb[:], a["x"].rearrange("b (t p) d -> p (b t) d", p=P)).then_inc(x_loaded, 16)
            for name, (r0, r1) in vector_columns().items():
                sp.dma_start(vrows[r0:r1, :], a[name].rearrange("(c p) -> c p", p=P)).then_inc(vec_loaded, 16)
            sp.wait_ge(x_loaded, 16)

        @block.gpsimd
        def _(pool):
            nc.gpsimd.memset(ident[:], 0.0).then_inc(id_zero, 1)
            nc.gpsimd.memset(neghalf[:], -0.5).then_inc(id_zero, 1)
            nc.gpsimd.memset(zero[:], 0.0).then_inc(id_zero, 1)
            pool.wait_ge(id_zero, 3)
            nc.gpsimd.affine_select(out=ident[:], in_=ident[:], compare_op=ALU.not_equal, fill=1.0, base=0,
                                    pattern=[[-1, P]], channel_multiplier=1).then_inc(id_ready, 1)
            pool.wait_ge(step, 3)
            nc.gpsimd.tensor_tensor(rstd[:], ve[:], neghalf[:], ALU.pow).then_inc(pool_step, 1)

        @block.vector
        def _(dve):
            dve.wait_ge(ctx_loaded, 16)
            nc.vector.bn_stats(six[:], ctx_sb[:]).then_inc(step, 1)
            dve.wait_ge(step, 1)
            nc.vector.bn_aggr(mv[:], six[:]).then_inc(step, 1)
            dve.wait_ge(step, 2)
            nc.vector.tensor_scalar(ve[:], mv[:, 1:2], EPS, None, ALU.add).then_inc(step, 1)
            dve.wait_ge(pool_step, 1)
            nc.vector.tensor_scalar(cn[:], ctx_sb[:], mv[:, 0:1], rstd[:, 0:1], ALU.subtract, ALU.mult).then_inc(step, 1)

        @block.tensor
        def _(pe):
            pe.wait_ge(id_ready, 1)
            pe.wait_ge(ctx_loaded, 16)
            for c in range(DC):
                nc.tensor.transpose(ps[:, 0, c * P:(c + 1) * P], ctx_sb[:, c * P:(c + 1) * P], ident[:]).then_inc(turned, 1)
            pe.wait_ge(vec_loaded, 16 * len(VECTORS))
            nc.tensor.transpose(ps[:, 2, 0:VROWS], vrows[:, :], ident[0:VROWS, 0:VROWS]).then_inc(turned, 1)
            pe.wait_ge(step, 4)
            for c in range(DC):
                nc.tensor.transpose(ps[:, 1, c * P:(c + 1) * P], cn[:, c * P:(c + 1) * P], ident[:]).then_inc(turned, 1)

        @block.scalar
        def _(act):
            act.wait_ge(turned, DC)
            for c in range(DC):
                nc.scalar.activation(ctx_t[:, c, :], ps[:, 0, c * P:(c + 1) * P], ACT.Copy).then_inc(evac, 1)
            act.wait_ge(turned, DC + 1)
            nc.scalar.activation(vecs[:, :], ps[:, 2, 0:VROWS], ACT.Copy).then_inc(evac, 1)
            act.wait_ge(evac, DC + 1)
            act.wait_ge(turned, 2 * DC + 1)
            w, b = (vecs[:, slice(*vector_columns()[n])] for n in ("L0_xattn_ln1_w", "L0_xattn_ln1_b"))
            for c in range(DC):
                nc.scalar.activation(ctx_ln_t[:, c, :], ps[:, 1, c * P:(c + 1) * P], ACT.Identity,
                                     bias=b[:, c:c + 1], scale=w[:, c:c + 1]).then_inc(evac, 1)
            act.wait_ge(evac, 2 * DC + 1)


def perceiver_attention(nc, a, x_sb, ln_t, ctx_ln_t, ident, ps):
    NQ, SLOTS = TPB, 4
    LAG = 3
    KPAD = TOK + P
    Q_PIECES = [(0, 0, 512), (1, 512, 512)]
    K_PIECES = [(2, 0, 512), (3, 512, 512), (0, TOK, CTX)]
    V_PIECES = [(4, 0, 4), (5, 4, 4), (6, 8, 1)]
    SPLITS = len(Q_PIECES) + len(K_PIECES)
    TB, CB, OB = 4, 6, 7
    psf = ps[:, :, :].rearrange("p b n -> p (b n)")
    with ExitStack() as ctx:
        sb = lambda n, s, dt=F32: ctx.enter_context(nc.sbuf_tensor(f"at_{n}", s, dt))
        sem = lambda n: ctx.enter_context(nc.semaphore(f"at_{n}"))
        w_pair = sb("w_pair", [P, 3, DC, P])
        wo = sb("wo", [P, PAIRS, D])
        lnb = sb("lnb", [P, DC, KPAD])
        q_split = sb("q_split", [P, 2, TOK], F32R)
        k_split = sb("k_split", [P, 2, KEYS], F32R)
        v_split = sb("v_split", [P, 2, KCH, 2, DH0], F32R)
        q_st = sb("q_st", [P, 2, TOK], F32R)
        k_st = sb("k_st", [P, 2, 2, KEYS], F32R)
        v_st = sb("v_st", [P, 2, KCH, 2, DH0], F32R)
        probs = sb("probs", [P, SLOTS, KPAD])
        pt = sb("pt", [P, 2, 2, KCH, 2 * P], F32R)
        s_ctx = sb("s_ctx", [P, NQ, CTX])
        ctx_nmx = sb("ctx_nmx", [P, NQ])
        tok_nmx, nmx = sb("tok_nmx", [P, SLOTS]), sb("nmx", [P, SLOTS])
        den, rden = sb("den", [P, 2, SLOTS]), sb("rden", [P, SLOTS])
        o_low = sb("o_low", [DH0, 2 * P])
        ot = sb("ot", [P, PAIRS, TOK])
        pads_zero, w_loaded, wo_loaded, lnb_loaded = sem("pads_zero"), sem("w_loaded"), sem("wo_loaded"), sem("lnb_loaded")
        qk_proj, v_proj, qk_high, qk_low, v_high, v_low = (
            sem(n) for n in ("qk_proj", "v_proj", "qk_high", "qk_low", "v_high", "v_low"))
        a_stacked, b_stacked, va_stacked, vb_stacked = (sem(n) for n in ("a_stacked", "b_stacked", "va_stacked", "vb_stacked"))
        s_done, max_done, exp_done, rden_done, normed = (sem(n) for n in ("s_done", "max_done", "exp_done", "rden_done", "normed"))
        t_done, pt_high, pt_low, pv_done, o_low_done, o_done = (
            sem(n) for n in ("t_done", "pt_high", "pt_low", "pv_done", "o_low_done", "o_done"))
        wo_done, x_added = sem("wo_done"), sem("x_added")
        c_done, c_copied, c_max, tok_max, den_sum = (sem(n) for n in ("c_done", "c_copied", "c_max", "tok_max", "den_sum"))
        block = ctx.enter_context(nc.Block())

        def pt_group(part, n, g):
            bank = TB + g
            buf = (n // 2) % 2
            if g < 2:
                cols = slice((n % 2) * P, (n % 2) * P + P)
                return pt[:, part, buf, 4 * g:4 * g + 4, cols], ps[:, bank, :].rearrange("p (c q) -> p c q", c=4)
            return pt[:, part, buf, KCH - 1, :], ps[:, bank, 0:2 * P]

        @block.sync
        def _(sp):
            for s in (a_stacked, b_stacked, va_stacked, vb_stacked):
                sp.sem_inc(s, LEAD)

            def load_weights(p):
                for i, (name, at) in enumerate((("L0_xattn_Wq", 0), ("L0_xattn_Wkv", 0), ("L0_xattn_Wkv", INNER))):
                    sp.dma_start(w_pair[:, i], a[name].rearrange("(c p) n -> p c n", p=P)[:, :, ds(p * P + at, P)]
                                 ).then_inc(w_loaded, 16)

            def stack(h, done):
                rows = slice(DH0 * h, DH0 * h + DH0)
                for half in range(2):
                    to = slice(DH0 * half, DH0 * half + DH0)
                    sp.dma_start(q_st[to, h, :].bitcast(F32), q_split[rows, half, :].bitcast(F32)).then_inc(done, 16)
                    sp.dma_start(k_st[to, h, :, :].bitcast(F32), k_split[rows, :, :].bitcast(F32)).then_inc(done, 16)

            with sp.Fori(0, BATCH) as b:
                sp.wait_ge(v_proj, b * (PAIRS * 3) + LEAD)
                sp.dma_start(lnb[:, :, 0:TOK], ln_t[:, :, ds(b * TOK, TOK)]).then_inc(lnb_loaded, 16)
                for i in range(2):
                    at = TOK + i * CTX
                    sp.dma_start(lnb[:, :, at:at + CTX], ctx_ln_t[:, :, ds(b * CTX, CTX)]).then_inc(lnb_loaded, 16)
                with sp.Fori(0, PAIRS) as p:
                    k = b * PAIRS + p
                    sp.wait_ge(v_proj, k * 3 + LEAD)
                    sp.wait_ge(lnb_loaded, b * 48 + 48)
                    load_weights(p)
                    sp.wait_ge(qk_low, (k + 1) * SPLITS + LEAD)
                    stack(0, a_stacked)
                    sp.wait_ge(v_low, (k + 1) * 3 + LEAD)
                    sp.wait_ge(pv_done, k * 8 - 4 + LEAD)
                    sp.dma_start(v_st[:, 0].bitcast(F32), v_split[:, 0].bitcast(F32)).then_inc(va_stacked, 16)
                    sp.wait_ge(s_done, k * 16 + LEAD)
                    stack(1, b_stacked)
                    sp.wait_ge(pv_done, k * 8 + LEAD)
                    sp.dma_start(v_st[:, 1].bitcast(F32), v_split[:, 1].bitcast(F32)).then_inc(vb_stacked, 16)
            sp.wait_ge(v_proj, BATCH * PAIRS * 3 + LEAD)
            load_weights(0)

        @block.gpsimd
        def _(pool):
            nc.gpsimd.memset(probs[:, :, KEYS:], 0.0).then_inc(pads_zero, 1)
            pool.dma_start(wo[:], a["L0_xattn_Wo"].rearrange("(c p) n -> p c n", p=P)).then_inc(wo_loaded, 16)
            with pool.Fori(0, BATCH * HEADS0 * NQ // SLOTS) as g:
                for i in range(SLOTS):
                    pool.wait_ge(rden_done, g * SLOTS + i + 1)
                    cols = probs[:, i, 0:KEYS]
                    nc.gpsimd.tensor_tensor(cols, cols, rden[:, i:i + 1].to_broadcast([P, KEYS]), ALU.mult).then_inc(normed, 1)

        @block.tensor
        def _(pe):
            for s in (qk_proj, v_proj, s_done, c_done, t_done, pv_done, wo_done):
                pe.sem_inc(s, LEAD)

            def scores(u, n, h):
                pe.wait_ge(exp_done, u * NQ + n - 1 + LEAD)
                for part in range(2):
                    for i in range(2):
                        mm = nc.tensor.matmul(ps[:, 2 * (n % 2) + i, :], q_st[:, h, (n % NQ) * P:(n % NQ) * P + P],
                                              k_st[:, h, part, i * 512:i * 512 + 512], start=(part == 0), stop=(part == 1))
                mm.then_inc(s_done, 1)

            def context_scores(u, n, h):
                pe.wait_ge(pt_low, u * (5 * NQ // 2) + 5 * (max(n - LAG, 0) // 2) + LEAD)
                for t in range(NQ):
                    for part in range(2):
                        mm = nc.tensor.matmul(ps[:, CB, t * CTX:(t + 1) * CTX], q_st[:, h, t * P:(t + 1) * P],
                                              k_st[:, h, part, TOK:KEYS], start=(part == 0), stop=(part == 1))
                mm.then_inc(c_done, 1)

            def turn(u, n, g, len_heads):
                gi = 5 * (n // 2) + 2 * (n % 2) + g
                if g == 0:
                    pe.wait_ge(normed, u * NQ + n + 1)
                last = 5 * (n // 2) - 1 if g == 2 else gi - (2 if n % 2 else 3)
                pe.wait_ge(pt_low, u * (5 * NQ // 2) + last + 1 + LEAD)
                if g == 2:
                    pe.wait_ge(c_copied, u + min((n + LAG) // NQ, len_heads - 1) + 1 + LEAD)
                pieces = [(n, 4 * g + i) for i in range(4)] if g < 2 else [(n - 1, KCH - 1), (n, KCH - 1)]
                for i, (m, c) in enumerate(pieces):
                    mm = nc.tensor.transpose(ps[:, TB + g, i * P:(i + 1) * P], probs[:, m % SLOTS, c * P:(c + 1) * P],
                                             ident[:])
                mm.then_inc(t_done, 1)

            def values(u, j, h, c0, c1):
                if c0 == 0:
                    pe.wait_ge(pt_low, u * (5 * NQ // 2) + j * 5 + 5 + LEAD)
                    pe.wait_ge(o_done, u * (NQ // 2) + j + LEAD)
                for c in range(c0, c1):
                    for part in range(2):
                        mm = nc.tensor.matmul(ps[:, OB, 0:2 * P], v_st[:, h, c].rearrange("p l d -> p (l d)"),
                                              pt[:, part, j % 2, c, :], start=(c == 0 and part == 0),
                                              stop=(c == KCH - 1 and part == 1))
                if c1 == KCH:
                    mm.then_inc(pv_done, 1)

            def project_qk(which, pieces):
                for bank, at, w in pieces:
                    for c in range(DC):
                        mm = nc.tensor.matmul(ps[:, bank, 0:w], w_pair[:, which, c, :], lnb[:, c, at:at + w],
                                              start=(c == 0), stop=(c == DC - 1))
                    mm.then_inc(qk_proj, 1)

            def project_v():
                for bank, c0, n in V_PIECES:
                    for c in range(n):
                        for f in range(DC):
                            mm = nc.tensor.matmul(ps[:, bank, c * P:(c + 1) * P], lnb[:, f, (c0 + c) * P:(c0 + c + 1) * P],
                                                  w_pair[:, 2, f, :], start=(f == 0), stop=(f == DC - 1))
                    mm.then_inc(v_proj, 1)

            def phase(u, k, heads, project, own_values):
                nt = NQ * len(heads)
                pe.wait_ge(qk_low, (k + 1) * SPLITS + LEAD)
                for n in range(nt + LAG):
                    m = n - LAG
                    if n < nt:
                        h, dk = heads[n // NQ]
                        if n % NQ == 0:
                            pe.wait_ge(b_stacked if h else a_stacked, (k + dk + 1) * 64 + LEAD)
                        scores(u, n, h)
                        if n % NQ == 0:
                            context_scores(u, n, h)
                    if n == 1 and own_values:
                        pe.wait_ge(pt_low, u * (5 * NQ // 2) + LEAD)
                        pe.wait_ge(c_copied, u + 1 + LEAD)
                        project_v()
                    cuts = False
                    if m >= 2:
                        j, cuts = (m - 2) // 2, True
                        h, dk = heads[j // (NQ // 2)]
                        if m % 2 == 0 and j % (NQ // 2) == 0:
                            pe.wait_ge(vb_stacked if h else va_stacked, (k + dk + 1) * 16 + LEAD)
                    if m >= 0:
                        if m == 0 and own_values:
                            pe.wait_ge(v_low, (k + 1) * 3 + LEAD)
                        if cuts and m % 2 == 1:
                            values(u, j, h, 5, KCH)
                        turn(u, m, 0, len(heads))
                        turn(u, m, 1, len(heads))
                        if m % 2 == 1:
                            turn(u, m, 2, len(heads))
                        if cuts and m % 2 == 0:
                            values(u, j, h, 0, 5)
                    if n == nt and project:
                        pe.wait_ge(w_loaded, (k + 2) * 48)
                        pe.wait_ge(exp_done, u * NQ + nt - 1 + LEAD)
                        project_qk(0, Q_PIECES)
                    if n == nt + LAG - 1 and project:
                        pe.wait_ge(exp_done, u * NQ + nt + LEAD)
                        project_qk(1, K_PIECES[:2])
                        pe.wait_ge(qk_low, (k + 1) * SPLITS + 1 + LEAD)
                        project_qk(1, K_PIECES[2:])
                h, dk = heads[-1]
                values(u, nt // 2 - 1, h, 0, KCH)

            pe.wait_ge(pads_zero, 1)
            pe.wait_ge(w_loaded, 48)
            project_qk(0, Q_PIECES)
            project_qk(1, K_PIECES[:2])
            pe.wait_ge(qk_low, 1 + LEAD)
            project_qk(1, K_PIECES[2:])
            with pe.Fori(0, BATCH) as b:
                pe.wait_ge(x_added, b * TPB + LEAD)
                phase(b * HEADS0, b * PAIRS, [(0, 0)], True, True)
                with pe.Fori(1, PAIRS) as p:
                    k = b * PAIRS + p
                    phase(k * 2 - 1, k, [(1, -1), (0, 0)], True, True)
                phase(b * HEADS0 + (HEADS0 - 1), b * PAIRS + PAIRS, [(1, -1)], False, False)
                pe.wait_ge(wo_loaded, 16)
                pe.wait_ge(o_done, (b + 1) * (HEADS0 * NQ // 2) + LEAD)
                for i in range(TPB):
                    if i >= 4:
                        pe.wait_ge(x_added, b * TPB + i - 3 + LEAD)
                    for pr in range(PAIRS):
                        mm = nc.tensor.matmul(ps[:, i % 4, 0:D], ot[:, pr, i * P:(i + 1) * P], wo[:, pr, :],
                                              start=(pr == 0), stop=(pr == PAIRS - 1))
                    mm.then_inc(wo_done, 1)

        @block.scalar
        def _(act):
            for s in (qk_high, v_high, c_copied, exp_done, pt_high, o_low_done):
                act.sem_inc(s, LEAD)

            def high_qk(k, which, pieces, i0):
                dst, scale = ((q_split, 1.0 / 8.0), (k_split, 1.0))[which]
                for i, (bank, at, w) in enumerate(pieces):
                    act.wait_ge(qk_proj, k * SPLITS + i0 + i + 1 + LEAD)
                    if i0 + i == 0:
                        act.wait_ge(a_stacked, k * 64 + LEAD)
                        act.wait_ge(b_stacked, k * 64 + LEAD)
                    nc.scalar.activation(dst[:, 0, at:at + w], ps[:, bank, 0:w], ACT.Copy, scale=scale).then_inc(qk_high, 1)

            def high_v(k):
                for i, (bank, c0, n) in enumerate(V_PIECES):
                    act.wait_ge(v_proj, k * 3 + i + 1 + LEAD)
                    if i == 0:
                        act.wait_ge(va_stacked, k * 16 + LEAD)
                        act.wait_ge(vb_stacked, k * 16 + LEAD)
                    nc.scalar.activation(v_split[:, :, c0:c0 + n, 0, :],
                                         ps[:, bank, 0:n * P].rearrange("p (c h d) -> p h c d", h=2, d=DH0),
                                         ACT.Copy).then_inc(v_high, 1)

            def copy_context(u, n):
                act.wait_ge(c_done, u + n // NQ + 1 + LEAD)
                act.wait_ge(exp_done, u * NQ + n + LEAD)
                nc.scalar.activation(s_ctx[:, :, :], ps[:, CB, :].rearrange("p (t c) -> p t c", c=CTX),
                                     ACT.Copy).then_inc(c_copied, 1)

            def exponential(u, n):
                slot = n % SLOTS
                act.wait_ge(max_done, u * NQ + n + 1 + LEAD)
                act.wait_ge(t_done, u * (5 * NQ // 2) + 5 * (n // 2 - 1) + LEAD)
                nc.scalar.activation(probs[:, slot, TOK:KEYS], s_ctx[:, n % NQ, :], ACT.Exp, bias=nmx[:, slot:slot + 1],
                                     accum_out=den[:, 1, slot:slot + 1])
                nc.scalar.activation(probs[:, slot, 0:TOK], psf[:, 1024 * (n % 2):1024 * (n % 2) + TOK], ACT.Exp,
                                     bias=nmx[:, slot:slot + 1], accum_out=den[:, 0, slot:slot + 1]).then_inc(exp_done, 1)

            def high_pt(u, n, g):
                gi = 5 * (n // 2) + 2 * (n % 2) + g
                act.wait_ge(t_done, u * (5 * NQ // 2) + gi + 1 + LEAD)
                if g == 0:
                    act.wait_ge(pv_done, u * (NQ // 2) + n // 2 - 1 + LEAD)
                dst, src = pt_group(0, n, g)
                nc.scalar.activation(dst, src, ACT.Copy).then_inc(pt_high, 1)

            def low_rows(u, j):
                act.wait_ge(pv_done, u * (NQ // 2) + j + 1 + LEAD)
                nc.scalar.activation(o_low[:, :], ps[DH0:P, OB, 0:2 * P], ACT.Copy).then_inc(o_low_done, 1)

            def phase(u, k, heads, project, own_values):
                nt = NQ * len(heads)
                for n in range(nt + LAG + 2):
                    m = n - LAG
                    if m >= 3 and m % 2 == 1:
                        low_rows(u, (m - 3) // 2)
                    if n < nt and n % NQ == 0:
                        copy_context(u, n)
                    if 0 <= m < nt:
                        high_pt(u, m, 0)
                        high_pt(u, m, 1)
                        if m % 2 == 1:
                            high_pt(u, m, 2)
                    if n < nt:
                        exponential(u, n)
                    if n == 1 and own_values:
                        high_v(k)
                    if n == nt and project:
                        high_qk(k + 1, 0, Q_PIECES, 0)
                    if n == nt + LAG and project:
                        high_qk(k + 1, 1, K_PIECES, len(Q_PIECES))

            high_qk(0, 0, Q_PIECES, 0)
            high_qk(0, 1, K_PIECES, len(Q_PIECES))
            with act.Fori(0, BATCH) as b:
                phase(b * HEADS0, b * PAIRS, [(0, 0)], True, True)
                with act.Fori(1, PAIRS) as p:
                    k = b * PAIRS + p
                    phase(k * 2 - 1, k, [(1, -1), (0, 0)], True, True)
                phase(b * HEADS0 + (HEADS0 - 1), b * PAIRS + PAIRS, [(1, -1)], False, False)

        @block.vector
        def _(dve):
            for s in (qk_low, v_low, c_max, tok_max, max_done, den_sum, pt_low, o_done, x_added):
                dve.sem_inc(s, LEAD)

            def low_qk(k, which, pieces, i0):
                dst, scale = ((q_split, 1.0 / 8.0), (k_split, 1.0))[which]
                for i, (bank, at, w) in enumerate(pieces):
                    dve.wait_ge(qk_high, k * SPLITS + i0 + i + 1 + LEAD)
                    nc.vector.scalar_tensor_tensor(dst[:, 1, at:at + w], ps[:, bank, 0:w], scale, dst[:, 0, at:at + w],
                                                   ALU.mult, ALU.subtract).then_inc(qk_low, 1)

            def low_v(k):
                for i, (bank, c0, n) in enumerate(V_PIECES):
                    dve.wait_ge(v_high, k * 3 + i + 1 + LEAD)
                    nc.vector.tensor_tensor(v_split[:, :, c0:c0 + n, 1, :],
                                            ps[:, bank, 0:n * P].rearrange("p (c h d) -> p h c d", h=2, d=DH0),
                                            v_split[:, :, c0:c0 + n, 0, :], ALU.subtract).then_inc(v_low, 1)

            def context_max(u, n):
                dve.wait_ge(c_copied, u + n // NQ + 1 + LEAD)
                dve.wait_ge(max_done, u * NQ + n + LEAD)
                nc.vector.tensor_reduce(ctx_nmx[:, :], s_ctx[:, :, :], AX.X, ALU.max, negate=True).then_inc(c_max, 1)

            def row_max(u, n):
                s, slot = u * NQ + n, n % SLOTS
                dve.wait_ge(s_done, s + 1 + LEAD)
                nc.vector.tensor_reduce(tok_nmx[:, slot:slot + 1], psf[:, 1024 * (n % 2):1024 * (n % 2) + TOK], AX.X,
                                        ALU.max, negate=True).then_inc(tok_max, 1)
                if n % NQ == 0:
                    context_max(u, n)
                    dve.wait_ge(c_max, u + n // NQ + 1 + LEAD)
                dve.wait_ge(tok_max, s + 1 + LEAD)
                nc.vector.tensor_tensor(nmx[:, slot:slot + 1], tok_nmx[:, slot:slot + 1], ctx_nmx[:, n % NQ:n % NQ + 1],
                                        ALU.min).then_inc(max_done, 1)

            def reciprocal(u, n):
                s, slot = u * NQ + n, n % SLOTS
                dve.wait_ge(exp_done, s + 1 + LEAD)
                nc.vector.tensor_tensor(den[:, 0, slot:slot + 1], den[:, 0, slot:slot + 1], den[:, 1, slot:slot + 1],
                                        ALU.add).then_inc(den_sum, 1)
                dve.wait_ge(den_sum, s + 1 + LEAD)
                nc.vector.reciprocal(rden[:, slot:slot + 1], den[:, 0, slot:slot + 1]).then_inc(rden_done, 1)

            def low_pt(u, n, g):
                dve.wait_ge(pt_high, u * (5 * NQ // 2) + 5 * (n // 2) + 2 * (n % 2) + g + 1 + LEAD)
                dst, src = pt_group(1, n, g)
                nc.vector.tensor_tensor(dst, src, pt_group(0, n, g)[0], ALU.subtract).then_inc(pt_low, 1)

            def join(u, j, h, pair):
                dve.wait_ge(o_low_done, u * (NQ // 2) + j + 1 + LEAD)
                cols = slice((j % (NQ // 2)) * 2 * P, (j % (NQ // 2)) * 2 * P + 2 * P)
                nc.vector.tensor_tensor(ot[DH0 * h:DH0 * h + DH0, pair, cols], ps[0:DH0, OB, 0:2 * P], o_low[:, :],
                                        ALU.add).then_inc(o_done, 1)

            def phase(u, k, heads, pairs, project, own_values):
                nt = NQ * len(heads)
                for n in range(nt + LAG + 2):
                    m = n - LAG
                    if n < nt:
                        row_max(u, n)
                    if 1 <= n <= nt:
                        reciprocal(u, n - 1)
                    if m >= 3 and m % 2 == 1:
                        j = (m - 3) // 2
                        join(u, j, heads[j // (NQ // 2)][0], pairs[j // (NQ // 2)])
                    if n == 1 and own_values:
                        low_v(k)
                    if 0 <= m < nt:
                        low_pt(u, m, 0)
                        low_pt(u, m, 1)
                        if m % 2 == 1:
                            low_pt(u, m, 2)
                    if n == nt and project:
                        low_qk(k + 1, 0, Q_PIECES, 0)
                    if n == nt + LAG and project:
                        low_qk(k + 1, 1, K_PIECES, len(Q_PIECES))

            low_qk(0, 0, Q_PIECES, 0)
            low_qk(0, 1, K_PIECES, len(Q_PIECES))
            with dve.Fori(0, BATCH) as b:
                phase(b * HEADS0, b * PAIRS, [(0, 0)], [0], True, True)
                with dve.Fori(1, PAIRS) as p:
                    k = b * PAIRS + p
                    phase(k * 2 - 1, k, [(1, -1), (0, 0)], [p - 1, p], True, True)
                phase(b * HEADS0 + (HEADS0 - 1), b * PAIRS + PAIRS, [(1, -1)], [PAIRS - 1], False, False)
                for i in range(TPB):
                    dve.wait_ge(wo_done, b * TPB + i + 1 + LEAD)
                    nc.vector.tensor_tensor(x_sb[:, b * TPB + i, :], ps[:, i % 4, 0:D], x_sb[:, b * TPB + i, :],
                                            ALU.add).then_inc(x_added, 1)
            dve.wait_ge(x_added, BATCH * TPB + LEAD)


def route(nc, a, outer, xn_t, h, ps, slots):
    results = nc.dram_tensor("slot_results", [SLOT_TILES * P, D], F32, kind="Internal").ap()
    keep = lambda n, s, dt=F32: outer.enter_context(nc.sbuf_tensor(f"moe_{n}", s, dt, side="right"))
    slot = [keep(f"slot{k}", [P, TILES], U32) for k in range(2)]
    share = [keep(f"share{k}", [P, TILES]) for k in range(2)]
    tile_expert = keep("tile_expert", [P, SLOT_TILES], I32)
    choose_slots(nc, a, xn_t, ps, slot, share, tile_expert)
    with ExitStack() as c1:
        scattered = c1.enter_context(nc.semaphore("moe_scattered"))
        block = c1.enter_context(nc.Block())

        @block.gpsimd
        def _(pool):
            for k in range(2):
                for t in range(TILES):
                    pool.indirect_dma_start(slots[:, :], bass.IndirectOffsetOnAxis(ap=slot[k][:, t:t + 1], axis=0),
                                            h[:, t, :], None).then_inc(scattered, 16)
            pool.wait_ge(scattered, 16 * 2 * TILES)
    return slots, results, slot, share, tile_expert


def run_experts(nc, a, x_sb, ident, ps, gamma, beta, tables, weights):
    slots, results, slot, share, tile_expert = tables
    expert_tiles(nc, a, ident, ps, gamma, beta, slots, results, tile_expert, weights)
    combine(nc, x_sb, slot, share, results)


def choose_slots(nc, a, xn_t, ps, slot, share, tile_expert):
    with ExitStack() as ctx:
        sb = lambda n, s, dt=F32: ctx.enter_context(nc.sbuf_tensor(f"rt_{n}", s, dt))
        sem = lambda n: ctx.enter_context(nc.semaphore(f"rt_{n}"))
        gw = sb("gw", [P, DC, E])
        TE = [P, TILES, E]
        prob, work, ohs, one1, one2, base = (sb(n, TE) for n in ("prob", "work", "ohs", "one1", "one2", "base"))
        scan = [sb(f"scan{i}", TE) for i in range(2)]
        top1, top2, red = sb("top1", [P, TILES]), sb("top2", [P, TILES]), sb("red", [P, TILES])
        escan = [sb(f"escan{i}", [P, E]) for i in range(2)]
        padded, start = sb("padded", [P, E]), sb("start", [P, E])
        erank = sb("erank", [P, E])
        tstart = sb("tstart", [P, SLOT_TILES])
        cmp = sb("cmp", [P, SLOT_TILES, E])
        tsum = sb("tsum", [P, SLOT_TILES])
        lower, ones = sb("lower", [P, P]), sb("ones", [P, P])
        gw_loaded, const, logits_done, v, exped, counted = (sem(n) for n in ("gw", "const", "logits", "v", "exped", "counted"))
        block = ctx.enter_context(nc.Block())

        @block.sync
        def _(sp):
            sp.dma_start(gw[:], a["L0_ffn_gate_w"].rearrange("(c p) e -> p c e", p=P)).then_inc(gw_loaded, 16)

        @block.gpsimd
        def _(pool):
            nc.gpsimd.memset(ones[:], 1.0).then_inc(const, 1)
            nc.gpsimd.memset(lower[:], 1.0).then_inc(const, 1)
            nc.gpsimd.iota(erank[:], [[-1, E]], base=E, channel_multiplier=0,
                           allow_small_or_imprecise_dtypes=True).then_inc(const, 1)
            nc.gpsimd.iota(tstart[:], [[P, SLOT_TILES]], base=0, channel_multiplier=0,
                           allow_small_or_imprecise_dtypes=True).then_inc(const, 1)
            pool.wait_ge(const, 4)
            nc.gpsimd.affine_select(out=lower[:], in_=lower[:], compare_op=ALU.is_gt, fill=0.0, base=0,
                                    pattern=[[1, P]], channel_multiplier=-1).then_inc(const, 1)

        @block.tensor
        def _(pe):
            pe.wait_ge(gw_loaded, 16)
            for t in range(TILES):
                for c in range(DC):
                    mm = nc.tensor.matmul(ps[:, 0, t * E:(t + 1) * E], xn_t[:, c, t * P:(t + 1) * P], gw[:, c, :],
                                          start=(c == 0), stop=(c == DC - 1))
            mm.then_inc(logits_done, 1)
            pe.wait_ge(const, 5)
            pe.wait_ge(counted, 1)
            flat = ohs[:, :, :].rearrange("p t e -> p (t e)")
            nc.tensor.matmul(ps[:, 1, 0:TILES * E], lower[:], flat, start=True, stop=True).then_inc(counted, 1)
            nc.tensor.matmul(ps[:, 2, 0:TILES * E], ones[:], flat, start=True, stop=True).then_inc(counted, 1)

        @block.scalar
        def _(act):
            act.wait_ge(v, 2)
            nc.scalar.activation(prob[:, :, :], work[:, :, :], ACT.Exp).then_inc(exped, 1)

        @block.vector
        def _(dve):
            n = [0]

            def step(ins):
                n[0] += 1
                ins.then_inc(v, 1)
                dve.wait_ge(v, n[0])

            def bcast(x):
                return x[:, :].unsqueeze(2).to_broadcast(TE)

            V = nc.vector
            logits = ps[:, 0, 0:TILES * E].rearrange("p (t e) -> p t e", e=E)
            prefix = ps[:, 1, 0:TILES * E].rearrange("p (t e) -> p t e", e=E)
            total = ps[:, 2, 0:TILES * E].rearrange("p (t e) -> p t e", e=E)
            rank = erank[:, :].unsqueeze(1).to_broadcast(TE)
            dve.wait_ge(logits_done, 1)
            step(V.tensor_reduce(red[:], logits, AX.X, ALU.max))
            step(V.tensor_tensor(work[:], logits, bcast(red), ALU.subtract))
            dve.wait_ge(exped, 1)
            step(V.tensor_reduce(red[:], prob[:], AX.X, ALU.add))
            step(V.reciprocal(red[:], red[:]))
            step(V.tensor_tensor(prob[:], prob[:], bcast(red), ALU.mult))
            dve.wait_ge(const, 5)

            def pick(one, top):
                step(V.tensor_reduce(top[:], prob[:], AX.X, ALU.max))
                step(V.tensor_tensor(work[:], prob[:], bcast(top), ALU.is_equal))
                step(V.tensor_tensor(work[:], work[:], rank, ALU.mult))
                step(V.tensor_reduce(red[:], work[:], AX.X, ALU.max))
                step(V.tensor_tensor(one[:], bcast(red), rank, ALU.is_equal))

            pick(one1, top1)
            step(V.scalar_tensor_tensor(prob[:], one1[:], -4.0, prob[:], ALU.mult, ALU.add))
            pick(one2, top2)
            step(V.tensor_tensor(red[:], top1[:], top2[:], ALU.add))
            step(V.reciprocal(red[:], red[:]))
            step(V.tensor_tensor(share[0][:], top1[:], red[:], ALU.mult))
            step(V.tensor_tensor(share[1][:], top2[:], red[:], ALU.mult))
            V.tensor_tensor(ohs[:], one1[:], one2[:], ALU.add).then_inc(counted, 1)
            dve.wait_ge(counted, 3)
            step(V.tensor_copy(scan[0][:], total))
            src, s = 0, 1
            while s < TILES:
                step(V.tensor_copy(scan[1 - src][:, 0:s, :], scan[src][:, 0:s, :]))
                step(V.tensor_tensor(scan[1 - src][:, s:, :], scan[src][:, s:, :], scan[src][:, :TILES - s, :], ALU.add))
                src, s = 1 - src, 2 * s
            inclusive = scan[src]
            step(V.tensor_scalar(padded[:], inclusive[:, TILES - 1, :], 1.0 / P, 127.0 / P - 0.5 + 0.5 / P, ALU.mult, ALU.add))
            step(V.tensor_scalar(padded[:], padded[:], ROUND, None, ALU.add))
            step(V.tensor_scalar(padded[:], padded[:], ROUND, float(P), ALU.subtract, ALU.mult))
            step(V.tensor_copy(escan[0][:], padded[:]))
            es, s = 0, 1
            while s < E:
                step(V.tensor_copy(escan[1 - es][:, 0:s], escan[es][:, 0:s]))
                step(V.tensor_tensor(escan[1 - es][:, s:], escan[es][:, s:], escan[es][:, :E - s], ALU.add))
                es, s = 1 - es, 2 * s
            end = escan[es]
            step(V.tensor_tensor(start[:], end[:], padded[:], ALU.subtract))
            step(V.tensor_tensor(base[:], inclusive[:], total, ALU.subtract))
            step(V.tensor_tensor(base[:], base[:], prefix, ALU.add))
            step(V.tensor_tensor(base[:], base[:], start[:, :].unsqueeze(1).to_broadcast(TE), ALU.add))
            for k, one in enumerate((one1, one2)):
                step(V.tensor_tensor(work[:], one[:], base[:], ALU.mult))
                step(V.tensor_reduce(red[:], work[:], AX.X, ALU.add))
                step(V.tensor_copy(slot[k][:], red[:]))
            SE = [P, SLOT_TILES, E]
            step(V.tensor_tensor(cmp[:], end[:, :].unsqueeze(1).to_broadcast(SE), tstart[:, :].unsqueeze(2).to_broadcast(SE),
                                 ALU.is_le))
            step(V.tensor_reduce(tsum[:], cmp[:], AX.X, ALU.add))
            step(V.tensor_scalar(tile_expert[:], tsum[:], float(E - 1), None, ALU.min))


def expert_tiles(nc, a, ident, ps, gamma, beta, slots, results, tile_expert, weights):
    w1, w2, w_loaded = weights
    with ExitStack() as ctx:
        sb = lambda n, s, dt=F32: ctx.enter_context(nc.sbuf_tensor(f"ex_{n}", s, dt))
        sem = lambda n: ctx.enter_context(nc.semaphore(f"ex_{n}"))
        FC = FF // P
        rows = sb("rows", [P, 2, D])
        b1r = sb("b1r", [P, 2, FF])
        b2r = sb("b2r", [P, 2, D])
        xt = sb("xt", [P, 2, DC, P])
        hid = sb("hid", [P, 2, FF])
        hid_t = sb("hid_t", [P, 2, FC, P])
        y = sb("y", [P, 2, D])
        rows_loaded, b1_loaded, b2_loaded, stored = ([sem(f"{n}{j}") for j in range(2)]
                                                     for n in ("rows_loaded", "b1_loaded", "b2_loaded", "stored"))
        x_turned, x_evac, h_done, h_biased, h_act = (sem(n) for n in ("x_turned", "x_evac", "h_done", "h_biased", "h_act"))
        g_turned, g_evac_act, g_evac_dve, y_done, y_biased = (sem(n) for n in ("g_turned", "g_evac_act", "g_evac_dve", "y_done", "y_biased"))
        XB, HB, TB, YB = 0, 1, 5, 7
        NT = SLOT_TILES
        block = ctx.enter_context(nc.Block())

        @block.sync
        def _(sp):
            for s in rows_loaded + b1_loaded + b2_loaded + stored:
                sp.sem_inc(s, LEAD)

            def load(s, j, store):
                e = sp.value_load(tile_expert[0:1, ds(s, 1)], min_val=0, max_val=E - 1)
                sp.wait_ge(x_turned, s - 1 + LEAD)
                sp.dma_start(rows[:, j, :], slots[ds(s * P, P), :]).then_inc(rows_loaded[j], 16)
                sp.wait_ge(h_biased, s - 1 + LEAD)
                sp.dma_start(b1r[:, j, :], a["L0_ffn_b1"][ds(e, 1), :].partition_broadcast(P)).then_inc(b1_loaded[j], 16)
                sp.wait_ge(y_biased, s - 1 + LEAD)
                sp.dma_start(b2r[:, j, :], a["L0_ffn_b2"][ds(e, 1), :].partition_broadcast(P)).then_inc(b2_loaded[j], 16)
                if store:
                    sp.dma_start(results[ds((s - 2) * P, P), :], y[:, j, :]).then_inc(stored[j], 16)

            for j in range(2):
                load(j, j, False)
            with sp.Fori(1, NT // 2) as u:
                for j in range(2):
                    load(u * 2 + j, j, True)
            for j in range(2):
                sp.wait_ge(y_biased, NT - 1 + j + LEAD)
                sp.dma_start(results[(NT - 2 + j) * P:(NT - 1 + j) * P, :], y[:, j, :]).then_inc(stored[j], 16)
            for j in range(2):
                sp.wait_ge(stored[j], NT // 2 * 16 + LEAD)

        @block.tensor
        def _(pe):
            for s in (x_turned, h_done, g_turned, y_done):
                pe.sem_inc(s, LEAD)

            def turn_rows(s, u, j):
                pe.wait_ge(rows_loaded[j], (u + 1) * 16 + LEAD)
                pe.wait_ge(x_evac, s * DC + LEAD)
                for c in range(DC):
                    mm = nc.tensor.transpose(ps[:, XB, c * P:(c + 1) * P], rows[:, j, c * P:(c + 1) * P], ident[:])
                mm.then_inc(x_turned, 1)

            def first_layer(s, j):
                e = pe.value_load(tile_expert[0:1, ds(s, 1)], min_val=0, max_val=E - 1)
                pe.wait_ge(x_evac, s * DC + DC + LEAD)
                pe.wait_ge(h_biased, s - 1 + LEAD)
                for nb in range(2):
                    for c in range(DC):
                        mm = nc.tensor.matmul(ps[:, HB + 2 * j + nb, :], xt[:, j, c, :],
                                              w1[:, ds(e * (DC * FF) + (c * FF + nb * 512), 512)],
                                              start=(c == 0), stop=(c == DC - 1))
                mm.then_inc(h_done, 1)

            def turn_hidden(s, j):
                pe.wait_ge(h_act, s + 1 + LEAD)
                pe.wait_ge(g_evac_act, s + LEAD)
                pe.wait_ge(g_evac_dve, s + LEAD)
                for f in range(FC):
                    mm = nc.tensor.transpose(ps[:, TB + f // 4, (f % 4) * P:(f % 4) * P + P],
                                             hid[:, j, f * P:(f + 1) * P], ident[:])
                    if f % 4 == 3:
                        mm.then_inc(g_turned, 1)

            def second_layer(s, j):
                e = pe.value_load(tile_expert[0:1, ds(s, 1)], min_val=0, max_val=E - 1)
                pe.wait_ge(g_evac_act, s + 1 + LEAD)
                pe.wait_ge(g_evac_dve, s + 1 + LEAD)
                pe.wait_ge(y_biased, s + LEAD)
                for f in range(FC):
                    mm = nc.tensor.matmul(ps[:, YB, 0:D], hid_t[:, j, f, :], w2[:, ds(e * (FC * D) + f * D, D)],
                                          start=(f == 0), stop=(f == FC - 1))
                mm.then_inc(y_done, 1)

            def step(s, j, nxt):
                if nxt:
                    turn_rows(*nxt)
                turn_hidden(s, j)
                if nxt:
                    first_layer(nxt[0], nxt[2])
                second_layer(s, j)

            turn_rows(0, 0, 0)
            pe.wait_ge(w_loaded, 32 * E)
            first_layer(0, 0)
            with pe.Fori(0, NT // 2 - 1) as u:
                step(u * 2, 0, (u * 2 + 1, u, 1))
                step(u * 2 + 1, 1, (u * 2 + 2, u + 1, 0))
            step(NT - 2, 0, (NT - 1, NT // 2 - 1, 1))
            step(NT - 1, 1, None)

        @block.scalar
        def _(act):
            for s in (x_evac, h_act, g_evac_act):
                act.sem_inc(s, LEAD)

            def rows_out(s, j):
                act.wait_ge(x_turned, s + 1 + LEAD)
                act.wait_ge(h_done, s - 1 + LEAD)
                for c in range(DC):
                    nc.scalar.activation(xt[:, j, c, :], ps[:, XB, c * P:(c + 1) * P], ACT.Identity,
                                         bias=beta[:, c:c + 1], scale=gamma[:, c:c + 1]).then_inc(x_evac, 1)

            def gelu(s, j):
                act.wait_ge(h_biased, s + 1 + LEAD)
                nc.scalar.activation(hid[:, j, :], hid[:, j, :], ACT.Gelu).then_inc(h_act, 1)

            def hidden_out(s, j):
                act.wait_ge(g_turned, s * 2 + 1 + LEAD)
                act.wait_ge(y_done, s - 1 + LEAD)
                nc.scalar.activation(hid_t[:, j, 0:4, :], ps[:, TB, :].rearrange("p (f q) -> p f q", f=4),
                                     ACT.Copy).then_inc(g_evac_act, 1)

            def step(s, j, nxt):
                if nxt:
                    rows_out(nxt[0], nxt[1])
                hidden_out(s, j)
                if nxt:
                    gelu(nxt[0], nxt[1])

            rows_out(0, 0)
            gelu(0, 0)
            with act.Fori(0, NT // 2 - 1) as u:
                step(u * 2, 0, (u * 2 + 1, 1))
                step(u * 2 + 1, 1, (u * 2 + 2, 0))
            step(NT - 2, 0, (NT - 1, 1))
            step(NT - 1, 1, None)

        @block.vector
        def _(dve):
            for s in (h_biased, g_evac_dve, y_biased):
                dve.sem_inc(s, LEAD)

            def add_b1(s, u, j):
                dve.wait_ge(h_done, s + 1 + LEAD)
                dve.wait_ge(b1_loaded[j], (u + 1) * 16 + LEAD)
                dve.wait_ge(g_turned, s * 2 - 2 + LEAD)
                nc.vector.tensor_tensor(hid[:, j, :].rearrange("p (b n) -> p b n", b=2), ps[:, HB + 2 * j:HB + 2 * j + 2, :],
                                        b1r[:, j, :].rearrange("p (b n) -> p b n", b=2), ALU.add).then_inc(h_biased, 1)

            def hidden_out(s, j):
                dve.wait_ge(g_turned, s * 2 + 2 + LEAD)
                dve.wait_ge(y_done, s - 1 + LEAD)
                nc.vector.tensor_copy(hid_t[:, j, 4:8, :], ps[:, TB + 1, :].rearrange("p (f q) -> p f q", f=4)
                                      ).then_inc(g_evac_dve, 1)

            def add_b2(s, u, j):
                dve.wait_ge(y_done, s + 1 + LEAD)
                dve.wait_ge(b2_loaded[j], (u + 1) * 16 + LEAD)
                dve.wait_ge(stored[j], u * 16 + LEAD)
                nc.vector.tensor_tensor(y[:, j, :], ps[:, YB, 0:D], b2r[:, j, :], ALU.add).then_inc(y_biased, 1)

            def step(s, u, j, nxt):
                hidden_out(s, j)
                if nxt:
                    add_b1(*nxt)
                add_b2(s, u, j)

            add_b1(0, 0, 0)
            with dve.Fori(0, NT // 2 - 1) as u:
                step(u * 2, u, 0, (u * 2 + 1, u, 1))
                step(u * 2 + 1, u, 1, (u * 2 + 2, u + 1, 0))
            step(NT - 2, NT // 2 - 1, 0, (NT - 1, NT // 2 - 1, 1))
            step(NT - 1, NT // 2 - 1, 1, None)


def combine(nc, x_sb, slot, share, results):
    with ExitStack() as ctx:
        NBUF = 8
        got = ctx.enter_context(nc.sbuf_tensor("cb_got", [P, NBUF, D], F32))
        gathered = [ctx.enter_context(nc.semaphore(f"cb_gathered{i}")) for i in range(NBUF)]
        added = ctx.enter_context(nc.semaphore("cb_added"))
        block = ctx.enter_context(nc.Block())

        @block.gpsimd
        def _(pool):
            for n in range(2 * TILES):
                if n >= NBUF:
                    pool.wait_ge(added, n - NBUF + 1)
                pool.indirect_dma_start(got[:, n % NBUF, :], None, results[:, :],
                                        bass.IndirectOffsetOnAxis(ap=slot[n % 2][:, n // 2:n // 2 + 1], axis=0)
                                        ).then_inc(gathered[n % NBUF], 16)

        @block.vector
        def _(dve):
            for n in range(2 * TILES):
                t = n // 2
                dve.wait_ge(gathered[n % NBUF], 16 * (n // NBUF + 1))
                if n % 2:
                    dve.wait_ge(added, n)
                nc.vector.scalar_tensor_tensor(x_sb[:, t, :], got[:, n % NBUF, :], share[n % 2][:, t:t + 1],
                                               x_sb[:, t, :], ALU.mult, ALU.add).then_inc(added, 1)
            dve.wait_ge(added, 2 * TILES)


def masked_attention(nc, x_sb, h_t, ctx_t, ident, ps, loaded):
    HEADS, DH, HALF = 16, 16, 8
    wq, wkv, wp, bproj, mask, w_loaded, m_loaded = loaded
    with ExitStack() as ctx:
        sb = lambda n, s, dt=F32: ctx.enter_context(nc.sbuf_tensor(f"ma_{n}", s, dt))
        sem = lambda n: ctx.enter_context(nc.semaphore(f"ma_{n}"))
        cap = sb("cap", [P, TILES, CTX])
        hmask = sb("hmask", [P, HALF])
        ctx2 = sb("ctx2", [P, DC, BATCH, 2, CTX])
        k_diag = sb("k_diag", [P, BATCH * 2 * HALF * CTX])
        kt = sb("kt", [P, 2, P])
        v_diag = sb("v_diag", [P, BATCH, HEADS // 2, P])
        vb = sb("vb", [P, HEADS // 2, P])
        qt = sb("qt", [P, 2, 512])
        score = sb("score", [P, 4, HEADS, CTX])
        top, den, etop = (sb(n, [P, 4, HEADS]) for n in ("top", "den", "etop"))
        pt = sb("pt", [P, 2, HEADS // 2, 4 * P])
        ot = sb("ot", [P, 2, 4 * P])
        const, dupd, kv_done, k_out, v_out, prep = (sem(n) for n in ("const", "dupd", "kv_done", "k_out", "v_out", "prep"))
        vb_ready, q_done, q_evac, s_done, capped, shifted, exped, top_step, den_step, summed, normed, t_done = (sem(n) for n in (
            "vb_ready", "q_done", "q_evac", "s_done", "capped", "shifted", "exped", "top_step", "den_step", "summed", "normed", "t_done"))
        t_act, t_dve, o_done, o_evac, p_done, x_added, etop_done = (sem(n) for n in (
            "t_act", "t_dve", "o_done", "o_evac", "p_done", "x_added", "etop_done"))
        FMAX = float(np.finfo(np.float32).max)
        block = ctx.enter_context(nc.Block())

        @block.gpsimd
        def _(pool):
            pool.sem_inc(normed, LEAD)
            pool.sem_inc(vb_ready, LEAD)
            nc.gpsimd.memset(hmask[:], 1.0).then_inc(const, 1)
            nc.gpsimd.memset(v_diag[:, :, :, :], 0.0).then_inc(const, 1)
            pool.wait_ge(const, 2)
            nc.gpsimd.affine_select(out=hmask[:], in_=hmask[:], compare_op=ALU.is_ge, fill=0.0, base=0,
                                    pattern=[[-DH, HALF]], channel_multiplier=1).then_inc(const, 1)
            pool.wait_ge(const, 3)
            nc.gpsimd.affine_select(out=hmask[:], in_=hmask[:], compare_op=ALU.is_ge, fill=0.0, base=DH - 1,
                                    pattern=[[DH, HALF]], channel_multiplier=-1).then_inc(const, 1)
            pool.wait_ge(v_out, BATCH * HEADS)
            with pool.Fori(0, BATCH) as b:
                pool.wait_ge(o_done, b * 2 + LEAD)
                nc.gpsimd.tensor_copy(vb[:, :, :], v_diag[:, b, :, :]).then_inc(vb_ready, 1)
                with pool.Fori(0, 2) as g2:
                    for j in range(4):
                        n = (b * 2 + g2) * 4 + j
                        pool.wait_ge(summed, n + 1 + LEAD)
                        nc.gpsimd.tensor_tensor(score[:, j], score[:, j],
                                                den[:, j, :].unsqueeze(2).to_broadcast([P, HEADS, CTX]),
                                                ALU.mult).then_inc(normed, 1)

        @block.tensor
        def _(pe):
            for s in (q_done, s_done, t_done, o_done, p_done):
                pe.sem_inc(s, LEAD)
            pe.wait_ge(w_loaded, 48)
            for m in range(2):
                for c in range(DC):
                    mm = nc.tensor.matmul(ps[:, 0, m * P:(m + 1) * P], wkv[:, c, m * P:(m + 1) * P], ctx_t[:, c, :],
                                          start=(c == 0), stop=(c == DC - 1))
            mm.then_inc(kv_done, 1)
            pe.wait_ge(dupd, DC)
            for b in range(BATCH):
                for c in range(DC):
                    mm = nc.tensor.matmul(ps[:, 1 + b, 0:D], ctx2[:, c, b, :, :].rearrange("p r k -> p (r k)"),
                                          wkv[:, c, D:2 * D], start=(c == 0), stop=(c == DC - 1))
            mm.then_inc(kv_done, 1)
            pe.wait_ge(k_out, 5)
            pe.wait_ge(v_out, BATCH * HEADS)

            def project_q(b, g2):
                g = b * 2 + g2
                pe.wait_ge(o_evac, (g - g2) * 2 + LEAD)
                for m in range(2):
                    for c in range(DC):
                        mm = nc.tensor.matmul(ps[:, m, :], wq[:, c, m * P:(m + 1) * P], h_t[:, c, ds(g * 512, 512)],
                                              start=(c == 0), stop=(c == DC - 1))
                mm.then_inc(q_done, 1)
                pe.wait_ge(q_evac, g + 1 + LEAD)

            def scores(b, g2, j):
                pe.wait_ge(capped, (b * 2 + g2) * 4 + j - 1 + LEAD)
                for m in range(2):
                    mm = nc.tensor.matmul(ps[:, 2 + 2 * (j % 2) + m, :], qt[:, m, j * P:(j + 1) * P],
                                          k_diag[:, ds(b * (2 * HALF * CTX) + m * (HALF * CTX), HALF * CTX)],
                                          start=True, stop=True)
                mm.then_inc(s_done, 1)

            def turn(b, g2, j):
                g = b * 2 + g2
                n = g * 4 + j
                pe.wait_ge(normed, n + 1 + LEAD)
                pe.wait_ge(t_act, n + LEAD)
                pe.wait_ge(t_dve, n + LEAD)
                pe.wait_ge(x_added, g * 4 + LEAD)
                for k in range(HEADS // 2):
                    mm = nc.tensor.transpose(ps[:, 6 + k // 4, (k % 4) * P:(k % 4) * P + P],
                                             score[:, j, 2 * k:2 * k + 2, :].rearrange("p h k -> p (h k)"), ident[:])
                mm.then_inc(t_done, 1)

            def values_and_projection(b, g2):
                g = b * 2 + g2
                pe.wait_ge(vb_ready, b + 1 + LEAD)
                pe.wait_ge(t_act, g * 4 + 4 + LEAD)
                pe.wait_ge(t_dve, g * 4 + 4 + LEAD)
                for k in range(HEADS // 2):
                    mm = nc.tensor.matmul(ps[:, k // 4, :], vb[:, k, :], pt[:, g2, k, :], start=(k % 4 == 0), stop=(k % 4 == 3))
                mm.then_inc(o_done, 1)
                pe.wait_ge(o_evac, g * 2 + 2 + LEAD)
                for j in range(4):
                    if j >= 2:
                        pe.wait_ge(x_added, g * 4 + j - 1 + LEAD)
                    for c in range(DC):
                        mm = nc.tensor.matmul(ps[:, 6 + j % 2, 0:D], ot[:, c, j * P:(j + 1) * P], wp[:, c, :],
                                              start=(c == 0), stop=(c == DC - 1))
                    mm.then_inc(p_done, 1)

            with pe.Fori(0, BATCH) as b:
                for g2 in range(2):
                    project_q(b, g2)
                    scores(b, g2, 0)
                    scores(b, g2, 1)
                    if g2:
                        values_and_projection(b, 0)
                    for j in range(4):
                        if j + 2 < 4:
                            scores(b, g2, j + 2)
                        turn(b, g2, j)
                values_and_projection(b, 1)

        @block.scalar
        def _(act):
            for s in (q_evac, exped, etop_done, t_act, o_evac):
                act.sem_inc(s, LEAD)
            for c in range(DC):
                nc.scalar.activation(ctx2[:, c], ctx_t[:, c, :].rearrange("p (b k) -> p b k", b=BATCH).unsqueeze(2)
                                     .to_broadcast([P, BATCH, 2, CTX]), ACT.Copy).then_inc(dupd, 1)
            act.wait_ge(kv_done, 1)
            nc.scalar.activation(kt[:, :, :], ps[:, 0, 0:2 * P].rearrange("p (m k) -> p m k", m=2), ACT.Copy).then_inc(k_out, 1)
            def outputs(b, g2):
                g = b * 2 + g2
                act.wait_ge(o_done, g + 1 + LEAD)
                act.wait_ge(p_done, g * 4 + LEAD)
                for c in range(2):
                    nc.scalar.activation(ot[:, c, :], ps[:, c, :], ACT.Copy).then_inc(o_evac, 1)

            with act.Fori(0, BATCH) as b:
                for g2 in range(2):
                    g = b * 2 + g2
                    act.wait_ge(q_done, g + 1 + LEAD)
                    act.wait_ge(s_done, g * 4 + LEAD)
                    nc.scalar.activation(qt[:, :, :], ps[:, 0:2, :], ACT.Copy).then_inc(q_evac, 1)
                    for j in range(5):
                        n = g * 4 + j
                        if j == 1 and g2:
                            outputs(b, 0)
                        if j < 4:
                            act.wait_ge(shifted, n + 1 + LEAD)
                            nc.scalar.activation(score[:, j], score[:, j], ACT.Exp, scale=0.25).then_inc(exped, 1)
                            nc.scalar.activation(etop[:, j, :], top[:, j, :], ACT.Exp, scale=-0.25).then_inc(etop_done, 1)
                        if j >= 1:
                            act.wait_ge(t_done, n + LEAD)
                            act.wait_ge(o_done, g - 1 + LEAD)
                            nc.scalar.activation(pt[:, g2, 0:4, (j - 1) * P:j * P],
                                                 ps[:, 6, :].rearrange("p (k q) -> p k q", k=4), ACT.Copy).then_inc(t_act, 1)
                outputs(b, 1)

        @block.vector
        def _(dve):
            for s in (capped, shifted, summed, t_dve, x_added):
                dve.sem_inc(s, LEAD)
            V = nc.vector
            dve.wait_ge(m_loaded, 32)
            V.tensor_scalar(cap[:, :, :], mask[:, :, :].bitcast(U8), -2.0, 1.0, ALU.mult, ALU.add).then_inc(prep, 1)
            V.tensor_tensor(x_sb[:, :, :], x_sb[:, :, :], bproj[:, :].unsqueeze(1).to_broadcast([P, TILES, D]),
                            ALU.add).then_inc(prep, 1)
            dve.wait_ge(prep, 2)
            V.tensor_scalar(cap[:, :, :], cap[:, :, :], FMAX, None, ALU.mult).then_inc(prep, 1)
            dve.wait_ge(prep, 3)
            dve.wait_ge(k_out, 1)
            dve.wait_ge(const, 4)
            for b in range(BATCH):
                for m in range(2):
                    o = (b * 2 + m) * HALF * CTX
                    V.tensor_tensor(k_diag[:, o:o + HALF * CTX].rearrange("p (h k) -> p h k", h=HALF),
                                    kt[:, m, b * CTX:(b + 1) * CTX].unsqueeze(1).to_broadcast([P, HALF, CTX]),
                                    hmask[:, :].unsqueeze(2).to_broadcast([P, HALF, CTX]), ALU.mult).then_inc(k_out, 1)
            dve.wait_ge(kv_done, 2)
            for b in range(BATCH):
                for h in range(HEADS):
                    r = slice(CTX * (h % 2), CTX * (h % 2) + CTX)
                    col = (h % HALF) * DH
                    V.tensor_copy(v_diag[r, b, h // 2, col:col + DH], ps[r, 1 + b, h * DH:(h + 1) * DH]).then_inc(v_out, 1)

            def shift(b, g2, j):
                n = (b * 2 + g2) * 4 + j
                sc = score[:, j]
                dve.wait_ge(s_done, n + 1 + LEAD)
                dve.wait_ge(t_done, n - 3 + LEAD)
                V.tensor_tensor(sc, ps[:, 2 + 2 * (j % 2):4 + 2 * (j % 2), :].rearrange("p m (h k) -> p (m h) k", k=CTX),
                                cap[:, ds(n, 1), :].to_broadcast([P, HEADS, CTX]), ALU.min).then_inc(capped, 1)
                dve.wait_ge(capped, n + 1 + LEAD)
                V.tensor_reduce(top[:, j, :], sc, AX.X, ALU.max).then_inc(top_step, 1)
                dve.wait_ge(top_step, n * 2 + 1)
                V.tensor_scalar(top[:, j, :], top[:, j, :], 0.0, None, ALU.max).then_inc(top_step, 1)
                dve.wait_ge(top_step, n * 2 + 2)
                V.tensor_tensor(sc, sc, top[:, j, :].unsqueeze(2).to_broadcast([P, HEADS, CTX]),
                                ALU.subtract).then_inc(shifted, 1)

            def total(b, g2, j):
                n = (b * 2 + g2) * 4 + j
                dve.wait_ge(exped, n + 1 + LEAD)
                V.tensor_reduce(den[:, j, :], score[:, j], AX.X, ALU.add).then_inc(den_step, 1)
                dve.wait_ge(etop_done, n + 1 + LEAD)
                dve.wait_ge(den_step, n * 2 + 1)
                V.tensor_tensor(den[:, j, :], den[:, j, :], etop[:, j, :], ALU.add).then_inc(den_step, 1)
                dve.wait_ge(den_step, n * 2 + 2)
                V.reciprocal(den[:, j, :], den[:, j, :]).then_inc(summed, 1)

            def add_to_x(b, g2):
                for j in range(4):
                    n = (b * 2 + g2) * 4 + j
                    dve.wait_ge(p_done, n + 1 + LEAD)
                    row = x_sb[:, ds(n, 1), :]
                    V.tensor_tensor(row, ps[:, 6 + j % 2, 0:D].unsqueeze(1), row, ALU.add).then_inc(x_added, 1)

            with dve.Fori(0, BATCH) as b:
                for g2 in range(2):
                    g = b * 2 + g2
                    shift(b, g2, 0)
                    for j in range(5):
                        if j + 1 < 4:
                            shift(b, g2, j + 1)
                        if j < 4:
                            total(b, g2, j)
                        if j == 0 and g2:
                            add_to_x(b, 0)
                        if j >= 1:
                            dve.wait_ge(t_done, g * 4 + j + LEAD)
                            dve.wait_ge(o_done, g - 1 + LEAD)
                            V.tensor_copy(pt[:, g2, 4:8, (j - 1) * P:j * P], ps[:, 7, :].rearrange("p (k q) -> p k q", k=4)
                                          ).then_inc(t_dve, 1)
                add_to_x(b, 1)
            dve.wait_ge(x_added, TILES + LEAD)


def phase_ffn(nc, x_sb, h_t, vecs, ps, loaded):
    FC, SLOTS, G = FF // P, 4, TILES // 4
    INV2PI = float(np.float32(1 / (2 * np.pi)))
    TWO_PI_HI = 6.28125
    TWO_PI_LO = 2 * np.pi - TWO_PI_HI
    PI_IN = float(np.nextafter(np.float32(np.pi), np.float32(0)))
    b1, theta, wr, wi = (vecs[n] for n in ("L1_ffn_b1", "L1_ffn_quantum_phases", "L1_ffn_quantum_weights_real",
                                           "L1_ffn_quantum_weights_imag"))
    w1, w2, b2, w_loaded = loaded
    with ExitStack() as ctx:
        sb = lambda n, s, dt=F32: ctx.enter_context(nc.sbuf_tensor(f"ff_{n}", s, dt))
        sem = lambda n: ctx.enter_context(nc.semaphore(f"ff_{n}"))
        red, cosv, sinv, coef = (sb(n, [P, FC]) for n in ("red", "cosv", "sinv", "coef"))
        hid, arg, turns, mixed = (sb(n, [P, SLOTS, 512]) for n in ("hid", "arg", "turns", "mixed"))
        small, s_act = sem("small"), sem("s_act")
        h_done, h_out, arg_done, k_rough, k_done, r_step, r_done, sin_done, q_done, relu_done, y_done, x_added = (
            sem(n) for n in ("h_done", "h_out", "arg_done", "k_rough", "k_done", "r_step", "r_done", "sin_done",
                             "q_done", "relu_done", "y_done", "x_added"))
        block = ctx.enter_context(nc.Block())

        @block.tensor
        def _(pe):
            for s in (h_done, y_done):
                pe.sem_inc(s, LEAD)
            pe.wait_ge(w_loaded, 48)
            with pe.Fori(0, G) as g:
                for n in range(FC + 5):
                    if n < FC:
                        pe.wait_ge(h_out, g * FC + (n - 3) + LEAD)
                        for c in range(DC):
                            mm = nc.tensor.matmul(ps[:, n % 4, :], w1[:, c, n * P:(n + 1) * P], h_t[:, c, ds(g * 512, 512)],
                                                  start=(c == 0), stop=(c == DC - 1))
                        mm.then_inc(h_done, 1)
                    if n >= 5:
                        f = n - 5
                        pe.wait_ge(relu_done, g * FC + f + 1 + LEAD)
                        if f == 0:
                            pe.wait_ge(x_added, g * 4 + LEAD)
                        for j in range(4):
                            mm = nc.tensor.matmul(ps[:, 4 + j, 0:D], mixed[:, f % SLOTS, j * P:(j + 1) * P], w2[:, f, :],
                                                  start=(f == 0), stop=(f == FC - 1))
                        mm.then_inc(y_done, 1)

        @block.scalar
        def _(act):
            for s in (h_out, k_done, sin_done, relu_done):
                act.sem_inc(s, LEAD)
            act.wait_ge(small, 6)
            nc.scalar.activation(sinv[:], red[:], ACT.Sin).then_inc(s_act, 1)
            nc.scalar.activation(cosv[:], cosv[:], ACT.Sin).then_inc(s_act, 1)
            with act.Fori(0, G) as g:
                for n in range(FC + 4):
                    if n < FC:
                        act.wait_ge(h_done, g * FC + n + 1 + LEAD)
                        act.wait_ge(q_done, g * FC + n - 3 + LEAD)
                        nc.scalar.activation(hid[:, n % SLOTS, :], ps[:, n % 4, :], ACT.Identity,
                                             bias=b1[:, n:n + 1]).then_inc(h_out, 1)
                    if 1 <= n <= FC:
                        f = n - 1
                        act.wait_ge(k_rough, g * FC + f + 1 + LEAD)
                        nc.scalar.activation(turns[:, f % SLOTS, :], turns[:, f % SLOTS, :], ACT.Copy,
                                             bias=-ROUND).then_inc(k_done, 1)
                    if 2 <= n <= FC + 1:
                        f = n - 2
                        act.wait_ge(r_done, g * FC + f + 1 + LEAD)
                        nc.scalar.activation(arg[:, f % SLOTS, :], arg[:, f % SLOTS, :], ACT.Sin).then_inc(sin_done, 1)
                    if n >= 4:
                        f = n - 4
                        act.wait_ge(q_done, g * FC + f + 1 + LEAD)
                        nc.scalar.activation(mixed[:, f % SLOTS, :], mixed[:, f % SLOTS, :], ACT.Relu).then_inc(relu_done, 1)

        @block.vector
        def _(dve):
            for s in (arg_done, k_rough, r_step, r_done, q_done, x_added):
                dve.sem_inc(s, LEAD)
            V = nc.vector
            n_small = [0]

            def step(ins):
                n_small[0] += 1
                ins.then_inc(small, 1)
                dve.wait_ge(small, n_small[0])

            step(V.tensor_scalar(red[:], theta, INV2PI, ROUND, ALU.mult, ALU.add))
            step(V.tensor_scalar(red[:], red[:], ROUND, None, ALU.subtract))
            step(V.scalar_tensor_tensor(coef[:], red[:], -TWO_PI_HI, theta, ALU.mult, ALU.add))
            step(V.scalar_tensor_tensor(red[:], red[:], -TWO_PI_LO, coef[:], ALU.mult, ALU.add))
            step(V.tensor_scalar(red[:], red[:], -PI_IN, PI_IN, ALU.max, ALU.min))
            V.tensor_scalar(coef[:], red[:], -1.0, None, ALU.mult).then_inc(s_act, 1)
            dve.wait_ge(s_act, 1)
            V.tensor_tensor(cosv[:], coef[:], red[:], ALU.min).then_inc(s_act, 1)
            dve.wait_ge(s_act, 2)
            step(V.tensor_scalar(cosv[:], cosv[:], float(np.pi / 2), None, ALU.add))
            dve.wait_ge(s_act, 4)
            step(V.tensor_tensor(cosv[:], cosv[:], wr, ALU.mult))
            step(V.tensor_tensor(sinv[:], sinv[:], wi, ALU.mult))
            step(V.tensor_tensor(coef[:], cosv[:], sinv[:], ALU.add))
            step(V.scalar_tensor_tensor(coef[:], coef[:], 0.1, wi, ALU.mult, ALU.mult))
            dve.wait_ge(w_loaded, 48)
            step(V.tensor_tensor(x_sb[:, :, :], x_sb[:, :, :], b2[:, :].unsqueeze(1).to_broadcast([P, TILES, D]), ALU.add))
            with dve.Fori(0, G) as g:
                for n in range(FC + 3):
                    if n < FC:
                        s = n % SLOTS
                        dve.wait_ge(h_out, g * FC + n + 1 + LEAD)
                        V.tensor_scalar(arg[:, s, :], hid[:, s, :], 0.1, theta[:, n:n + 1], ALU.mult, ALU.add).then_inc(arg_done, 1)
                        dve.wait_ge(arg_done, g * FC + n + 1 + LEAD)
                        V.tensor_scalar(turns[:, s, :], arg[:, s, :], INV2PI, ROUND, ALU.mult, ALU.add).then_inc(k_rough, 1)
                    if 1 <= n <= FC:
                        f = n - 1
                        s = f % SLOTS
                        dve.wait_ge(k_done, g * FC + f + 1 + LEAD)
                        V.scalar_tensor_tensor(arg[:, s, :], turns[:, s, :], -TWO_PI_HI, arg[:, s, :], ALU.mult, ALU.add).then_inc(r_step, 1)
                        dve.wait_ge(r_step, g * (2 * FC) + 2 * f + 1 + LEAD)
                        V.scalar_tensor_tensor(arg[:, s, :], turns[:, s, :], -TWO_PI_LO, arg[:, s, :], ALU.mult, ALU.add).then_inc(r_step, 1)
                        dve.wait_ge(r_step, g * (2 * FC) + 2 * f + 2 + LEAD)
                        V.tensor_scalar(arg[:, s, :], arg[:, s, :], -PI_IN, PI_IN, ALU.max, ALU.min).then_inc(r_done, 1)
                    if n >= 3:
                        f = n - 3
                        s = f % SLOTS
                        dve.wait_ge(sin_done, g * FC + f + 1 + LEAD)
                        dve.wait_ge(y_done, g * FC + f - 3 + LEAD)
                        V.scalar_tensor_tensor(mixed[:, s, :], arg[:, s, :], coef[:, f:f + 1], hid[:, s, :], ALU.mult,
                                               ALU.add).then_inc(q_done, 1)
                for j in range(4):
                    dve.wait_ge(y_done, g * FC + FC + LEAD)
                    row = x_sb[:, ds(g * 4 + j, 1), :]
                    V.tensor_tensor(row, ps[:, 4 + j, 0:D].unsqueeze(1), row, ALU.add).then_inc(x_added, 1)
            dve.wait_ge(x_added, TILES + LEAD)


def store_out(nc, out, x_sb):
    with ExitStack() as ctx:
        stored = ctx.enter_context(nc.semaphore("stored"))
        block = ctx.enter_context(nc.Block())

        @block.sync
        def _(sp):
            sp.dma_start(out.rearrange("b (t p) d -> p (b t) d", p=P), x_sb[:]).then_inc(stored, 16)
            sp.wait_ge(stored, 16)


def build(nc, a, out):
    slots = nc.dram_tensor("slot_rows", [SLOT_TILES * P, D], F32, kind="Internal").ap()
    with ExitStack() as ctx:
        sb = lambda n, s, dt=F32: ctx.enter_context(nc.sbuf_tensor(n, s, dt))
        ps = ctx.enter_context(nc.psum_tensor("ps", [P, 8, 512], F32))
        ident = sb("ident", [P, P])
        x_sb = sb("x_sb", [P, TILES, D])
        ctx_sb = sb("ctx_sb", [P, D])
        ctx_t = sb("ctx_t", [P, DC, P])
        vecs = sb("vecs", [P, VROWS])
        aff = {n: vecs[:, r0:r1] for n, (r0, r1) in vector_columns().items()}
        with ExitStack() as c0:
            ctx_ln_t = c0.enter_context(nc.sbuf_tensor("ctx_ln_t", [P, DC, P], F32))
            ln_t = c0.enter_context(nc.sbuf_tensor("ln_t", [P, DC, TILES * P], F32))
            with nc.sbuf_tensor("h0", [P, TILES, D], F32) as h, nc.sbuf_tensor("zero", [P, D], F32) as zero, \
                    nc.semaphore("slots_zeroed") as zeroed:
                def clear_slots(sp):
                    sp.dma_start(slots.rearrange("(t p) d -> p t d", p=P),
                                 zero[:, :].unsqueeze(1).to_broadcast([P, SLOT_TILES, D])).then_inc(zeroed, 16)
                    sp.wait_ge(zeroed, 16)

                load_and_prepare(nc, a, x_sb, ctx_sb, ctx_t, ctx_ln_t, ident, ps, vecs, zero)
                layer_norm_transposed(nc, "ln0", x_sb, h, ps, ident, (aff["L0_xattn_ln2_w"], aff["L0_xattn_ln2_b"]),
                                      ln_t, nested=True, add_residual=False, prefetch=clear_slots)
            perceiver_attention(nc, a, x_sb, ln_t, ctx_ln_t, ident, ps)
        with ExitStack() as c1:
            w1 = c1.enter_context(nc.sbuf_tensor("ex_w1", [P, E * DC * FF], F32))
            w2 = c1.enter_context(nc.sbuf_tensor("ex_w2", [P, E * FF // P * D], F32))
            w_loaded = c1.enter_context(nc.semaphore("ex_w_loaded"))

            def load_experts(sp):
                w1_src = a["L0_ffn_w1"].rearrange("e (c p) h -> p e c h", p=P)
                w2_src = a["L0_ffn_w2"].rearrange("e (f p) d -> p e f d", p=P)
                w1_dst = w1[:, :].rearrange("p (e c h) -> p e c h", e=E, c=DC)
                w2_dst = w2[:, :].rearrange("p (e f d) -> p e f d", e=E, f=FF // P)
                for e in range(E):
                    sp.dma_start(w1_dst[:, e], w1_src[:, e]).then_inc(w_loaded, 16)
                    sp.dma_start(w2_dst[:, e], w2_src[:, e]).then_inc(w_loaded, 16)

            with nc.sbuf_tensor("h1", [P, TILES, D], F32) as h, nc.sbuf_tensor("xn_t", [P, DC, TILES * P], F32) as xn_t:
                layer_norm_transposed(nc, "ln1", x_sb, h, ps, ident, (aff["L0_ffn_gamma"], aff["L0_ffn_beta"]), xn_t,
                                      nested=True, add_residual=True, keep_rows=True, prefetch=load_experts)
                tables = route(nc, a, c1, xn_t, h, ps, slots)
            run_experts(nc, a, x_sb, ident, ps, aff["L0_ffn_gamma"], aff["L0_ffn_beta"], tables, (w1, w2, w_loaded))
        wq, wkv, wp = sb("ma_wq", [P, DC, D]), sb("ma_wkv", [P, DC, 2 * D]), sb("ma_wp", [P, DC, D])
        bproj = sb("ma_bproj", [P, D])
        mask = sb("ma_mask", [P, TILES, CTX // 4], I32)
        w1, w2, b2 = sb("ff_w1", [P, DC, FF]), sb("ff_w2", [P, FF // P, D]), sb("ff_b2", [P, D])
        ma_w_loaded, ma_m_loaded, ff_w_loaded = (ctx.enter_context(nc.semaphore(n)) for n in (
            "ma_w_loaded", "ma_m_loaded", "ff_w_loaded"))
        ma_loaded = wq, wkv, wp, bproj, mask, ma_w_loaded, ma_m_loaded
        ff_loaded = w1, w2, b2, ff_w_loaded

        def load_second_layer(sp):
            sp.dma_start(wkv[:], a["L1_xattn_Wkv"].rearrange("(c p) n -> p c n", p=P)).then_inc(ma_w_loaded, 16)
            sp.dma_start(wq[:], a["L1_xattn_Wq"].rearrange("(c p) n -> p c n", p=P)).then_inc(ma_w_loaded, 16)
            sp.dma_start(wp[:], a["L1_xattn_Wproj"].rearrange("(c p) n -> p c n", p=P)).then_inc(ma_w_loaded, 16)
            sp.dma_start(mask[:], a["mask_BxSxS2_bk0"].rearrange("b (t p) k -> p (b t) k", p=P)).then_inc(ma_m_loaded, 16)
            sp.dma_start(bproj[:], a["L1_xattn_bproj"].partition_broadcast(P)).then_inc(ma_m_loaded, 16)
            sp.dma_start(w1[:], a["L1_ffn_W1"].rearrange("(c p) n -> p c n", p=P)).then_inc(ff_w_loaded, 16)
            sp.dma_start(w2[:], a["L1_ffn_W2"].rearrange("(f p) n -> p f n", p=P)).then_inc(ff_w_loaded, 16)
            sp.dma_start(b2[:], a["L1_ffn_b2"].partition_broadcast(P)).then_inc(ff_w_loaded, 16)

        with nc.sbuf_tensor("h2_t", [P, DC, TILES * P], F32) as h_t:
            layer_norm_transposed(nc, "ln2", x_sb, None, ps, ident, None, h_t, nested=False, add_residual=False,
                                  prefetch=load_second_layer)
            masked_attention(nc, x_sb, h_t, ctx_t, ident, ps, ma_loaded)
        with nc.sbuf_tensor("h3_t", [P, DC, TILES * P], F32) as h_t:
            layer_norm_transposed(nc, "ln3", x_sb, None, ps, ident, None, h_t, nested=False, add_residual=False)
            phase_ffn(nc, x_sb, h_t, aff, ps, ff_loaded)
        store_out(nc, out, x_sb)


NAMES = ['x', 'ctx_1024', 'mask_BxSxS2_bk0', 'L0_xattn_Wq', 'L0_xattn_Wkv', 'L0_xattn_Wo', 'L0_xattn_ln1_w',
         'L0_xattn_ln1_b', 'L0_xattn_ln2_w', 'L0_xattn_ln2_b', 'L0_ffn_gate_w', 'L0_ffn_w1', 'L0_ffn_b1', 'L0_ffn_w2',
         'L0_ffn_b2', 'L0_ffn_gamma', 'L0_ffn_beta', 'L1_xattn_Wq', 'L1_xattn_Wkv', 'L1_xattn_Wproj', 'L1_xattn_bproj',
         'L1_ffn_W1', 'L1_ffn_b1', 'L1_ffn_quantum_phases', 'L1_ffn_quantum_weights_real',
         'L1_ffn_quantum_weights_imag', 'L1_ffn_W2', 'L1_ffn_b2']


def kernel(**inputs):
    import concourse.bacc as bacc
    from concourse.bass_utils import run_bass_kernel_spmd

    nc = bacc.Bacc("TRN2", target_bir_lowering=False, num_devices=1)
    arrays, handles = {}, {}
    for name in NAMES:
        v = np.ascontiguousarray(inputs[name])
        if v.dtype == np.bool_:
            v = v.view(np.int32)
        arrays[f"in_{name}"] = v
        handles[name] = nc.dram_tensor(f"in_{name}", v.shape, mybir.dt.from_np(v.dtype), kind="ExternalInput").ap()
    out = nc.dram_tensor("out_0", (BATCH, TOK, D), F32, kind="ExternalOutput").ap()
    build(nc, handles, out)
    r = run_bass_kernel_spmd(nc, [arrays], core_ids=[0])
    return r.results[0]["out_0"]
```
